# Optimizing a Trainium2 kernel written in Bass

```python
import numpy as np
import jax
import jax.numpy as jnp

def _softmax(x, axis=-1):
    return jax.nn.softmax(x, axis=axis)

def _gelu(x):
    return jax.nn.gelu(x, approximate=True)

def _silu(x):
    return jax.nn.silu(x)

def _sigmoid(x):
    return jax.nn.sigmoid(x)

def _layernorm(x, axis=-1, eps=1e-05):
    m = jnp.mean(x, axis=axis, keepdims=True)
    v = jnp.var(x, axis=axis, keepdims=True)
    return (x - m) / jnp.sqrt(v + eps)

def _scatter_add(tgt, idx, src, axis=0):
    return tgt.at[idx].add(src)

def _segment_sum(src, seg, n):
    return jax.ops.segment_sum(src, seg, n)
kernel_name = 'mk_xattn_ffn_d1_seqx_r8_1c924b'

def setup_inputs(seed: int=0):
    np.random.seed(seed)
    _w = jnp.asarray

    def _rec_inputs():
        import jax
        import jax.numpy as jnp
        _rk = jax.random.key(seed)
        x = 7.22e-05 + 1 * jax.random.normal(jax.random.fold_in(_rk, 1), (128, 64, 128), jnp.float32)
        _lenS = 64 - jax.random.randint(jax.random.fold_in(_rk, 7), (128,), 0, max(1, 64 // 4) + 1, jnp.int32)
        _lenS2 = 64 - jax.random.randint(jax.random.fold_in(_rk, 8), (128,), 0, max(1, 64 // 4) + 1, jnp.int32)
        _ctx_1024P = jax.random.normal(jax.random.fold_in(_rk, 11), (128, 16, 128), jnp.float32)
        _ctx_1024c = jax.random.dirichlet(jax.random.fold_in(_rk, 511), 0.3 * jnp.ones((16,), jnp.float32), (128, 64))
        _ctx_1024t = jnp.einsum('bsk,bkd->bsd', _ctx_1024c, _ctx_1024P)
        _ctx_1024t = _ctx_1024t * jax.lax.rsqrt(jnp.mean(jnp.square(_ctx_1024t)) + 1e-12) * 0.953939
        ctx_1024 = 4.13588e-05 + 0.999923 * (_ctx_1024t + 0.3 * jax.random.normal(jax.random.fold_in(_rk, 611), (128, 64, 128), jnp.float32))
        return (x, ctx_1024)
    x, ctx_1024 = _rec_inputs()

    def _L0_xattn_setup():
        import jax, jax.numpy as jnp
        import numpy as np
        D_MODEL = 128
        HEADS = 16
        D_HEAD = D_MODEL // HEADS
        SEQ = 256
        C = 2
        K_TOP = int(C * np.log(SEQ))
        key = jax.random.key(seed)
        ks = jax.random.split(key, 5)
        s = 0.02
        return {'Q': jax.random.normal(ks[0], (4, SEQ, D_MODEL), jnp.float32), 'K': jax.random.normal(ks[1], (4, SEQ, D_MODEL), jnp.float32), 'V': jax.random.normal(ks[2], (4, SEQ, D_MODEL), jnp.float32), 'Wq': jax.random.normal(ks[3], (D_MODEL, D_HEAD), jnp.float32) * s, 'bq': jnp.zeros((D_HEAD,), jnp.float32), 'Wout': jax.random.normal(ks[4], (HEADS * D_HEAD, D_MODEL), jnp.float32) * s, 'bout': jnp.zeros((D_MODEL,), jnp.float32)}
    _L0_xattn_all = _L0_xattn_setup()
    _L0_xattn_in = {k: v for k, v in _L0_xattn_all.items() if k in ('Wq', 'bq', 'Wout', 'bout')}
    del _L0_xattn_all

    def _L0_ffn_setup():
        import jax, jax.numpy as jnp
        import numpy as np
        DIM, HEADS, FFN, E = (128, 16, 512, 8)
        B, S = (2, 128)
        EPS = 1e-05

        def _ln(x, g, b):
            mu = jnp.mean(x, axis=-1, keepdims=True)
            var = jnp.mean((x - mu) ** 2, axis=-1, keepdims=True)
            return (x - mu) * jax.lax.rsqrt(var + EPS) * g + b
        key = jax.random.key(seed)
        ks = jax.random.split(key, 20)
        sd = 0.02
        d, f = (DIM, FFN)
        return {'x': jax.random.normal(ks[0], (B, S, d), jnp.float32), 'ln1_g': jnp.ones((d,), jnp.float32), 'ln1_b': jnp.zeros((d,), jnp.float32), 'Wqkv': jax.random.normal(ks[1], (d, 3 * d), jnp.float32) * sd, 'bqkv': jnp.zeros((3 * d,), jnp.float32), 'Wo': jax.random.normal(ks[2], (d, d), jnp.float32) * sd, 'bo': jnp.zeros((d,), jnp.float32), 'ln2_g': jnp.ones((d,), jnp.float32), 'ln2_b': jnp.zeros((d,), jnp.float32), 'gate_w': jax.random.normal(ks[3], (d, E), jnp.float32) * sd, 'W1': jax.random.normal(ks[4], (E, d, f), jnp.float32) * sd, 'b1': jnp.zeros((E, f), jnp.float32), 'W2': jax.random.normal(ks[5], (E, f, d), jnp.float32) * sd, 'b2': jnp.zeros((E, d), jnp.float32), 'rW1': jax.random.normal(ks[6], (d, f), jnp.float32) * sd, 'rb1': jnp.zeros((f,), jnp.float32), 'rW2': jax.random.normal(ks[7], (f, d), jnp.float32) * sd, 'rb2': jnp.zeros((d,), jnp.float32), 'coef_w': jax.random.normal(ks[8], (d, 2), jnp.float32) * sd, 'coef_b': jnp.zeros((2,), jnp.float32)}
    _L0_ffn_all = _L0_ffn_setup()
    _L0_ffn_in = {k: v for k, v in _L0_ffn_all.items() if k in ('ln1_g', 'ln1_b', 'Wqkv', 'bqkv', 'Wo', 'bo', 'ln2_g', 'ln2_b', 'gate_w', 'W1', 'b1', 'W2', 'b2', 'rW1', 'rb1', 'rW2', 'rb2', 'coef_w', 'coef_b')}
    del _L0_ffn_all
    return {'x': x, 'ctx_1024': ctx_1024, 'L0_xattn_Wq': _L0_xattn_in['Wq'], 'L0_xattn_bq': _L0_xattn_in['bq'], 'L0_xattn_Wout': _L0_xattn_in['Wout'], 'L0_xattn_bout': _L0_xattn_in['bout'], 'L0_ffn_ln1_g': _L0_ffn_in['ln1_g'], 'L0_ffn_ln1_b': _L0_ffn_in['ln1_b'], 'L0_ffn_Wqkv': _L0_ffn_in['Wqkv'], 'L0_ffn_bqkv': _L0_ffn_in['bqkv'], 'L0_ffn_Wo': _L0_ffn_in['Wo'], 'L0_ffn_bo': _L0_ffn_in['bo'], 'L0_ffn_ln2_g': _L0_ffn_in['ln2_g'], 'L0_ffn_ln2_b': _L0_ffn_in['ln2_b'], 'L0_ffn_gate_w': _L0_ffn_in['gate_w'], 'L0_ffn_W1': _L0_ffn_in['W1'], 'L0_ffn_b1': _L0_ffn_in['b1'], 'L0_ffn_W2': _L0_ffn_in['W2'], 'L0_ffn_b2': _L0_ffn_in['b2'], 'L0_ffn_rW1': _L0_ffn_in['rW1'], 'L0_ffn_rb1': _L0_ffn_in['rb1'], 'L0_ffn_rW2': _L0_ffn_in['rW2'], 'L0_ffn_rb2': _L0_ffn_in['rb2'], 'L0_ffn_coef_w': _L0_ffn_in['coef_w'], 'L0_ffn_coef_b': _L0_ffn_in['coef_b']}

def reference(x, ctx_1024, L0_xattn_Wq, L0_xattn_bq, L0_xattn_Wout, L0_xattn_bout, L0_ffn_ln1_g, L0_ffn_ln1_b, L0_ffn_Wqkv, L0_ffn_bqkv, L0_ffn_Wo, L0_ffn_bo, L0_ffn_ln2_g, L0_ffn_ln2_b, L0_ffn_gate_w, L0_ffn_W1, L0_ffn_b1, L0_ffn_W2, L0_ffn_b2, L0_ffn_rW1, L0_ffn_rb1, L0_ffn_rW2, L0_ffn_rb2, L0_ffn_coef_w, L0_ffn_coef_b):
    import jax
    import jax.numpy as jnp

    def _L0_xattn_ref(Q, K, V, Wq, bq, Wout, bout):
        import jax, jax.numpy as jnp
        import numpy as np
        D_MODEL = 128
        HEADS = 16
        D_HEAD = D_MODEL // HEADS
        SEQ = 256
        C = 2
        K_TOP = int(C * np.log(SEQ))
        B, L, _ = Q.shape
        q = (Q @ Wq + bq).transpose(0, 2, 1)
        k_ = (K @ Wq + bq).transpose(0, 2, 1)
        v = (V @ Wq + bq).transpose(0, 2, 1)
        Qf = jnp.fft.fft(q.astype(jnp.complex64))
        Kf = jnp.fft.fft(k_.astype(jnp.complex64))
        corr = jnp.real(jnp.fft.ifft(Qf * jnp.conj(Kf)))
        corr = corr.mean(axis=(0, 1))
        W_topk, I_topk = jax.lax.top_k(corr, K_TOP)
        W_topk = jax.nn.softmax(W_topk)

        def body(R, ws):
            w, shift = ws
            return (R + w * jnp.roll(v, -shift, axis=-1), None)
        R3, _ = jax.lax.scan(body, jnp.zeros_like(v), (W_topk, I_topk))
        R = jnp.broadcast_to(R3[:, None], (B, HEADS, D_HEAD, L)).reshape(B, L, HEADS * D_HEAD)
        return R @ Wout + bout

    def _L0_ffn_ref(x, ln1_g, ln1_b, Wqkv, bqkv, Wo, bo, ln2_g, ln2_b, gate_w, W1, b1, W2, b2, rW1, rb1, rW2, rb2, coef_w, coef_b):
        import jax, jax.numpy as jnp
        import numpy as np
        DIM, HEADS, FFN, E = (128, 16, 512, 8)
        B, S = (2, 128)
        EPS = 1e-05

        def _ln(x, g, b):
            mu = jnp.mean(x, axis=-1, keepdims=True)
            var = jnp.mean((x - mu) ** 2, axis=-1, keepdims=True)
            return (x - mu) * jax.lax.rsqrt(var + EPS) * g + b
        b, s, d = x.shape
        h, dh = (HEADS, d // HEADS)
        xn = _ln(x, ln1_g, ln1_b)
        qkv = xn @ Wqkv + bqkv
        q, k, v = jnp.split(qkv, 3, axis=-1)
        q = q.reshape(b, s, h, dh)
        k = k.reshape(b, s, h, dh)
        v = v.reshape(b, s, h, dh)
        scores = jnp.einsum('bqhd,bkhd->bhqk', q, k) / jnp.sqrt(jnp.float32(dh))
        attn = jax.nn.softmax(scores, axis=-1)
        ctx = jnp.einsum('bhqk,bkhd->bqhd', attn, v).reshape(b, s, d)
        x = x + ctx @ Wo + bo
        xn2 = _ln(x, ln2_g, ln2_b)
        xt = xn2.reshape(b * s, d)
        probs = jax.nn.softmax(xt @ gate_w, axis=-1)
        gate_val = jnp.max(probs, axis=-1, keepdims=True)
        expert_idx = jnp.argmax(probs, axis=-1)
        oh = jax.nn.one_hot(expert_idx, E, dtype=xt.dtype)
        xe = jnp.einsum('te,td->etd', oh, xt)
        he = jax.nn.gelu(jnp.einsum('etd,edf->etf', xe, W1) + b1[:, None, :], approximate=False)
        ye = jnp.einsum('etf,efd->etd', he, W2) + b2[:, None, :]
        moe_out = jnp.einsum('te,etd->td', oh, ye) * gate_val
        rm = jax.nn.gelu(xt @ rW1 + rb1, approximate=False) @ rW2 + rb2
        coef = jax.nn.softmax(xt @ coef_w + coef_b, axis=-1)
        ff = moe_out * coef[:, 0:1] + rm * coef[:, 1:2]
        return x + ff.reshape(b, s, d)
    x = x + _L0_xattn_ref(_layernorm(x, axis=-1), ctx_1024, ctx_1024, L0_xattn_Wq, L0_xattn_bq, L0_xattn_Wout, L0_xattn_bout)
    x = x + _L0_ffn_ref(_layernorm(x, axis=-1), L0_ffn_ln1_g, L0_ffn_ln1_b, L0_ffn_Wqkv, L0_ffn_bqkv, L0_ffn_Wo, L0_ffn_bo, L0_ffn_ln2_g, L0_ffn_ln2_b, L0_ffn_gate_w, L0_ffn_W1, L0_ffn_b1, L0_ffn_W2, L0_ffn_b2, L0_ffn_rW1, L0_ffn_rb1, L0_ffn_rW2, L0_ffn_rb2, L0_ffn_coef_w, L0_ffn_coef_b)
    return x

_drawn_inputs = setup_inputs


def setup_inputs(seed=0):
    import zlib

    import numpy as np

    out = dict(_drawn_inputs(seed))
    spreads = {'L0_xattn_bq': (0.0, 0.1),
     'L0_xattn_bout': (0.0, 0.1),
     'L0_ffn_ln1_g': (1.0, 0.6),
     'L0_ffn_ln1_b': (0.0, 0.8),
     'L0_ffn_bqkv': (0.0, 0.728),
     'L0_ffn_bo': (0.0, 0.1),
     'L0_ffn_ln2_g': (1.0, 0.6),
     'L0_ffn_ln2_b': (0.0, 0.8),
     'L0_ffn_b1': (0.0, 0.8),
     'L0_ffn_b2': (0.0, 0.8),
     'L0_ffn_rb1': (0.0, 0.8),
     'L0_ffn_rb2': (0.0, 0.889),
     'L0_ffn_coef_b': (0.0, 0.8)}
    factors = {'L0_ffn_Wqkv': 8.0,
     'L0_ffn_Wo': 4.627,
     'L0_ffn_gate_w': 8.0,
     'L0_ffn_W1': 8.0,
     'L0_ffn_W2': 8.0,
     'L0_ffn_rW1': 3.97,
     'L0_ffn_rW2': 3.623,
     'L0_ffn_coef_w': 8.0}
    for name, (base, spread) in spreads.items():
        noise = np.random.default_rng([zlib.crc32(name.encode()), seed]).standard_normal(out[name].shape)
        drawn = base * np.exp(spread * noise) if base else spread * noise
        out[name] = jnp.asarray(drawn.astype(out[name].dtype))
    for name, factor in factors.items():
        out[name] = (out[name] * factor).astype(out[name].dtype)
    return out
```

```python
from contextlib import ExitStack

import concourse.bass as bass
from concourse import mybir

F32 = mybir.dt.float32
BF16 = mybir.dt.bfloat16
I32 = mybir.dt.int32
U16 = mybir.dt.uint16
ALU = mybir.AluOpType
ACT = mybir.ActivationFunctionType
AX = mybir.AxisListType

P = 128
B, L, D = 128, 64, 128
NT = B * L // P
GT = 4
NG = NT // GT
GB = GT * P // L
DQ = 8
H, DH = 16, 8
E = 8
FF = 512
FC = FF // P
SLOTS = NT + E
K_TOP = 11
EPS = 1e-5
NEG = -3.0e38
BF16_ONE = 0x3F80
W1W = FF + FC

C_G1, C_B1, C_G2, C_B2, C_BQ, C_BK, C_BV, C_RB1 = 0, 1, 2, 3, 4, 5, 6, 7
C_MQ = C_RB1 + FC
C_MK = C_MQ + 4
NCOL = C_MK + 2


def groups(eng, step, first, last, lo, hi):
    for g in range(first, lo):
        step(g, g % 2)
    with eng.Fori(0, (hi - lo) // 2) as i:
        step(i * 2 + lo, 0)
        step(i * 2 + (lo + 1), 1)
    for g in range(hi, last + 1):
        step(g, g % 2)


def valid(g, n=NG):
    return not isinstance(g, int) or 0 <= g < n


def wait(eng, sem, count, most=NG):
    if isinstance(count, int):
        count = min(count, most)
        if count <= 0:
            return
    eng.wait_ge(sem, count)


def nth(g, par, most=NG):
    if isinstance(g, int):
        g = min(g, most - 2 + par)
    return 8 * (g - par + 2)


def settle(eng, cell):
    eng.memset(cell, 0.0)


def build(nc, a, out):
    ctx = ExitStack()
    with ctx:
        def sb(name, shape, dt=F32, scope=ctx):
            return scope.enter_context(nc.sbuf_tensor(name, shape, dt))

        def sem(name):
            return ctx.enter_context(nc.semaphore(name))

        bank = [ctx.enter_context(nc.psum_tensor(f"bank{i}", [P, 512], F32)) for i in range(6)]
        pair = ctx.enter_context(nc.psum_tensor("pair", [P, 2, 512], F32))

        corr_dram = nc.dram_tensor("corr_dram", [L, 2 * L], F32, kind="Internal").ap()
        shift_dram = nc.dram_tensor("shift_dram", [1, 2 * L], F32, kind="Internal").ap()
        xs_dram = nc.dram_tensor("xs_dram", [SLOTS * P, D], F32, kind="Internal").ap()
        ys_dram = nc.dram_tensor("ys_dram", [SLOTS * P, D], F32, kind="Internal").ap()
        xt_dram = nc.dram_tensor("xt_dram", [NG, P, GT * P], F32, kind="Internal").ap()

        cols = sb("cols", [P, NCOL])
        ident = sb("ident", [P, P])
        ones = sb("ones", [P, P])
        x3 = sb("x3", [P, NT, D])
        xh2 = sb("xh2", [P, NT, D])
        logits = sb("logits", [P, NT, E + 2])
        coefb = sb("coefb", [P, 2])
        s_const = sem("s_const")
        x2_dram = nc.dram_tensor("x2_dram", [B * L, D], F32, kind="Internal").ap()
        K = dict(x2_dram=x2_dram, nc=nc, a=a, out=out, sb=sb, sem=sem, bank=bank, pair=pair, cols=cols, ident=ident,
                 ones=ones, x3=x3, xh2=xh2, xt_dram=xt_dram, logits=logits, coefb=coefb, s_const=s_const,
                 corr_dram=corr_dram, shift_dram=shift_dram, xs_dram=xs_dram, ys_dram=ys_dram)
        with ExitStack() as mid:
            vts = sb("vts", [P, NT, 2, 4], scope=mid)
            m2 = sb("m2", [P, D], scope=mid)
            cvec = sb("cvec", [P, D], scope=mid)
            wo = sb("wo", [P, D], scope=mid)
            with ExitStack() as scope:
                correlate(K, scope, vts, m2, cvec, wo)
            with ExitStack() as scope:
                attention(K, scope, vts, m2, cvec, wo)
        with ExitStack() as scope:
            experts(K, scope)


def correlate(K, scope, vts, m2, cvec, wo):
    nc, a, bank, cols, ident, ones = K["nc"], K["a"], K["bank"], K["cols"], K["ident"], K["ones"]
    s_const, sem = K["s_const"], K["sem"]
    corr_dram, shift_dram = K["corr_dram"], K["shift_dram"]

    def sb(name, shape, dt=F32):
        return K["sb"](name, shape, dt, scope)

    wq8 = sb("wq8", [P, DQ])
    bq8 = sb("bq8", [P, DQ])
    sel = sb("sel", [P, 2, L])
    wout = sb("wout", [P, D])
    bo_bc = sb("bo_bc", [P, D])
    xin = sb("xin1", [P, 2, GT, D])
    cin = sb("cin1", [P, 2, GT, D])
    xn = sb("xn1", [P, 2, GT, D])
    cT = sb("cT1", [P, 2, GT * P])
    xT = sb("xT1", [P, 2, GT * P])
    st6 = sb("st6", [P, 2, GT, 6])
    mv = sb("mv1", [P, 2, GT, 2])
    ve = sb("ve1", [P, 2, GT])
    rs = sb("rs1", [P, 2, GT])
    nhalf = sb("nhalf1", [P, GT])
    eps = sb("eps1", [P, GT])
    idle = sb("idle1", [P, 1])
    kq = sb("kq", [P, 2, NT, DQ])

    s_x, s_c = ([sem(f"{n}{i}") for i in range(2)] for n in ("c_x", "c_c"))
    d_nh, d_bs, d_st, d_norm, d_kq = (sem(n) for n in ("c_nh", "c_bs", "c_st", "c_norm", "c_kq"))
    p_ve, p_rs = sem("c_ve"), sem("c_rs")
    t_c, t_x, t_mm = sem("c_tc"), sem("c_tx"), sem("c_mm")
    e_c, e_x = sem("c_ec"), sem("c_ex")
    NCONST = 7
    s_constp = sem("s_constp")
    x_src = a["x"].rearrange("(t p) d -> p t d", p=P)
    c_src = a["ctx"].rearrange("(t p) d -> p t d", p=P)

    with nc.Block() as block:
        @block.sync
        def _(sp):
            sp.dma_start(ident[:], a["ident"]).then_inc(s_const, 16)
            sp.dma_start(wq8[:], a["wq8"]).then_inc(s_const, 16)

            def load(g, par):
                if valid(g):
                    wait(sp, t_c, g - 1)
                    sp.dma_start(cin[:, par], c_src[:, bass.ds(g * GT, GT), :]).then_inc(s_c[par], 16)
                    wait(sp, d_norm, g - 1)
                    sp.dma_start(xin[:, par], x_src[:, bass.ds(g * GT, GT), :]).then_inc(s_x[par], 16)
            groups(sp, load, 0, NG - 1, 2, NG)

        @block.gpsimd
        def _(pool):
            pool.dma_start(bq8[:], a["bq8"].partition_broadcast(P)).then_inc(s_constp, 16)
            pool.dma_start(cols[:], a["cols"]).then_inc(s_constp, 16)
            pool.dma_start(sel[:], a["sel"]).then_inc(s_constp, 16)
            pool.dma_start(wout[:], a["wout_rev"]).then_inc(s_constp, 16)
            pool.dma_start(bo_bc[:], a["bo"].partition_broadcast(P)).then_inc(s_constp, 16)
            pool.dma_start(wo[:], a["wo"]).then_inc(s_constp, 16)
            pool.dma_start(K["coefb"][:], a["coef_b"].partition_broadcast(P)).then_inc(s_constp, 16)

            pool.wait_ge(d_nh, 1)

            def rstd(g, par):
                if valid(g + 1):
                    o = 1 - par
                    wait(pool, d_st, g + 2)
                    wait(pool, d_norm, g)
                    pool.tensor_tensor(ve[:, o], mv[:, o, :, 1], eps[:], ALU.add).then_inc(p_ve, 1)
                    wait(pool, p_ve, g + 2)
                    pool.tensor_tensor(rs[:, o], ve[:, o], nhalf[:], ALU.pow).then_inc(p_rs, 1)
            groups(pool, rstd, -1, NG, 2, NG - 2)

        @block.vector
        def _(dve):
            nc.vector.memset(eps[:], EPS)
            nc.vector.memset(nhalf[:], -0.5).then_inc(d_nh, 1)
            nc.vector.memset(ones[:], 1.0)

            def step(g, par):
                o = 1 - par
                if valid(g + 1):
                    wait(dve, s_x[o], nth(g + 1, o), 16 * NG)
                    wait(dve, d_st, g)
                    for t in range(GT):
                        last = nc.vector.bn_stats(st6[:, o, t], xin[:, o, t])
                    last.then_inc(d_bs, 1)
                    wait(dve, d_bs, g + 2)
                    wait(dve, d_norm, g)
                    settle(nc.vector, idle[:])
                    for t in range(GT):
                        last = nc.vector.bn_aggr(mv[:, o, t], st6[:, o, t])
                    last.then_inc(d_st, 1)
                if valid(g):
                    wait(dve, p_rs, g + 1)
                    wait(dve, t_x, g - 1)
                    for t in range(GT):
                        last = nc.vector.tensor_scalar(xn[:, par, t], xin[:, par, t], mv[:, par, t, 0:1],
                                                       rs[:, par, t:t + 1], ALU.subtract, ALU.mult)
                    last.then_inc(d_norm, 1)
                if valid(g - 1):
                    if isinstance(g, int) and g == 1:
                        dve.wait_ge(s_constp, 16 * NCONST)
                    wait(dve, t_mm, g)
                    nc.vector.tensor_tensor(
                        kq[:, :, bass.ds((g - 1) * GT, GT), :],
                        bank[4 + o][:, 0:2 * GT * DQ].rearrange("p (w t j) -> p w t j", w=2, t=GT),
                        bq8[:].unsqueeze(1).unsqueeze(1).broadcast_to([P, 2, GT, DQ]),
                        ALU.add).then_inc(d_kq, 1)
            groups(dve, step, -1, NG, 2, NG - 2)

        @block.scalar
        def _(act):
            def step(g, par):
                if valid(g):
                    wait(act, t_mm, g - 1)
                    wait(act, t_c, g + 1)
                    nc.scalar.copy(cT[:, par], bank[par][:]).then_inc(e_c, 1)
                    wait(act, t_x, g + 1)
                    nc.scalar.copy(xT[:, par], bank[2 + par][:]).then_inc(e_x, 1)
            groups(act, step, 0, NG - 1, 2, NG)

        @block.tensor
        def _(pe):
            pe.wait_ge(s_const, 32)
            pe.wait_ge(s_constp, 16 * NCONST)

            def step(g, par):
                if valid(g):
                    wait(pe, s_c[par], nth(g, par), 16 * NG)
                    wait(pe, e_c, g - 1)
                    for t in range(GT):
                        last = nc.tensor.transpose(bank[par][:, t * P:(t + 1) * P], cin[:, par, t], ident[:])
                    last.then_inc(t_c, 1)
                    wait(pe, d_norm, g + 1)
                    wait(pe, e_x, g - 1)
                    for t in range(GT):
                        last = nc.tensor.transpose(bank[2 + par][:, t * P:(t + 1) * P], xn[:, par, t], ident[:])
                    last.then_inc(t_x, 1)
                if valid(g - 1):
                    o = 1 - par
                    wait(pe, e_x, g)
                    wait(pe, d_kq, g - 2)
                    for w, src in enumerate((cT, xT)):
                        for t in range(GT):
                            c = (w * GT + t) * DQ
                            last = nc.tensor.matmul(bank[4 + o][:, c:c + DQ], src[:, o, t * P:(t + 1) * P],
                                                    wq8[:], start=True, stop=True)
                    last.then_inc(t_mm, 1)
            groups(pe, step, 0, NG, 2, NG)

    kT = sb("kT", [P, 4, P])
    qT = sb("qT", [P, 4, P])
    g2 = sb("g2", [L, 2, L])
    gs = sb("gs", [L, L])
    cor = sb("cor", [P, L])
    c2 = sb("c2", [P, L])
    c3 = sb("c3", [P, L])
    top = sb("top", [P, 16])
    nmax = sb("nmax", [P, 1])
    ew = sb("ew", [P, L])
    wsh = sb("wsh", [P, L])
    wsum = sb("wsum", [P, 2])
    wrow = sb("wrow", [P, 2, L])
    circ = sb("circ", [P, P])
    bvb = sb("bvb", [P, P])
    m_t, m_g, m_v, m_cor, m_m2, m_cv = (sem(n) for n in ("m_t", "m_g", "m_v", "m_cor", "m_m2", "m_cv"))
    m_e, m_g2, m_bv, m_link, m_ex, m_w, m_z = (sem(n) for n in ("m_e", "m_g2", "m_bv", "m_link", "m_ex", "m_w", "m_z"))
    m_gd, m_gl, m_wd, m_wl = (sem(n) for n in ("m_gd", "m_gl", "m_wd", "m_wl"))

    with nc.Block() as block:
        @block.sync
        def _(sp):
            sp.wait_ge(m_g2, 1)
            sp.dma_start(corr_dram, g2[:].rearrange("t a s -> t (a s)")).then_inc(m_gd, 16)
            sp.wait_ge(m_gd, 16)
            sp.dma_start(gs[:], bass.AP(corr_dram.tensor, 0, [[2 * L + 1, L], [1, L]])).then_inc(m_gl, 16)
            sp.wait_ge(m_w, 1)
            sp.dma_start(shift_dram, wrow[0:1].rearrange("p a s -> p (a s)")).then_inc(m_wd, 16)
            sp.wait_ge(m_wd, 16)
            sp.wait_ge(m_z, 1)
            for i in range(2):
                sp.dma_start(circ[i * L:(i + 1) * L, i * L:(i + 1) * L],
                             bass.AP(shift_dram.tensor, 0, [[1, L], [1, L]])).then_inc(m_wl, 16)
            sp.wait_ge(m_wl, 32)

        @block.tensor
        def _(pe):
            for w in range(2):
                for blk in range(4):
                    last = nc.tensor.transpose(bank[w][:, blk * P:(blk + 1) * P],
                                               kq[:, w, 16 * blk:16 * blk + 16, :].rearrange("p t j -> p (t j)"),
                                               ident[:])
                last.then_inc(m_t, 1)
            pe.wait_ge(m_e, 2)
            n = 0
            for blk in range(4):
                for b in range(2):
                    last = nc.tensor.matmul(bank[2][0:L, 0:L], kT[:, blk, b * L:(b + 1) * L],
                                            qT[:, blk, b * L:(b + 1) * L], start=(n == 0), stop=(n == 7))
                    n += 1
            last.then_inc(m_g, 1)
            for i in range(2):
                for blk in range(4):
                    for b in range(2):
                        c = (blk * 2 + b) * L
                        last = nc.tensor.matmul(bank[3][i * L:(i + 1) * L, c:c + L], kT[:, blk, b * L:(b + 1) * L],
                                                sel[:, i], start=True, stop=True)
            last.then_inc(m_v, 1)
            pe.wait_ge(m_bv, 1)
            nc.tensor.matmul(bank[5][:, 0:D], bvb[:], wo[:], start=True, stop=True).then_inc(m_cv, 1)
            pe.wait_ge(m_gl, 16)
            nc.tensor.matmul(bank[4][:, 0:L], ones[0:L, :], gs[:], start=True, stop=True).then_inc(m_cor, 1)
            pe.wait_ge(m_wl, 32)
            nc.tensor.matmul(bank[4][:, P:2 * P], circ[:], wout[:], start=True, stop=True).then_inc(m_m2, 1)

        @block.scalar
        def _(act):
            act.wait_ge(m_t, 2)
            nc.scalar.copy(qT[:].rearrange("p b l -> p (b l)"), bank[1][:]).then_inc(m_e, 1)
            act.wait_ge(m_link, 6)
            nc.scalar.activation(ew[:], cor[:], ACT.Exp, bias=nmax[:]).then_inc(m_ex, 1)

        @block.vector
        def _(dve):
            dve.wait_ge(m_t, 1)
            nc.vector.tensor_copy(kT[:].rearrange("p b l -> p (b l)"), bank[0][:]).then_inc(m_e, 1)
            nc.vector.memset(circ[:], 0.0).then_inc(m_z, 1)
            nc.vector.tensor_scalar(bvb[:], ones[:], cols[:, C_BV:C_BV + 1], None, ALU.mult).then_inc(m_bv, 1)
            dve.wait_ge(m_g, 1)
            nc.vector.tensor_copy(g2[:], bank[2][0:L, 0:L].unsqueeze(1).broadcast_to([L, 2, L])).then_inc(m_g2, 1)
            dve.wait_ge(m_v, 1)
            for blk in range(4):
                nc.vector.tensor_copy(
                    vts[:, 16 * blk:16 * blk + 16].rearrange("p t b r -> p b t r"),
                    bank[3][:, blk * P:(blk + 1) * P].rearrange("p (b t r) -> p b t r", b=2, t=16))
            dve.wait_ge(m_cv, 1)
            nc.vector.tensor_tensor(cvec[:], bank[5][:, 0:D], bo_bc[:], ALU.add)

            links = [0]

            def link(ins):
                links[0] += 1
                ins.then_inc(m_link, 1)
                dve.wait_ge(m_link, links[0])

            dve.wait_ge(m_cor, 1)
            link(nc.vector.tensor_scalar(cor[:], bank[4][:, 0:L], 1.0 / (B * DQ), None, ALU.mult))
            link(nc.vector.max(top[:, 0:8], cor[:]))
            link(nc.vector.match_replace(c2[:], top[:, 0:8], cor[:], NEG))
            link(nc.vector.max(top[:, 8:16], c2[:]))
            link(nc.vector.memset(top[:, K_TOP:16], NEG))
            link(nc.vector.tensor_scalar(nmax[:], top[:, 0:1], -1.0, None, ALU.mult))
            link(nc.vector.match_replace(c3[:], top[:, 8:16], c2[:], NEG))
            link(nc.vector.tensor_tensor(c2[:], c3[:], cor[:], ALU.is_lt))
            dve.wait_ge(m_ex, 1)
            link(nc.vector.tensor_tensor(wsh[:], ew[:], c2[:], ALU.mult))
            link(nc.vector.tensor_reduce(wsum[:, 0:1], wsh[:], AX.X, ALU.add))
            link(nc.vector.reciprocal(wsum[:, 1:2], wsum[:, 0:1]))
            nc.vector.tensor_scalar(wrow[:], wsh[:].unsqueeze(1).broadcast_to([P, 2, L]), wsum[:, 1:2], None,
                                    ALU.mult).then_inc(m_w, 1)
            dve.wait_ge(m_m2, 1)
            nc.vector.tensor_copy(m2[:], bank[4][:, P:2 * P])


def attention(K, scope, vts, m2, cvec, wo):
    nc, a, bank, pair, cols, ident = K["nc"], K["a"], K["bank"], K["pair"], K["cols"], K["ident"]
    x3, xh2, xt_dram, logits, sem, s_const = K["x3"], K["xh2"], K["xt_dram"], K["logits"], K["sem"], K["s_const"]

    def sb(name, shape, dt=F32):
        return K["sb"](name, shape, dt, scope)

    wqk = sb("wqk", [P, 2 * D])
    wv = sb("wv", [P, 2, L])
    gc = sb("gc", [P, E + 2])
    bout = sb("bout", [P, D])
    identb = sb("identb", [P, P], BF16)
    msel = sb("msel", [32, 8, P], BF16)
    dmask = sb("dmask", [P, 4, L])
    xin = sb("xin", [P, 2, GT, D])
    x2 = sb("x2", [P, 2, GT, D])
    x1 = sb("x1", [P, 2, GT, D])
    xh = sb("xh", [P, 2, GT, D])
    vtx = sb("vtx", [P, 2, GT * P])
    xnT = sb("xnT", [P, 2, GT * P])
    qm = sb("qm", [P, 2, GB, 4, L])
    km = sb("km", [P, 2, GB, 2, L])
    qmb = sb("qmb", [P, 2, GB, 4, L], BF16)
    kmb = sb("kmb", [P, 2, GB, 2, L], BF16)
    vm = sb("vm", [P, 2, GB, 2, 4, L])
    pt = sb("pt", [P, 2, 2, 2, 4 * L])
    rd = sb("rd", [P, 2, P])
    ctxT = sb("ctxT", [P, 2, GT * P])
    mx = sb("mx", [P, 2, 16])
    mhl = sb("mhl", [P, 2, 32], BF16)
    mT = sb("mT", [32, 2, P], BF16)
    st6 = sb("st6a", [P, GT, 6])
    mv = sb("mva", [P, 2, GT, 2])
    st6b = sb("st6b", [P, GT, 6])
    mvb = sb("mvb", [P, GT, 2])
    rsb = sb("rsb", [P, GT])
    veb = sb("veb", [P, GT])
    pw = sb("pw", [P, 5, GT])
    rs = sb("rs", [P, 2, GT])
    r2 = sb("r2", [P, 2, GT])
    nhalf = sb("nhalf", [P, GT])
    eps = sb("eps", [P, GT])
    idle = sb("idle", [P, 1])
    bqm = sb("bqm", [P, 6])
    x2nT = sb("x2nT", [P, 2, GT * P])
    xh2s = sb("xh2s", [P, 2, GT, D])
    lgT = sb("lgT", [E + 2, GT * P])
    zero = sb("zero", [P, GT, D])

    g0, g1 = bank[0], bank[1]
    sbank = [bank[2], bank[3]]
    cd = bank[4]
    mps = bank[5][:, 0:P // 2].bitcast(BF16)
    lps = g1[:, 0:GT * (E + 2)]

    s_c2, s_z = sem("s_c2"), sem("s_z")
    s_xi, s_xt, s_x2 = ([sem(f"{n}{i}") for i in range(2)] for n in ("s_xi", "s_xt", "s_x2"))
    x2_dst = K["x2_dram"].rearrange("(t p) d -> p t d", p=P)
    (t_a, t_b, t_q, t_k, t_v, t_o, t_b2, t_g, t_l) = (sem("t_" + n) for n in "a b q k v o b2 g l".split())
    t_s, t_m, t_st, t_pv = (sem(n) for n in ("t_s", "t_m", "t_st", "t_pv"))
    e_vtx, e_qm, e_km, e_xh, e_x2n, e_lg, e_exp, e_mt = (
        sem("e_" + n) for n in "vtx qm km xh x2n lg exp mt".split())
    (d_c, d_max, d_mhi, d_mh, d_rd, d_ctx, d_xnT, d_qb, d_vm, d_x3, d_bsb, d_stb, d_xh2, d_x2, d_bs, d_st,
     d_x1, d_lg) = (sem("d_" + n) for n in
                    "c max mhi mh rd ctx xnT qb vm x3 bsb stb xh2 x2 bs st x1 lg".split())
    p_xb, p_c, p_b, p_rsb, p_r, p_x3, p_xh2 = (sem("p_" + n) for n in "xb c b rsb r x3 xh2".split())
    NC2 = 7
    LO, HI = 4, NG - 2
    FIRST, LAST = -2, NG + 2
    x_src = a["x"].rearrange("(t p) d -> p t d", p=P)

    with nc.Block() as block:
        @block.sync
        def _(sp):
            for dst, src in ((wqk[:], a["wqk"]), (wv[:], a["wv"]), (gc[:], a["gc"]), (identb[:].bitcast(U16), a["identb"]),
                             (msel[:].bitcast(U16), a["msel"]), (dmask[:], a["dmask"])):
                sp.dma_start(dst, src).then_inc(s_c2, 16)
            sp.dma_start(bout[:], a["bout"].partition_broadcast(P)).then_inc(s_c2, 16)

            def step(g, par):
                if valid(g + 3):
                    wait(sp, d_x2, g + 2)
                    sp.dma_start(xin[:, 1 - par], x_src[:, bass.ds((g + 3) * GT, GT), :]).then_inc(s_xi[1 - par], 16)
                if valid(g + 2):
                    wait(sp, d_x2, g + 3)
                    sp.dma_start(x2_dst[:, bass.ds((g + 2) * GT, GT), :], x2[:, par]).then_inc(s_x2[par], 16)
                if valid(g - 2):
                    wait(sp, e_x2n, g - 1)
                    sp.dma_start(xt_dram[bass.ds(g - 2, 1)].rearrange("g p c -> p (g c)"),
                                 x2nT[:, par]).then_inc(s_xt[par], 16)
            groups(sp, step, -3, LAST, LO, NG - 4)
            for i in range(2):
                sp.wait_ge(s_xt[i], 8 * NG)
                sp.wait_ge(s_x2[i], 8 * NG)
            sp.wait_ge(d_c, 1)
            zdst = K["xs_dram"].rearrange("(t p) d -> p t d", p=P)
            with sp.Fori(0, SLOTS // GT) as i:
                sp.dma_start(zdst[:, bass.ds(i * GT, GT), :], zero[:]).then_inc(s_z, 16)
            sp.wait_ge(s_z, 16 * (SLOTS // GT))

        @block.gpsimd
        def _(pool):
            pool.wait_ge(s_c2, 16 * NC2)
            pool.wait_ge(d_c, 1)
            bout_bc = bout[:].unsqueeze(1).broadcast_to([P, GT, D])
            cvec_bc = cvec[:].unsqueeze(1).broadcast_to([P, GT, D])

            def step(g, par):
                o = 1 - par
                if valid(g + 2):
                    wait(pool, s_xi[par], nth(g + 2, par), 16 * NG)
                    pool.tensor_tensor(xin[:, par], xin[:, par], bout_bc, ALU.add).then_inc(p_xb, 1)
                if valid(g - 1):
                    wait(pool, d_stb, g)
                    wait(pool, d_xh2, g - 1)
                    pool.tensor_tensor(veb[:], mvb[:, :, 1], eps[:], ALU.add).then_inc(p_b, 1)
                    wait(pool, p_b, g)
                    pool.tensor_tensor(rsb[:], veb[:], nhalf[:], ALU.pow).then_inc(p_rsb, 1)
                if valid(g + 2):
                    wait(pool, d_st, g + 3)
                    wait(pool, d_x1, g + 1)
                    wait(pool, e_xh, g + 1)
                    n = (g + 2) * 5
                    pool.tensor_tensor(pw[:, 0], mv[:, par, :, 1], eps[:], ALU.add).then_inc(p_c, 1)
                    wait(pool, p_c, n + 1, 5 * NG)
                    pool.tensor_tensor(rs[:, par], pw[:, 0], nhalf[:], ALU.pow).then_inc(p_c, 1)
                    wait(pool, p_c, n + 2, 5 * NG)
                    pool.tensor_tensor(pw[:, 1], rs[:, par], rs[:, par], ALU.mult).then_inc(p_c, 1)
                    wait(pool, p_c, n + 3, 5 * NG)
                    pool.tensor_tensor(pw[:, 2], pw[:, 1], mv[:, par, :, 1], ALU.mult).then_inc(p_c, 1)
                    wait(pool, p_c, n + 4, 5 * NG)
                    pool.tensor_tensor(pw[:, 3], pw[:, 2], eps[:], ALU.add).then_inc(p_c, 1)
                    wait(pool, p_c, n + 5, 5 * NG)
                    pool.tensor_tensor(r2[:, par], pw[:, 3], nhalf[:], ALU.pow).then_inc(p_r, 1)
                    wait(pool, d_x1, g + 3)
                    pool.tensor_tensor(x3[:, bass.ds((g + 2) * GT, GT), :], x1[:, par], cvec_bc,
                                       ALU.add).then_inc(p_x3, 1)
                if valid(g - 1):
                    wait(pool, d_xh2, g)
                    pool.tensor_copy(xh2[:, bass.ds((g - 1) * GT, GT), :], xh2s[:, o]).then_inc(p_xh2, 1)
            groups(pool, step, FIRST, LAST, LO, HI)

        @block.scalar
        def _(act):
            act.wait_ge(d_c, 1)

            def xpose_max(T, t):
                if valid(T + 2, NT):
                    q = t % 2
                    wait(act, t_m, T + 3, NT)
                    wait(act, t_st, T + 1, NT)
                    nc.scalar.copy(mT[:, q], mps[0:32, :]).then_inc(e_mt, 1)

            def step(g, par):
                o = 1 - par
                for t in range(GT):
                    T = g * GT + t
                    if valid(T + 1, NT):
                        q = (t + 1) % 2
                        wait(act, t_st, T + 2, NT)
                        wait(act, t_pv, T, NT)
                        nc.scalar.activation(pt[:, q].rearrange("p r b c -> p (r b c)"),
                                             pair[:].rearrange("p r c -> p (r c)"), ACT.Exp).then_inc(e_exp, 1)
                    if t == 0 and valid(g + 2):
                        wait(act, t_a, g + 1)
                        nc.scalar.copy(
                            vtx[:, par].rearrange("p (t l r) -> p t l r", l=16, r=4),
                            vts[:, bass.ds((g + 2) * GT, GT)].rearrange("p t b r -> p (t b) r").unsqueeze(2)
                            .broadcast_to([P, GB, 16, 4])).then_inc(e_vtx, 1)
                    if t == 1 and valid(g + 1):
                        wait(act, t_k, g + 2)
                        wait(act, t_st, g * GT, NT)
                        wait(act, d_qb, g)
                        for h2 in range(2):
                            last = nc.scalar.activation(
                                km[:, o, :, h2], g1[:].rearrange("p (b k) -> p b k", b=GB), ACT.Identity,
                                bias=bqm[:, 4 + h2:5 + h2], scale=cols[:, C_MK + h2:C_MK + h2 + 1])
                        last.then_inc(e_km, 1)
                    if t == 3 and valid(g - 2):
                        wait(act, t_b2, g - 1)
                        wait(act, t_g, g - 3)
                        wait(act, s_xt[par], nth(g - 4, par), 16 * NG)
                        nc.scalar.activation(x2nT[:, par], g1[:], ACT.Identity,
                                             bias=cols[:, C_B2:C_B2 + 1],
                                             scale=cols[:, C_G2:C_G2 + 1]).then_inc(e_x2n, 1)
                    xpose_max(T, t)
                    if t == 0 and valid(g + 1):
                        wait(act, t_q, g + 2)
                        wait(act, t_st, g * GT, NT)
                        wait(act, d_qb, g)
                        for hp in range(4):
                            last = nc.scalar.activation(
                                qm[:, o, :, hp], g0[:].rearrange("p (b q) -> p b q", b=GB), ACT.Identity,
                                bias=bqm[:, hp:hp + 1], scale=cols[:, C_MQ + hp:C_MQ + hp + 1])
                        last.then_inc(e_qm, 1)
                    if t == 3 and valid(g + 2):
                        wait(act, p_r, g + 3)
                        wait(act, d_x1, g + 3)
                        wait(act, t_b, g + 1)
                        for i in range(GT):
                            last = nc.scalar.activation(xh[:, par, i], x1[:, par, i], ACT.Copy,
                                                        scale=r2[:, par, i:i + 1])
                        last.then_inc(e_xh, 1)
                    if t == 3 and valid(g - 2):
                        wait(act, t_g, g - 1)
                        wait(act, t_l, g - 2)
                        nc.scalar.copy(lgT[:], g0[0:E + 2, :]).then_inc(e_lg, 1)
            groups(act, step, FIRST, LAST, LO, HI)

        @block.vector
        def _(dve):
            nc.vector.memset(zero[:], 0.0)
            nc.vector.memset(nhalf[:], -0.5)
            nc.vector.memset(eps[:], EPS)
            nc.vector.memset(vm[:], 0.0)
            for hp in range(4):
                nc.vector.tensor_tensor(bqm[:, hp:hp + 1], cols[:, C_BQ:C_BQ + 1],
                                        cols[:, C_MQ + hp:C_MQ + hp + 1], ALU.mult)
            for h2 in range(2):
                last = nc.vector.tensor_tensor(bqm[:, 4 + h2:5 + h2], cols[:, C_BK:C_BK + 1],
                                               cols[:, C_MK + h2:C_MK + h2 + 1], ALU.mult)
            last.then_inc(d_c, 1)
            dve.wait_ge(d_c, 1)

            def maxima(T, t):
                if valid(T + 2, NT):
                    q = t % 2
                    wait(dve, t_s, T + 3, NT)
                    for r in range(2):
                        last = nc.vector.tensor_reduce(mx[:, q, 8 * r:8 * r + 8],
                                                       sbank[r][:].rearrange("p (n k) -> p n k", k=L), AX.X, ALU.max)
                    last.then_inc(d_max, 1)
                    wait(dve, d_max, T + 3, NT)
                    wait(dve, t_m, T + 1, NT)
                    nc.vector.tensor_scalar(mhl[:, q, 0:16], mx[:, q], -1.0, None, ALU.mult).then_inc(d_mhi, 1)
                    wait(dve, d_mhi, T + 3, NT)
                    nc.vector.scalar_tensor_tensor(mhl[:, q, 16:32], mx[:, q], -1.0, mhl[:, q, 0:16],
                                                   ALU.mult, ALU.subtract).then_inc(d_mh, 1)

            def normalise(g, T, t, par):
                if valid(T, NT):
                    q = t % 2
                    wait(dve, t_pv, T + 1, NT)
                    nc.vector.reciprocal(rd[:, q], cd[:, P:2 * P]).then_inc(d_rd, 1)
                    wait(dve, d_rd, T + 1, NT)
                    if t == 0:
                        wait(dve, t_o, g - 1)
                    nc.vector.tensor_tensor(ctxT[:, par, t * P:(t + 1) * P], cd[:, 0:P], rd[:, q],
                                            ALU.mult).then_inc(d_ctx, 1)

            def step(g, par):
                o = 1 - par
                for t in range(GT):
                    T = g * GT + t
                    maxima(T, t)
                    if t == 0:
                        if valid(g + 1):
                            wait(dve, t_b, g + 2)
                            wait(dve, t_v, g)
                            nc.vector.tensor_scalar(xnT[:, o], g1[:], cols[:, C_G1:C_G1 + 1],
                                                    cols[:, C_B1:C_B1 + 1], ALU.mult, ALU.add).then_inc(d_xnT, 1)
                    if t == 1 and valid(g + 1):
                        wait(dve, e_qm, g + 2)
                        wait(dve, t_s, g * GT, NT)
                        nc.vector.tensor_copy(qmb[:, o].rearrange("p b h q -> p (b h q)"),
                                              qm[:, o].rearrange("p b h q -> p (b h q)"))
                        wait(dve, e_km, g + 2)
                        nc.vector.tensor_copy(kmb[:, o].rearrange("p b h k -> p (b h k)"),
                                              km[:, o].rearrange("p b h k -> p (b h k)")).then_inc(d_qb, 1)
                    if t == 2 and valid(g - 1):
                        wait(dve, t_o, g)
                        wait(dve, p_x3, g)
                        xg = x3[:, bass.ds((g - 1) * GT, GT), :]
                        nc.vector.tensor_tensor(xg, xg, g1[:].rearrange("p (t d) -> p t d", t=GT),
                                                ALU.add).then_inc(d_x3, 1)
                        wait(dve, d_x3, g)
                        settle(nc.vector, idle[:])
                        for i in range(GT):
                            last = nc.vector.bn_stats(st6b[:, i], x3[:, (g - 1) * GT + i, :])
                        last.then_inc(d_bsb, 1)
                        wait(dve, d_bsb, g)
                        settle(nc.vector, idle[:])
                        for i in range(GT):
                            last = nc.vector.bn_aggr(mvb[:, i], st6b[:, i])
                        last.then_inc(d_stb, 1)
                    normalise(g, T, t, par)
                    if t == 0 and valid(g - 3):
                        wait(dve, t_l, g - 2)
                        nc.vector.tensor_copy(logits[:, bass.ds((g - 3) * GT, GT), :],
                                              lps.rearrange("p (t e) -> p t e", t=GT)).then_inc(d_lg, 1)
                    if t == 1 and valid(g + 1):
                        wait(dve, t_v, g + 2)
                        wait(dve, t_pv, g * GT, NT)
                        for h2 in range(2):
                            rows = slice(h2 * L, (h2 + 1) * L)
                            dst = vm[rows, o].rearrange("p b r h (c e d) -> p (b r) (h c) (e d)", c=4, e=2)
                            last = nc.vector.tensor_copy(
                                dst[:, :, 0:16:5, h2 * DH:(h2 + 1) * DH],
                                g0[rows].rearrange("p (n h d) -> p n h d", h=4, d=DH))
                        last.then_inc(d_vm, 1)
                    if t == 2 and valid(g + 2):
                        wait(dve, t_a, g + 3)
                        wait(dve, p_xb, g + 3)
                        wait(dve, d_x1, g + 1)
                        wait(dve, s_x2[par], nth(g, par), 16 * NG)
                        nc.vector.tensor_tensor(x2[:, par], g0[:].rearrange("p (t d) -> p t d", t=GT),
                                                xin[:, par], ALU.add).then_inc(d_x2, 1)
                        wait(dve, d_x2, g + 3)
                        for i in range(GT):
                            last = nc.vector.bn_stats(st6[:, i], x2[:, par, i])
                        last.then_inc(d_bs, 1)
                        wait(dve, d_bs, g + 3)
                        wait(dve, p_r, g + 1)
                        settle(nc.vector, idle[:])
                        for i in range(GT):
                            last = nc.vector.bn_aggr(mv[:, par, i], st6[:, i])
                        last.then_inc(d_st, 1)
                    if t == 3 and valid(g - 1):
                        wait(dve, p_rsb, g)
                        wait(dve, t_b2, g - 2)
                        wait(dve, p_xh2, g - 2)
                        for i in range(GT):
                            last = nc.vector.tensor_scalar(xh2s[:, o, i], x3[:, (g - 1) * GT + i, :],
                                                           mvb[:, i, 0:1], rsb[:, i:i + 1], ALU.subtract, ALU.mult)
                        last.then_inc(d_xh2, 1)
                    if t == 3 and valid(g + 2):
                        wait(dve, p_c, (g + 2) * 5 + 2, 5 * NG)
                        wait(dve, e_xh, g + 1)
                        wait(dve, p_x3, g + 1)
                        for i in range(GT):
                            last = nc.vector.tensor_scalar(x1[:, par, i], x2[:, par, i], mv[:, par, i, 0:1],
                                                           rs[:, par, i:i + 1], ALU.subtract, ALU.mult)
                        last.then_inc(d_x1, 1)
            groups(dve, step, FIRST, LAST, LO, HI)

        @block.tensor
        def _(pe):
            pe.wait_ge(s_c2, 16 * NC2)

            def scores_q(T, t, qpar):
                if valid(T + 2, NT):
                    wait(pe, d_max, T + 2, NT)
                    lb = (t + 2) % GT * 2
                    for b in range(2):
                        for hh in range(2):
                            for r in range(2):
                                rows = slice(r * L, (r + 1) * L)
                                c = (b * 2 + hh) * P
                                last = nc.tensor.matmul(
                                    sbank[r][:, c:c + P],
                                    qmb[rows, qpar, lb + b, 2 * hh:2 * hh + 2].rearrange("p h q -> p (h q)"),
                                    kmb[rows, qpar, lb + b].rearrange("p h k -> p (h k)"),
                                    start=True, stop=True)
                    last.then_inc(t_s, 1)

            def scores_k(T, t, kpar):
                if valid(T + 1, NT):
                    q = (t + 1) % 2
                    wait(pe, e_exp, T + 1, NT)
                    lb = (t + 1) % GT * 2
                    for b in range(2):
                        for r in range(2):
                            rows = slice(r * L, (r + 1) * L)
                            nc.tensor.matmul(
                                pair[:, r, b * 4 * L:(b + 1) * 4 * L],
                                km[rows, kpar, lb + b].rearrange("p h k -> p (h k)"),
                                qm[rows, kpar, lb + b].rearrange("p h q -> p (h q)"),
                                start=(b == 0), stop=False, skip_group_check=True)
                    wait(pe, e_mt, T + 2, NT)
                    for r in range(2):
                        for b in range(2):
                            for hh in range(2):
                                n = (r * 2 + b) * 2 + hh
                                c = (b * 2 + hh) * P
                                last = nc.tensor.matmul(pair[:, r, c:c + P], msel[:, n], mT[:, q],
                                                        start=False, stop=(b == 1 and hh == 1),
                                                        skip_group_check=True)
                    last.then_inc(t_st, 1)

            def weighted(g, T, t, par):
                if valid(T, NT):
                    q = t % 2
                    wait(pe, e_exp, T + 1, NT)
                    if t == 0:
                        wait(pe, d_vm, g + 1)
                    wait(pe, d_ctx, T, NT)
                    for den in range(2):
                        for b in range(2):
                            for hp in range(4):
                                for r in range(2):
                                    lhs = dmask[:, hp] if den else vm[:, par, t * 2 + b, r, hp]
                                    c = den * P + b * L
                                    last = nc.tensor.matmul(
                                        cd[r * L:(r + 1) * L, c:c + L], lhs,
                                        pt[:, q, r, b, hp * L:(hp + 1) * L], start=(hp == 0), stop=(hp == 3))
                    last.then_inc(t_pv, 1)

            def xpose_max(T, t):
                if valid(T + 2, NT):
                    q = t % 2
                    wait(pe, d_mh, T + 3, NT)
                    wait(pe, e_mt, T + 2, NT)
                    nc.tensor.transpose(mps[0:32, :], mhl[:, q], identb[:]).then_inc(t_m, 1)

            def step(g, par):
                o = 1 - par
                for t in range(GT):
                    T = g * GT + t
                    scores_k(T, t, par if t < 3 else o)
                    if t == 2 and valid(g + 1):
                        wait(pe, d_qb, g + 2)
                    scores_q(T, t, par if t < 2 else o)
                    if t == 0 and valid(g + 1):
                        wait(pe, e_xh, g + 2)
                        wait(pe, e_x2n, g - 2)
                        for i in range(GT):
                            last = nc.tensor.transpose(g1[:, i * P:(i + 1) * P], xh[:, o, i], ident[:])
                        last.then_inc(t_b, 1)
                    if t == 1 and valid(g + 1):
                        wait(pe, d_lg, g - 2)
                        nc.tensor.matmul(g1[:], wqk[:, D:2 * D], xnT[:, o], start=True, stop=True).then_inc(t_k, 1)
                    if t == 2 and valid(g - 1):
                        wait(pe, d_ctx, g * GT, NT)
                        wait(pe, e_km, g + 2)
                        wait(pe, d_lg, g - 2)
                        for i in range(GT):
                            last = nc.tensor.matmul(g1[:, i * P:(i + 1) * P], ctxT[:, o, i * P:(i + 1) * P], wo[:],
                                                    start=True, stop=True)
                        last.then_inc(t_o, 1)
                    if t == 3 and valid(g - 2):
                        wait(pe, d_xh2, g - 1)
                        wait(pe, d_x3, g)
                        wait(pe, d_lg, g - 2)
                        for i in range(GT):
                            last = nc.tensor.transpose(g1[:, i * P:(i + 1) * P], xh2s[:, par, i], ident[:])
                        last.then_inc(t_b2, 1)
                    weighted(g, T, t, par)
                    xpose_max(T, t)
                    if t == 0 and valid(g + 1):
                        wait(pe, d_xnT, g + 2)
                        wait(pe, e_lg, g - 2)
                        nc.tensor.matmul(g0[:], wqk[:, 0:D], xnT[:, o], start=True, stop=True).then_inc(t_q, 1)
                    if t == 0 and valid(g - 3):
                        wait(pe, e_lg, g - 2)
                        wait(pe, d_xnT, g + 2)
                        for i in range(GT):
                            last = nc.tensor.matmul(lps[:, i * (E + 2):(i + 1) * (E + 2)],
                                                    lgT[:, i * P:(i + 1) * P], ident[0:E + 2, 0:E + 2],
                                                    start=True, stop=True)
                        last.then_inc(t_l, 1)
                    if t == 1 and valid(g + 1):
                        wait(pe, e_qm, g + 2)
                        for b in range(GB):
                            for h2 in range(2):
                                last = nc.tensor.matmul(g0[h2 * L:(h2 + 1) * L, b * L:(b + 1) * L],
                                                        xnT[:, o, b * L:(b + 1) * L], wv[:, h2],
                                                        start=True, stop=True)
                        last.then_inc(t_v, 1)
                    if t == 2 and valid(g + 2):
                        wait(pe, e_vtx, g + 3)
                        wait(pe, d_vm, g + 2)
                        for i in range(GT):
                            last = nc.tensor.matmul(g0[:, i * P:(i + 1) * P], vtx[:, par, i * P:(i + 1) * P], m2[:],
                                                    start=True, stop=True)
                        last.then_inc(t_a, 1)
                    if t == 3 and valid(g - 2):
                        wait(pe, e_x2n, g - 1)
                        wait(pe, d_x2, g + 3)
                        wait(pe, d_vm, g + 2)
                        wait(pe, e_lg, g - 2)
                        nc.tensor.matmul(g0[0:E + 2, :], gc[:], x2nT[:, par],
                                         start=True, stop=True).then_inc(t_g, 1)
            groups(pe, step, FIRST, LAST, LO, HI)


def experts(K, scope):
    nc, a, out, bank, pair, cols, ident, ones = (K[n] for n in "nc a out bank pair cols ident ones".split())
    x3, xh2, xt_dram, logits, sem = K["x3"], K["xh2"], K["xt_dram"], K["logits"], K["sem"]
    xs_dram, ys_dram = K["xs_dram"], K["ys_dram"]

    def sb(name, shape, dt=F32):
        return K["sb"](name, shape, dt, scope)

    w1 = sb("w1", [P, E, W1W])
    w2 = sb("w2", [P, E, FC * D])
    b2 = sb("b2", [1, E * D])
    rw1 = sb("rw1", [P, FF])
    rw2 = sb("rw2", [P, FC, D])
    rb2 = sb("rb2", [P, D])
    one = sb("one", [P, P])
    c1 = sb("c1", [P, NT])
    c0g = sb("c0g", [P, NT])
    slot = sb("slot", [P, NT], I32)
    eid = sb("eid", [1, SLOTS], I32)
    s_w, d_idx = sem("r_w"), sem("r_idx")
    NW = 9
    with ExitStack() as rt:
        def rb(name, shape, dt=F32):
            return K["sb"](name, shape, dt, rt)

        prio = rb("prio", [P, E])
        triu = rb("triu", [P, P], BF16)
        oneb = rb("oneb", [P, P], BF16)
        jrow = rb("jrow", [1, SLOTS])
        dif = rb("dif", [P, NT, E])
        ex = rb("ex", [P, NT, E])
        oh = rb("oh", [P, NT, E])
        ohb = rb("ohb", [P, NT, E], BF16)
        tmp = rb("tmp", [P, NT, E])
        cum = [rb(f"cum{i}", [P, NT + 1, E]) for i in range(2)]
        cumb = rb("cumb", [P, NT + 1, E], BF16)
        r1 = rb("r1", [P, NT])
        gate = rb("gate", [P, NT])
        cl = rb("cl", [P, NT, 2])
        ec = rb("ec", [P, NT, 2])
        small = rb("small", [P, 8, E])
        smalli = rb("smalli", [P, 2, E], I32)
        cmp = rb("cmp", [1, SLOTS, E])
        er = rb("er", [1, SLOTS])
        r_d, r_e, r_ec, r_oh, r_cum, r_rank, r_tot = (sem("r_" + n) for n in "d e ec oh cum rank tot".split())
        s_r = sem("s_r")

        def per_tile(v):
            return v[:].unsqueeze(2).broadcast_to([P, NT, E])

        with nc.Block() as block:
            @block.sync
            def _(sp):
                for dst, src in ((prio[:], a["prio"].partition_broadcast(P)), (triu[:].bitcast(U16), a["triu"]),
                                 (oneb[:].bitcast(U16), a["oneb"]), (jrow[:], a["jrow"])):
                    sp.dma_start(dst, src).then_inc(s_r, 16)
                for dst, src in ((rw1[:], a["rw1"]), (rw2[:], a["rw2"]), (rb2[:], a["rb2"].partition_broadcast(P)),
                                 (b2[:], a["b2"]), (one[:], a["one"]), (w1[:, 0:4], a["w1"][:, 0:4]),
                                 (w2[:, 0:4], a["w2"][:, 0:4]), (w1[:, 4:8], a["w1"][:, 4:8]),
                                 (w2[:, 4:8], a["w2"][:, 4:8])):
                    sp.dma_start(dst, src).then_inc(s_w, 16)

            @block.scalar
            def _(act):
                act.wait_ge(r_e, 1)
                nc.scalar.activation(ex[:].rearrange("p t e -> p (t e)"), dif[:].rearrange("p t e -> p (t e)"),
                                     ACT.Exp).then_inc(r_ec, 1)
                act.wait_ge(r_e, 2)
                nc.scalar.activation(ec[:].rearrange("p t e -> p (t e)"), cl[:].rearrange("p t e -> p (t e)"),
                                     ACT.Exp).then_inc(r_ec, 1)

            @block.tensor
            def _(pe):
                pe.wait_ge(s_r, 64)
                pe.wait_ge(r_oh, 1)
                pe.wait_ge(r_cum, 1)
                nc.tensor.matmul(bank[0][:], triu[:], ohb[:].rearrange("p t e -> p (t e)"), start=True, stop=False)
                nc.tensor.matmul(bank[0][:], oneb[:], cumb[:, 0:NT].rearrange("p t e -> p (t e)"),
                                 start=False, stop=True)
                nc.tensor.matmul(bank[1][:, 0:E], oneb[:], cumb[:, NT], start=True, stop=True).then_inc(r_rank, 1)

            @block.vector
            def _(dve):
                links = [0]

                def link(ins):
                    links[0] += 1
                    ins.then_inc(r_d, 1)
                    dve.wait_ge(r_d, links[0])

                lg = logits[:, :, 0:E]
                link(nc.vector.tensor_reduce(r1[:], lg, AX.X, ALU.max))
                nc.vector.tensor_tensor(dif[:], lg, per_tile(r1), ALU.subtract).then_inc(r_e, 1)
                dve.wait_ge(r_e, 1)
                dve.wait_ge(s_r, 64)
                link(nc.vector.scalar_tensor_tensor(tmp[:], dif[:], 0.0,
                                                    prio[:].unsqueeze(1).broadcast_to([P, NT, E]), ALU.is_ge, ALU.mult))
                link(nc.vector.tensor_reduce(r1[:], tmp[:], AX.X, ALU.max))
                link(nc.vector.tensor_tensor(oh[:], tmp[:], per_tile(r1), ALU.is_equal))
                nc.vector.tensor_copy(ohb[:], oh[:]).then_inc(r_oh, 1)
                nc.vector.memset(cum[0][:, 0], 0.0)
                nc.vector.memset(cum[1][:, 0], 0.0)
                link(nc.vector.tensor_copy(cum[0][:, 1:NT + 1], oh[:]))
                k, src, dst = 1, cum[0], cum[1]
                while k < NT:
                    nc.vector.tensor_copy(dst[:, 1:k + 1], src[:, 1:k + 1])
                    link(nc.vector.tensor_tensor(dst[:, k + 1:NT + 1], src[:, k + 1:NT + 1], src[:, 1:NT + 1 - k],
                                                 ALU.add))
                    k, src, dst = 2 * k, dst, src
                nc.vector.tensor_copy(cumb[:], src[:]).then_inc(r_cum, 1)
                dve.wait_ge(r_ec, 1)
                link(nc.vector.tensor_reduce(r1[:], ex[:], AX.X, ALU.add))
                link(nc.vector.reciprocal(gate[:], r1[:]))
                link(nc.vector.tensor_tensor(cl[:], logits[:, :, E:E + 2],
                                             K["coefb"][:].unsqueeze(1).broadcast_to([P, NT, 2]), ALU.add))
                link(nc.vector.tensor_reduce(r1[:], cl[:], AX.X, ALU.max))
                nc.vector.tensor_tensor(cl[:], cl[:], r1[:].unsqueeze(2).broadcast_to([P, NT, 2]),
                                        ALU.subtract).then_inc(r_e, 1)
                dve.wait_ge(r_ec, 2)
                link(nc.vector.tensor_reduce(r1[:], ec[:], AX.X, ALU.add))
                link(nc.vector.reciprocal(c0g[:], r1[:]))
                link(nc.vector.tensor_tensor(c1[:], ec[:, :, 1], c0g[:], ALU.mult))
                link(nc.vector.tensor_tensor(c0g[:], ec[:, :, 0], c0g[:], ALU.mult))
                link(nc.vector.tensor_tensor(c0g[:], c0g[:], gate[:], ALU.mult))
                dve.wait_ge(r_rank, 1)
                link(nc.vector.tensor_scalar(smalli[:, 0], bank[1][:, 0:E], float(P - 1), None, ALU.add))
                link(nc.vector.tensor_scalar(smalli[:, 1], smalli[:, 0], 7, None, ALU.logical_shift_right))
                link(nc.vector.tensor_copy(small[:, 0], smalli[:, 1]))
                k, i = 1, 0
                while k < E:
                    nc.vector.tensor_copy(small[:, i + 1, 0:k], small[:, i, 0:k])
                    link(nc.vector.tensor_tensor(small[:, i + 1, k:E], small[:, i, k:E], small[:, i, 0:E - k], ALU.add))
                    k, i = 2 * k, i + 1
                end = small[:, i]
                link(nc.vector.tensor_tensor(small[:, i + 1], end, small[:, 0], ALU.subtract))
                link(nc.vector.tensor_scalar(small[:, i + 2], small[:, i + 1], float(P), None, ALU.mult))
                link(nc.vector.tensor_tensor(cmp[:], jrow[:].unsqueeze(2).broadcast_to([1, SLOTS, E]),
                                             end[0:1].unsqueeze(1).broadcast_to([1, SLOTS, E]), ALU.is_ge))
                link(nc.vector.tensor_reduce(er[:], cmp[:], AX.X, ALU.add))
                link(nc.vector.tensor_scalar(eid[:], er[:], float(E - 1), None, ALU.min))
                link(nc.vector.tensor_tensor(tmp[:], bank[0][:].rearrange("p (t e) -> p t e", e=E),
                                             small[:, i + 2].unsqueeze(1).broadcast_to([P, NT, E]), ALU.add))
                link(nc.vector.tensor_tensor(tmp[:], tmp[:], oh[:], ALU.mult))
                link(nc.vector.tensor_reduce(r1[:], tmp[:], AX.X, ALU.add))
                nc.vector.tensor_copy(slot[:], r1[:]).then_inc(d_idx, 1)
                dve.wait_ge(d_idx, 1)

    hs = sb("hs", [P, 2, FC, GT * P])
    x2g = sb("x2g", [P, 2, GT, D])
    x2_v = K["x2_dram"].rearrange("(t p) d -> p t d", p=P)
    f_a = sem("f_a")
    tmp2 = sb("tmp2", [P, GT, D])
    xg = sb("xg", [P, 2, GT * P])
    xsl = sb("xsl", [P, 2, 2, D])
    xsT = sb("xsT", [P, 2, 2 * P])
    w1b = sb("w1b", [P, 2, W1W])
    hT = sb("hT", [P, 2, FC, P])
    ysb = sb("ysb", [P, 2, 2, D])
    gb = sb("gb", [P, 2, GT, D])
    rbank = bank[2]
    xbank = bank[3]
    s_sc = sem("s_sc")
    s_xr = [sem(f"s_xr{i}") for i in range(2)]
    s_xs, s_ys, s_g, s_out, s_xg = ([sem(f"{n}{i}") for i in range(2)] for n in "s_xs s_ys s_g s_out s_xg".split())
    f_l1, f_ge, f_l2, f_r, f_x3, f_fin = (sem("f_" + n) for n in "l1 ge l2 r x3 fin".split())
    x_tr, x_xt, x_w1, x_l1, x_ge, x_l2, x_y = (sem("x_" + n) for n in "tr xt w1 l1 ge l2 y".split())
    HALF = NG // 2
    NU = SLOTS // 2
    out_v = out.rearrange("(t p) d -> p t d", p=P)
    xs_v = xs_dram.rearrange("(t p) d -> p t d", p=P)
    ys_v = ys_dram.rearrange("(t p) d -> p t d", p=P)

    with nc.Block() as block:
        @block.sync
        def _(sp):
            sp.wait_ge(s_sc, 16 * NT)

            def step(u, par):
                if valid(u, NU):
                    wait(sp, x_tr, u - 1, NU)
                    sp.dma_start(xsl[:, par], xs_v[:, bass.ds(u * 2, 2), :]).then_inc(s_xs[par], 16)
                if valid(u - 2, NU):
                    wait(sp, x_y, 2 * (u - 1), SLOTS)
                    sp.dma_start(ys_v[:, bass.ds((u - 2) * 2, 2), :], ysb[:, par]).then_inc(s_ys[par], 16)
            groups(sp, step, 0, NU + 1, 2, NU)

            def store(g, par):
                wait(sp, f_fin, g + 1)
                sp.dma_start(out_v[:, bass.ds(g * GT, GT), :], gb[:, par]).then_inc(s_out[par], 16)
            groups(sp, store, 0, NG - 1, 2, NG)
            for i in range(2):
                sp.wait_ge(s_ys[i], 8 * NU)
                sp.wait_ge(s_out[i], 8 * NG)

        @block.gpsimd
        def _(pool):
            for T in range(NT):
                pool.indirect_dma_start(xs_dram, bass.IndirectOffsetOnAxis(ap=slot[:, T:T + 1], axis=0),
                                        xh2[:, T], None).then_inc(s_sc, 16)
            pool.wait_ge(s_sc, 16 * NT)
            for i in range(2):
                pool.wait_ge(s_ys[i], 8 * NU)
            for T in range(NT):
                g = T // GT
                if T % GT == 0:
                    wait(pool, s_out[g % 2], nth(g - 2, g % 2), 16 * NG)
                pool.indirect_dma_start(gb[:, g % 2, T % GT], None, ys_dram,
                                        bass.IndirectOffsetOnAxis(ap=slot[:, T:T + 1], axis=0)).then_inc(s_g[g % 2], 16)

        @block.scalar
        def _(act):
            def load(g, par):
                wait(act, f_l1, FC * (g - 1), FC * NG)
                act.dma_start(xg[:, par], xt_dram[bass.ds(g, 1)].rearrange("g p c -> p (g c)")).then_inc(s_xg[par], 16)
                wait(act, f_a, g - 1)
                act.dma_start(x2g[:, par], x2_v[:, bass.ds(g * GT, GT), :]).then_inc(s_xr[par], 16)

            def shared(lo, hi):
                load(lo, lo % 2)

                def step(g, par):
                    if not isinstance(g, int) or g + 1 < hi:
                        load(g + 1, 1 - par)
                    for j in range(FC):
                        wait(act, f_l2, g - 1)
                        wait(act, f_l1, FC * g + j + 1, FC * NG)
                        nc.scalar.activation(hs[:, par, j], bank[j % 2][:], ACT.Gelu,
                                             bias=cols[:, C_RB1 + j:C_RB1 + j + 1]).then_inc(f_ge, 1)
                groups(act, step, lo, hi - 1, lo + 2, hi - 2)
            shared(0, HALF)

            def step(u, par):
                for k in range(2):
                    v = u * 2 + k
                    wait(act, x_l1, v + 1, SLOTS)
                    wait(act, x_l2, v - 1, SLOTS)
                    for j in range(FC):
                        last = nc.scalar.activation(hT[:, k, j], pair[:, k, j * P:(j + 1) * P], ACT.Gelu,
                                                    bias=w1b[:, k, FF + j:FF + j + 1])
                    last.then_inc(x_ge, 1)
            groups(act, step, 0, NU - 1, 2, NU)
            shared(HALF, NG)

        @block.vector
        def _(dve):
            rb2_bc = rb2[:].unsqueeze(1).broadcast_to([P, GT, D])
            dve.wait_ge(s_w, 16 * NW)

            def shared(g, par):
                rows = x3[:, bass.ds(g * GT, GT), :]
                wait(dve, s_xr[par], nth(g, par), 16 * NG)
                nc.vector.tensor_tensor(rows, rows, x2g[:, par], ALU.add).then_inc(f_a, 1)
                wait(dve, f_l2, g + 1)
                wait(dve, f_x3, g)
                nc.vector.tensor_tensor(tmp2[:], rbank[:].rearrange("p (t d) -> p t d", t=GT), rb2_bc,
                                        ALU.add).then_inc(f_r, 1)
                wait(dve, f_r, g + 1)
                wait(dve, f_a, g + 1)
                for i in range(GT):
                    T = g * GT + i
                    last = nc.vector.scalar_tensor_tensor(x3[:, T, :], tmp2[:, i], c1[:, bass.ds(T, 1)],
                                                          x3[:, T, :], ALU.mult, ALU.add)
                last.then_inc(f_x3, 1)

            def final(g, par):
                wait(dve, s_g[par], GT * nth(g, par), 16 * NT)
                wait(dve, f_x3, g + 1)
                for i in range(GT):
                    T = g * GT + i
                    last = nc.vector.scalar_tensor_tensor(gb[:, par, i], gb[:, par, i], c0g[:, bass.ds(T, 1)],
                                                          x3[:, T, :], ALU.mult, ALU.add)
                last.then_inc(f_fin, 1)

            groups(dve, shared, 0, HALF - 1, 2, HALF)

            def spread(u, par):
                wait(dve, x_tr, u + 1, NU)
                wait(dve, x_l1, 2 * (u - 1), SLOTS)
                nc.vector.tensor_scalar(xsT[:, par], xbank[:, 0:2 * P], cols[:, C_G2:C_G2 + 1],
                                        cols[:, C_B2:C_B2 + 1], ALU.mult, ALU.add).then_inc(x_xt, 1)

            def rows_out(v, pair_of_v, par, k):
                wait(dve, x_l2, v + 1, SLOTS)
                if k == 0:
                    wait(dve, s_ys[par], nth(pair_of_v - 2, par, NU), 16 * NU)
                nc.vector.tensor_copy(ysb[:, par, k], bank[4 + k][:, 0:D]).then_inc(x_y, 1)

            def step(u, par):
                if valid(u, NU):
                    spread(u, par)
                for k in range(2):
                    v = u * 2 + k
                    if valid(u, NU):
                        wait(dve, x_ge, v - 1, SLOTS)
                        e = dve.value_load(eid[0:1, bass.ds(v, 1)], min_val=0, max_val=E - 1)
                        nc.vector.tensor_copy(w1b[:, k], w1[:, e, :]).then_inc(x_w1, 1)
                    if valid(v - 1, SLOTS):
                        rows_out(v - 1, u - 1 + k, par if k else 1 - par, 1 - k)
            groups(dve, step, 0, NU, 2, NU)

            def tail(g, par):
                shared(g, par)
                final(g - HALF, par)
            groups(dve, tail, HALF, NG - 1, HALF + 2, NG)
            groups(dve, final, HALF, NG - 1, HALF, NG)

        @block.tensor
        def _(pe):
            pe.wait_ge(s_w, 16 * NW)

            def shared(lo, hi):
                def step(g, par):
                    if not isinstance(g, int) or g < hi:
                        wait(pe, s_xg[par], nth(g, par), 16 * NG)
                        for j in range(FC):
                            wait(pe, f_ge, FC * g + j - 1, FC * NG)
                            nc.tensor.matmul(bank[j % 2][:], rw1[:, j * P:(j + 1) * P],
                                             xg[:, par],
                                             start=True, stop=True).then_inc(f_l1, 1)
                    if not isinstance(g, int) or g > lo:
                        wait(pe, f_ge, FC * g, FC * NG)
                        wait(pe, f_r, g - 1)
                        for i in range(GT):
                            for j in range(FC):
                                last = nc.tensor.matmul(rbank[:, i * P:(i + 1) * P],
                                                        hs[:, 1 - par, j, i * P:(i + 1) * P], rw2[:, j],
                                                        start=(j == 0), stop=(j == FC - 1))
                        last.then_inc(f_l2, 1)
                groups(pe, step, lo, hi, lo + 2, hi)
            shared(0, HALF)

            def turn(u, par):
                wait(pe, s_xs[par], nth(u, par, NU), 16 * NU)
                wait(pe, x_xt, u, NU)
                for k in range(2):
                    last = nc.tensor.transpose(xbank[:, k * P:(k + 1) * P], xsl[:, par, k], ident[:])
                last.then_inc(x_tr, 1)

            def layer2(v, k):
                wait(pe, x_ge, v + 1, SLOTS)
                wait(pe, x_y, v - 1, SLOTS)
                e = pe.value_load(eid[0:1, bass.ds(v, 1)], min_val=0, max_val=E - 1)
                y = bank[4 + k][:, 0:D]
                for j in range(FC):
                    nc.tensor.matmul(y, hT[:, k, j], w2[:, e, j * D:(j + 1) * D], start=(j == 0), stop=False)
                nc.tensor.matmul(y, one[0:1, :], b2[0:1, bass.ds(e * D, D)], start=False, stop=True).then_inc(x_l2, 1)

            def step(u, par):
                if isinstance(u, int) and u == 0:
                    turn(u, par)
                for k in range(2):
                    v = u * 2 + k
                    if valid(u, NU):
                        if k == 0:
                            wait(pe, x_xt, u + 1, NU)
                        wait(pe, x_w1, v + 1, SLOTS)
                        wait(pe, x_ge, v - 1, SLOTS)
                        for j in range(FC):
                            last = nc.tensor.matmul(pair[:, k, j * P:(j + 1) * P], w1b[:, k, j * P:(j + 1) * P],
                                                    xsT[:, par, k * P:(k + 1) * P], start=True, stop=True)
                        last.then_inc(x_l1, 1)
                    if k == 0 and valid(u + 1, NU):
                        turn(u + 1, 1 - par)
                    if valid(v - 1, SLOTS):
                        layer2(v - 1, 1 - k)
            groups(pe, step, 0, NU, 2, NU - 2)
            shared(HALF, NG)


_OUT = ((B, L, D), "float32")


def layouts(i):
    import numpy as np
    f = np.float32
    heads = np.arange(P) // DH
    rev = (L - np.arange(L)) % L
    mq = np.stack([((heads % 8) // 2 == hp) / np.sqrt(DH) for hp in range(4)], 1).astype(f)
    mk = np.stack([heads % 2 == h2 for h2 in range(2)], 1).astype(f)
    wqkv, bqkv = i["L0_ffn_Wqkv"], i["L0_ffn_bqkv"]
    msel = np.zeros((32, 8, 2, L), np.uint16)
    for n in range(8):
        for h2 in range(2):
            msel[2 * n + h2, n, h2] = BF16_ONE
            msel[16 + 2 * n + h2, n, h2] = BF16_ONE
    sel = np.zeros((16, DQ, 2, 16, 4), f)
    for r in range(4):
        for p in range(2):
            sel[np.arange(16), 2 * r + p, p, np.arange(16), r] = 1
    dmask = np.zeros((2, L, 4, 4, 2, DH), f)
    for hp in range(4):
        for h2 in range(2):
            dmask[h2, :, hp, hp, h2] = 1
    w1 = i["L0_ffn_W1"].transpose(1, 0, 2)
    b1 = i["L0_ffn_b1"].reshape(E, FC, P).transpose(2, 0, 1)
    return {
        "x": i["x"].reshape(B * L, D),
        "ctx": i["ctx_1024"].reshape(B * L, D),
        "wq8": i["L0_xattn_Wq"],
        "bq8": i["L0_xattn_bq"].reshape(1, DQ),
        "wout_rev": np.concatenate([i["L0_xattn_Wout"][rev], i["L0_xattn_Wout"][L + rev]], 0),
        "bout": i["L0_xattn_bout"].reshape(1, D),
        "cols": np.concatenate([np.stack([i["L0_ffn_ln1_g"], i["L0_ffn_ln1_b"], i["L0_ffn_ln2_g"],
                                          i["L0_ffn_ln2_b"], bqkv[0:D], bqkv[D:2 * D], bqkv[2 * D:]], 1),
                                i["L0_ffn_rb1"].reshape(FC, P).T, mq, mk], 1),
        "wqk": wqkv[:, 0:2 * D],
        "wv": wqkv[:, 2 * D:].reshape(D, 8, 2, DH).transpose(0, 2, 1, 3).reshape(D, 2, L),
        "wo": i["L0_ffn_Wo"],
        "bo": i["L0_ffn_bo"].reshape(1, D),
        "gc": np.concatenate([i["L0_ffn_gate_w"], i["L0_ffn_coef_w"]], 1),
        "coef_b": i["L0_ffn_coef_b"].reshape(1, 2),
        "w1": np.concatenate([w1, b1], 2),
        "w2": i["L0_ffn_W2"].reshape(E, FC, P, D).transpose(2, 0, 1, 3).reshape(P, E, FC * D),
        "b2": i["L0_ffn_b2"].reshape(1, E * D),
        "rw1": i["L0_ffn_rW1"],
        "rw2": i["L0_ffn_rW2"].reshape(FC, P, D).transpose(1, 0, 2),
        "rb2": i["L0_ffn_rb2"].reshape(1, D),
        "ident": np.eye(P, dtype=f),
        "identb": np.diag(np.full(P, BF16_ONE, np.uint16)),
        "one": np.ones((P, P), f),
        "oneb": np.full((P, P), BF16_ONE, np.uint16),
        "triu": np.triu(np.full((P, P), BF16_ONE, np.uint16), 1),
        "sel": sel.reshape(P, 2, L),
        "msel": msel.reshape(32, 8, P),
        "dmask": dmask.reshape(P, 4, L),
        "prio": np.arange(E, 0, -1, dtype=f).reshape(1, E),
        "jrow": np.arange(SLOTS, dtype=f).reshape(1, SLOTS),
    }


def kernel(**inputs):
    import numpy as np
    import concourse.bacc as bacc
    from concourse.bass_utils import run_bass_kernel_spmd

    nc = bacc.Bacc("TRN2", target_bir_lowering=False, num_devices=1)
    arrays = {n: np.ascontiguousarray(v) for n, v in layouts({n: np.asarray(v) for n, v in inputs.items()}).items()}
    aps = {n: nc.dram_tensor(f"in_{n}", v.shape, mybir.dt.from_np(v.dtype), kind="ExternalInput").ap()
           for n, v in arrays.items()}
    out = nc.dram_tensor("out_0", (B * L, D), F32, kind="ExternalOutput").ap()
    build(nc, aps, out)
    r = run_bass_kernel_spmd(nc, [{f"in_{n}": v for n, v in arrays.items()}], core_ids=[0])
    return r.results[0]["out_0"].reshape(_OUT[0])
```

```python
from contextlib import ExitStack

import concourse.bass as bass
from concourse import mybir

F32 = mybir.dt.float32
BF16 = mybir.dt.bfloat16
I32 = mybir.dt.int32
U16 = mybir.dt.uint16
ALU = mybir.AluOpType
ACT = mybir.ActivationFunctionType
AX = mybir.AxisListType

P = 128
B, L, D = 128, 64, 128
NT = B * L // P
GT = 4
NG = NT // GT
GB = GT * P // L
IB = 4
DQ = 8
H, DH = 16, 8
E = 8
FF = 512
FC = FF // P
SLOTS = NT + E
K_TOP = 11
EPS = 1e-5
NEG = -3.0e38
BF16_ONE = 0x3F80
W1W = FF + FC + D
XW = D + 2
VW = L + H // 2
YB = 4

C_G1, C_B1, C_G2, C_B2, C_BQ, C_BK, C_BV, C_RB1 = 0, 1, 2, 3, 4, 5, 6, 7
C_MQ = C_RB1 + FC
C_MK = C_MQ + 4
NCOL = C_MK + 2


def groups(eng, step, first, last, lo, hi, n=2):
    assert lo % n == 0 and hi % n == 0
    for g in range(first, lo):
        step(g, g % n)
    with eng.Fori(0, (hi - lo) // n) as i:
        for k in range(n):
            step(i * n + (lo + k), k)
    for g in range(hi, last + 1):
        step(g, g % n)


def valid(g, n=NG):
    return not isinstance(g, int) or 0 <= g < n


def wait(eng, sem, count, most=NG):
    if isinstance(count, int):
        count = min(count, most)
        if count <= 0:
            return
    eng.wait_ge(sem, count)


def nth(g, par, most=NG, n=2):
    if isinstance(g, int):
        g = min(g, most - n + par)
    return 16 // n * (g - par + n)


def settle(eng, cell):
    eng.memset(cell, 0.0)


def build(nc, a, out):
    ctx = ExitStack()
    with ctx:
        def sb(name, shape, dt=F32, scope=ctx):
            return scope.enter_context(nc.sbuf_tensor(name, shape, dt))

        def sem(name):
            return ctx.enter_context(nc.semaphore(name))

        bank = [ctx.enter_context(nc.psum_tensor(f"bank{i}", [P, 512], F32)) for i in range(6)]
        pair = ctx.enter_context(nc.psum_tensor("pair", [P, 2, 512], F32))

        corr_dram = nc.dram_tensor("corr_dram", [L, 2 * L], F32, kind="Internal").ap()
        shift_dram = nc.dram_tensor("shift_dram", [1, 2 * L], F32, kind="Internal").ap()
        xs_dram = nc.dram_tensor("xs_dram", [SLOTS * P, XW], F32, kind="Internal").ap()
        xt_dram = nc.dram_tensor("xt_dram", [NG, P, GT * P], F32, kind="Internal").ap()

        cols = sb("cols", [P, NCOL])
        ident = sb("ident", [P, P])
        ones = sb("ones", [P, P])
        x3 = sb("x3", [P, NT, D])
        xh2 = sb("xh2", [P, NT, XW])
        logits = sb("logits", [P, NT, E + 2])
        coefb = sb("coefb", [P, 2])
        s_const = sem("s_const")
        x2_dram = nc.dram_tensor("x2_dram", [B * L, D], F32, kind="Internal").ap()
        K = dict(x2_dram=x2_dram, nc=nc, a=a, out=out, sb=sb, sem=sem, bank=bank, pair=pair, cols=cols, ident=ident,
                 ones=ones, x3=x3, xh2=xh2, xt_dram=xt_dram, logits=logits, coefb=coefb, s_const=s_const,
                 corr_dram=corr_dram, shift_dram=shift_dram, xs_dram=xs_dram)
        with ExitStack() as mid:
            vts = sb("vts", [P, NT, 2, 4], scope=mid)
            m2 = sb("m2", [P, D], scope=mid)
            cvec = sb("cvec", [P, D], scope=mid)
            wo = sb("wo", [P, D], scope=mid)
            vm = sb("vm", [P, 2, GB, 2, 4, VW], scope=mid)
            with ExitStack() as scope:
                correlate(K, scope, vts, m2, cvec, wo, vm)
            with ExitStack() as scope:
                attention(K, scope, vts, m2, cvec, wo, vm)
        with ExitStack() as scope:
            experts(K, scope)


def correlate(K, scope, vts, m2, cvec, wo, vm):
    nc, a, bank, cols, ident, ones = K["nc"], K["a"], K["bank"], K["cols"], K["ident"], K["ones"]
    s_const, sem = K["s_const"], K["sem"]
    corr_dram, shift_dram = K["corr_dram"], K["shift_dram"]

    def sb(name, shape, dt=F32):
        return K["sb"](name, shape, dt, scope)

    wq8 = sb("wq8", [P, DQ])
    bq8 = sb("bq8", [P, DQ])
    sel = sb("sel", [P, 2, L])
    wout = sb("wout", [P, D])
    bo_bc = sb("bo_bc", [P, D])
    xin = sb("xin1", [P, IB, GT, D])
    cin = sb("cin1", [P, IB, GT, D])
    xn = sb("xn1", [P, 2, GT, D])
    cT = sb("cT1", [P, 2, GT * P])
    xT = sb("xT1", [P, 2, GT * P])
    st6 = sb("st6", [P, 2, GT, 6])
    mv = sb("mv1", [P, 2, GT, 2])
    ve = sb("ve1", [P, 2, GT])
    rs = sb("rs1", [P, 2, GT])
    nhalf = sb("nhalf1", [P, GT])
    eps = sb("eps1", [P, GT])
    idle = sb("idle1", [P, 1])
    kq = sb("kq", [P, 2, NT, DQ])

    s_x, s_c = ([sem(f"{n}{i}") for i in range(IB)] for n in ("c_x", "c_c"))
    d_nh, d_bs, d_st, d_norm, d_kq = (sem(n) for n in ("c_nh", "c_bs", "c_st", "c_norm", "c_kq"))
    p_ve, p_rs = sem("c_ve"), sem("c_rs")
    t_c, t_x, t_mm = sem("c_tc"), sem("c_tx"), sem("c_mm")
    e_c, e_x = sem("c_ec"), sem("c_ex")
    NCONST = 7
    s_constp = sem("s_constp")
    x_src = a["x"].rearrange("(t p) d -> p t d", p=P)
    c_src = a["ctx"].rearrange("(t p) d -> p t d", p=P)

    with nc.Block() as block:
        @block.sync
        def _(sp):
            sp.dma_start(ident[:], a["ident"]).then_inc(s_const, 16)
            sp.dma_start(wq8[:], a["wq8"]).then_inc(s_const, 16)

            def load(g, buf):
                wait(sp, t_c, g - IB + 1)
                sp.dma_start(cin[:, buf], c_src[:, bass.ds(g * GT, GT), :]).then_inc(s_c[buf], 16)
                wait(sp, d_norm, g - IB + 1)
                sp.dma_start(xin[:, buf], x_src[:, bass.ds(g * GT, GT), :]).then_inc(s_x[buf], 16)
            groups(sp, load, 0, NG - 1, IB, NG, IB)

        @block.gpsimd
        def _(pool):
            pool.dma_start(bq8[:], a["bq8"].partition_broadcast(P)).then_inc(s_constp, 16)
            pool.dma_start(cols[:], a["cols"]).then_inc(s_constp, 16)
            pool.dma_start(sel[:], a["sel"]).then_inc(s_constp, 16)
            pool.dma_start(wout[:], a["wout_rev"]).then_inc(s_constp, 16)
            pool.dma_start(bo_bc[:], a["bo"].partition_broadcast(P)).then_inc(s_constp, 16)
            pool.dma_start(wo[:], a["wo"]).then_inc(s_constp, 16)
            pool.dma_start(K["coefb"][:], a["coef_b"].partition_broadcast(P)).then_inc(s_constp, 16)
            pool.memset(vm[:], 0.0)
            pool.wait_ge(d_nh, 1)

            def rstd(g, buf):
                if valid(g + 1):
                    o = (buf + 1) % 2
                    wait(pool, d_st, g + 2)
                    wait(pool, d_norm, g)
                    pool.tensor_tensor(ve[:, o], mv[:, o, :, 1], eps[:], ALU.add).then_inc(p_ve, 1)
                    wait(pool, p_ve, g + 2)
                    pool.tensor_tensor(rs[:, o], ve[:, o], nhalf[:], ALU.pow).then_inc(p_rs, 1)
            groups(pool, rstd, -1, NG, IB, NG - IB, IB)

        @block.vector
        def _(dve):
            nc.vector.memset(eps[:], EPS)
            nc.vector.memset(nhalf[:], -0.5).then_inc(d_nh, 1)
            nc.vector.memset(ones[:], 1.0)

            def step(g, buf):
                par = buf % 2
                o = 1 - par
                nxt = (buf + 1) % IB
                if valid(g + 1):
                    wait(dve, s_x[nxt], nth(g + 1, nxt, NG, IB), 16 * NG)
                    wait(dve, d_st, g)
                    for t in range(GT):
                        last = nc.vector.bn_stats(st6[:, o, t], xin[:, nxt, t])
                    last.then_inc(d_bs, 1)
                    wait(dve, d_bs, g + 2)
                    wait(dve, d_norm, g)
                    settle(nc.vector, idle[:])
                    for t in range(GT):
                        last = nc.vector.bn_aggr(mv[:, o, t], st6[:, o, t])
                    last.then_inc(d_st, 1)
                if valid(g):
                    wait(dve, p_rs, g + 1)
                    wait(dve, t_x, g - 1)
                    for t in range(GT):
                        last = nc.vector.tensor_scalar(xn[:, par, t], xin[:, buf, t], mv[:, par, t, 0:1],
                                                       rs[:, par, t:t + 1], ALU.subtract, ALU.mult)
                    last.then_inc(d_norm, 1)
                if valid(g - 2):
                    if isinstance(g, int) and g == 2:
                        dve.wait_ge(s_constp, 16 * NCONST)
                    wait(dve, t_mm, g - 1)
                    nc.vector.tensor_tensor(
                        kq[:, :, bass.ds((g - 2) * GT, GT), :],
                        bank[4 + par][:, 0:2 * GT * DQ].rearrange("p (w t j) -> p w t j", w=2, t=GT),
                        bq8[:].unsqueeze(1).unsqueeze(1).broadcast_to([P, 2, GT, DQ]),
                        ALU.add).then_inc(d_kq, 1)
            groups(dve, step, -1, NG + 1, IB, NG - IB, IB)

        @block.scalar
        def _(act):
            def step(g, par):
                wait(act, t_mm, g - 1)
                wait(act, t_c, g + 1)
                nc.scalar.copy(cT[:, par], bank[par][:]).then_inc(e_c, 1)
                wait(act, t_x, g + 1)
                nc.scalar.copy(xT[:, par], bank[2 + par][:]).then_inc(e_x, 1)
            groups(act, step, 0, NG - 1, 2, NG)

        @block.tensor
        def _(pe):
            pe.wait_ge(s_const, 32)
            pe.wait_ge(s_constp, 16 * NCONST)

            def step(g, buf):
                par = buf % 2
                if valid(g):
                    wait(pe, s_c[buf], nth(g, buf, NG, IB), 16 * NG)
                    wait(pe, e_c, g - 1)
                    for t in range(GT):
                        last = nc.tensor.transpose(bank[par][:, t * P:(t + 1) * P], cin[:, buf, t], ident[:])
                    last.then_inc(t_c, 1)
                if valid(g - 1):
                    o = 1 - par
                    wait(pe, e_c, g)
                    wait(pe, e_x, g)
                    wait(pe, d_kq, g - 2)
                    for w, src in enumerate((cT, xT)):
                        for t in range(GT):
                            c = (w * GT + t) * DQ
                            last = nc.tensor.matmul(bank[4 + o][:, c:c + DQ], src[:, o, t * P:(t + 1) * P],
                                                    wq8[:], start=True, stop=True)
                    last.then_inc(t_mm, 1)
                if valid(g):
                    wait(pe, d_norm, g + 1)
                    wait(pe, e_x, g - 1)
                    for t in range(GT):
                        last = nc.tensor.transpose(bank[2 + par][:, t * P:(t + 1) * P], xn[:, par, t], ident[:])
                    last.then_inc(t_x, 1)
            groups(pe, step, 0, NG, IB, NG, IB)

    kT = sb("kT", [P, 4, P])
    qT = sb("qT", [P, 4, P])
    g2 = sb("g2", [L, 2, L])
    gs = sb("gs", [L, L])
    cor = sb("cor", [P, L])
    c2 = sb("c2", [P, L])
    c3 = sb("c3", [P, L])
    top = sb("top", [P, 16])
    nmax = sb("nmax", [P, 1])
    ew = sb("ew", [P, L])
    wsh = sb("wsh", [P, L])
    wsum = sb("wsum", [P, 2])
    wrow = sb("wrow", [P, 2, L])
    circ = sb("circ", [P, P])
    bvb = sb("bvb", [P, P])
    m_t, m_g, m_v, m_cor, m_m2, m_cv = (sem(n) for n in ("m_t", "m_g", "m_v", "m_cor", "m_m2", "m_cv"))
    m_e, m_g2, m_bv, m_link, m_ex, m_w, m_z = (sem(n) for n in ("m_e", "m_g2", "m_bv", "m_link", "m_ex", "m_w", "m_z"))
    m_gd, m_gl, m_wd, m_wl = (sem(n) for n in ("m_gd", "m_gl", "m_wd", "m_wl"))

    with nc.Block() as block:
        @block.sync
        def _(sp):
            sp.wait_ge(m_g2, 1)
            sp.dma_start(corr_dram, g2[:].rearrange("t a s -> t (a s)")).then_inc(m_gd, 16)
            sp.wait_ge(m_gd, 16)
            sp.dma_start(gs[:], bass.AP(corr_dram.tensor, 0, [[2 * L + 1, L], [1, L]])).then_inc(m_gl, 16)
            sp.wait_ge(m_w, 1)
            sp.dma_start(shift_dram, wrow[0:1].rearrange("p a s -> p (a s)")).then_inc(m_wd, 16)
            sp.wait_ge(m_wd, 16)
            sp.wait_ge(m_z, 1)
            for i in range(2):
                sp.dma_start(circ[i * L:(i + 1) * L, i * L:(i + 1) * L],
                             bass.AP(shift_dram.tensor, 0, [[1, L], [1, L]])).then_inc(m_wl, 16)
            sp.wait_ge(m_wl, 32)

        @block.tensor
        def _(pe):
            for w in range(2):
                for blk in range(4):
                    last = nc.tensor.transpose(bank[w][:, blk * P:(blk + 1) * P],
                                               kq[:, w, 16 * blk:16 * blk + 16, :].rearrange("p t j -> p (t j)"),
                                               ident[:])
                last.then_inc(m_t, 1)
            pe.wait_ge(m_e, 2)
            n = 0
            for blk in range(4):
                for b in range(2):
                    last = nc.tensor.matmul(bank[2][0:L, 0:L], kT[:, blk, b * L:(b + 1) * L],
                                            qT[:, blk, b * L:(b + 1) * L], start=(n == 0), stop=(n == 7))
                    n += 1
            last.then_inc(m_g, 1)
            for i in range(2):
                for blk in range(4):
                    for b in range(2):
                        c = (blk * 2 + b) * L
                        last = nc.tensor.matmul(bank[3][i * L:(i + 1) * L, c:c + L], kT[:, blk, b * L:(b + 1) * L],
                                                sel[:, i], start=True, stop=True)
            last.then_inc(m_v, 1)
            pe.wait_ge(m_bv, 1)
            nc.tensor.matmul(bank[5][:, 0:D], bvb[:], wo[:], start=True, stop=True).then_inc(m_cv, 1)
            pe.wait_ge(m_gl, 16)
            nc.tensor.matmul(bank[4][:, 0:L], ones[0:L, :], gs[:], start=True, stop=True).then_inc(m_cor, 1)
            pe.wait_ge(m_wl, 32)
            nc.tensor.matmul(bank[4][:, P:2 * P], circ[:], wout[:], start=True, stop=True).then_inc(m_m2, 1)

        @block.scalar
        def _(act):
            act.wait_ge(m_t, 2)
            nc.scalar.copy(qT[:].rearrange("p b l -> p (b l)"), bank[1][:]).then_inc(m_e, 1)
            act.wait_ge(m_link, 6)
            nc.scalar.activation(ew[:], cor[:], ACT.Exp, bias=nmax[:]).then_inc(m_ex, 1)

        @block.vector
        def _(dve):
            dve.wait_ge(m_t, 1)
            nc.vector.tensor_copy(kT[:].rearrange("p b l -> p (b l)"), bank[0][:]).then_inc(m_e, 1)
            nc.vector.memset(circ[:], 0.0).then_inc(m_z, 1)
            nc.vector.tensor_scalar(bvb[:], ones[:], cols[:, C_BV:C_BV + 1], None, ALU.mult).then_inc(m_bv, 1)
            dve.wait_ge(m_g, 1)
            nc.vector.tensor_copy(g2[:], bank[2][0:L, 0:L].unsqueeze(1).broadcast_to([L, 2, L])).then_inc(m_g2, 1)
            dve.wait_ge(m_v, 1)
            for blk in range(4):
                nc.vector.tensor_copy(
                    vts[:, 16 * blk:16 * blk + 16].rearrange("p t b r -> p b t r"),
                    bank[3][:, blk * P:(blk + 1) * P].rearrange("p (b t r) -> p b t r", b=2, t=16))
            dve.wait_ge(m_cv, 1)
            nc.vector.tensor_tensor(cvec[:], bank[5][:, 0:D], bo_bc[:], ALU.add)

            links = [0]

            def link(ins):
                links[0] += 1
                ins.then_inc(m_link, 1)
                dve.wait_ge(m_link, links[0])

            dve.wait_ge(m_cor, 1)
            link(nc.vector.tensor_scalar(cor[:], bank[4][:, 0:L], 1.0 / (B * DQ), None, ALU.mult))
            link(nc.vector.max(top[:, 0:8], cor[:]))
            link(nc.vector.match_replace(c2[:], top[:, 0:8], cor[:], NEG))
            link(nc.vector.max(top[:, 8:16], c2[:]))
            link(nc.vector.memset(top[:, K_TOP:16], NEG))
            link(nc.vector.tensor_scalar(nmax[:], top[:, 0:1], -1.0, None, ALU.mult))
            link(nc.vector.match_replace(c3[:], top[:, 8:16], c2[:], NEG))
            link(nc.vector.tensor_tensor(c2[:], c3[:], cor[:], ALU.is_lt))
            dve.wait_ge(m_ex, 1)
            link(nc.vector.tensor_tensor(wsh[:], ew[:], c2[:], ALU.mult))
            link(nc.vector.tensor_reduce(wsum[:, 0:1], wsh[:], AX.X, ALU.add))
            link(nc.vector.reciprocal(wsum[:, 1:2], wsum[:, 0:1]))
            nc.vector.tensor_scalar(wrow[:], wsh[:].unsqueeze(1).broadcast_to([P, 2, L]), wsum[:, 1:2], None,
                                    ALU.mult).then_inc(m_w, 1)
            dve.wait_ge(m_m2, 1)
            nc.vector.tensor_copy(m2[:], bank[4][:, P:2 * P])


def attention(K, scope, vts, m2, cvec, wo, vm):
    nc, a, bank, pair, cols, ident = K["nc"], K["a"], K["bank"], K["pair"], K["cols"], K["ident"]
    x3, xh2, xt_dram, logits, sem, s_const = K["x3"], K["xh2"], K["xt_dram"], K["logits"], K["sem"], K["s_const"]

    def sb(name, shape, dt=F32):
        return K["sb"](name, shape, dt, scope)

    wqk = sb("wqk", [P, 2 * D])
    wv = sb("wv", [P, 2, L])
    gc = sb("gc", [P, E + 2])
    bout = sb("bout", [P, D])
    identb = sb("identb", [P, P], BF16)
    msel = sb("msel", [32, 8, P], BF16)
    dmask = sb("dmask", [P, 4, H // 2])
    dspread = sb("dspread", [H // 2, L])
    xin = sb("xin", [P, 2, GT, D])
    x2 = sb("x2", [P, 2, GT, D])
    x1 = sb("x1", [P, 2, GT, D])
    xh = sb("xh", [P, 2, GT, D])
    vtx = sb("vtx", [P, 2, GT * P])
    xnT = sb("xnT", [P, 2, GT * P])
    qm = sb("qm", [P, 2, GB, 4, L])
    km = sb("km", [P, 2, GB, 2, L])
    qmb = sb("qmb", [P, 2, GB, 4, L], BF16)
    kmb = sb("kmb", [P, 2, GB, 2, L], BF16)
    pt = sb("pt", [P, 2, 2, 2, 4 * L])
    rd = sb("rd", [P, 2, P])
    ctxT = sb("ctxT", [P, 2, GT * P])
    mx = sb("mx", [P, 2, 16])
    mhl = sb("mhl", [P, 2, 32], BF16)
    mT = sb("mT", [32, 2, P], BF16)
    st6 = sb("st6a", [P, GT, 6])
    mv = sb("mva", [P, 2, GT, 2])
    st6b = sb("st6b", [P, GT, 6])
    mvb = sb("mvb", [P, GT, 2])
    rsb = sb("rsb", [P, GT])
    veb = sb("veb", [P, GT])
    pw = sb("pw", [P, 5, GT])
    rs = sb("rs", [P, 2, GT])
    r2 = sb("r2", [P, 2, GT])
    nhalf = sb("nhalf", [P, GT])
    eps = sb("eps", [P, GT])
    idle = sb("idle", [P, 1])
    bqm = sb("bqm", [P, 6])
    x2nT = sb("x2nT", [P, 2, GT * P])
    xh2s = sb("xh2s", [P, 2, GT, D])
    dn = sb("dn", [H // 2, 2, 2 * P])
    blank = sb("blank", [P, GT, XW])

    g0, g1 = bank[0], bank[1]
    sbank = [bank[2], bank[3]]
    cd = bank[4]
    mps = bank[5][:, 0:P // 2].bitcast(BF16)
    lps = g1[:, 0:GT * (E + 2)]

    s_c2, s_z = sem("s_c2"), sem("s_z")
    s_xi, s_xt, s_x2 = ([sem(f"{n}{i}") for i in range(2)] for n in ("s_xi", "s_xt", "s_x2"))
    x2_dst = K["x2_dram"].rearrange("(t p) d -> p t d", p=P)
    (t_a, t_b, t_q, t_k, t_v, t_o, t_b2, t_l) = (sem("t_" + n) for n in "a b q k v o b2 l".split())
    t_s, t_m, t_st, t_pv, t_dn = (sem(n) for n in ("t_s", "t_m", "t_st", "t_pv", "t_dn"))
    e_vtx, e_qm, e_km, e_xh, e_x2n, e_dn, e_exp, e_mt = (
        sem("e_" + n) for n in "vtx qm km xh x2n dn exp mt".split())
    (d_c, d_max, d_mhi, d_mh, d_rd, d_ctx, d_xnT, d_qb, d_vm, d_x3, d_bsb, d_stb, d_xh2, d_x2, d_bs, d_st,
     d_x1, d_lg) = (sem("d_" + n) for n in
                    "c max mhi mh rd ctx xnT qb vm x3 bsb stb xh2 x2 bs st x1 lg".split())
    p_xb, p_c, p_b, p_rsb, p_r, p_x3, p_xh2 = (sem("p_" + n) for n in "xb c b rsb r x3 xh2".split())
    NC2 = 9
    NZ = SLOTS // GT
    z_dst = K["xs_dram"].rearrange("(t p) d -> p t d", p=P)
    LO, HI = 4, NG - 2
    FIRST, LAST = -2, NG + 2
    x_src = a["x"].rearrange("(t p) d -> p t d", p=P)

    with nc.Block() as block:
        @block.sync
        def _(sp):
            for dst, src in ((wqk[:], a["wqk"]), (wv[:], a["wv"]), (gc[:], a["gc"]), (identb[:].bitcast(U16), a["identb"]),
                             (msel[:].bitcast(U16), a["msel"]), (dmask[:], a["dmask"]), (dspread[:], a["dspread"]),
                             (blank[:], a["blank"])):
                sp.dma_start(dst, src).then_inc(s_c2, 16)
            sp.dma_start(bout[:], a["bout"].partition_broadcast(P)).then_inc(s_c2, 16)

            def step(g, par):
                if valid(g + 3):
                    wait(sp, d_x2, g + 2)
                    sp.dma_start(xin[:, 1 - par], x_src[:, bass.ds((g + 3) * GT, GT), :]).then_inc(s_xi[1 - par], 16)
                if valid(g + 2):
                    wait(sp, d_x2, g + 3)
                    sp.dma_start(x2_dst[:, bass.ds((g + 2) * GT, GT), :], x2[:, par]).then_inc(s_x2[par], 16)
                if valid(g - 2):
                    wait(sp, e_x2n, g - 1)
                    sp.dma_start(xt_dram[bass.ds(g - 2, 1)].rearrange("g p c -> p (g c)"),
                                 x2nT[:, par]).then_inc(s_xt[par], 16)
                if valid(g + 2, NZ):
                    sp.dma_start(z_dst[:, bass.ds((g + 2) * GT, GT), :], blank[:]).then_inc(s_z, 16)
            sp.wait_ge(s_c2, 16 * NC2)
            sp.dma_start(K["out"][B * L:, :].rearrange("(t p) d -> p t d", p=P), blank[:, :, 0:D]).then_inc(s_z, 16)
            groups(sp, step, -3, LAST, LO, NG - 4)
            for i in range(2):
                sp.wait_ge(s_xt[i], 8 * NG)
                sp.wait_ge(s_x2[i], 8 * NG)
            sp.wait_ge(s_z, 16 * (NZ + 1))

        @block.gpsimd
        def _(pool):
            pool.wait_ge(s_c2, 16 * NC2)
            pool.wait_ge(d_c, 1)
            bout_bc = bout[:].unsqueeze(1).broadcast_to([P, GT, D])
            cvec_bc = cvec[:].unsqueeze(1).broadcast_to([P, GT, D])

            def step(g, par):
                o = 1 - par
                if valid(g + 2):
                    wait(pool, s_xi[par], nth(g + 2, par), 16 * NG)
                    pool.tensor_tensor(xin[:, par], xin[:, par], bout_bc, ALU.add).then_inc(p_xb, 1)
                if valid(g - 1):
                    wait(pool, d_stb, g)
                    wait(pool, d_xh2, g - 1)
                    pool.tensor_tensor(veb[:], mvb[:, :, 1], eps[:], ALU.add).then_inc(p_b, 1)
                    wait(pool, p_b, g)
                    pool.tensor_tensor(rsb[:], veb[:], nhalf[:], ALU.pow).then_inc(p_rsb, 1)
                if valid(g + 2):
                    wait(pool, d_st, g + 3)
                    wait(pool, d_x1, g + 1)
                    wait(pool, e_xh, g + 1)
                    n = (g + 2) * 5
                    pool.tensor_tensor(pw[:, 0], mv[:, par, :, 1], eps[:], ALU.add).then_inc(p_c, 1)
                    wait(pool, p_c, n + 1, 5 * NG)
                    pool.tensor_tensor(rs[:, par], pw[:, 0], nhalf[:], ALU.pow).then_inc(p_c, 1)
                    wait(pool, p_c, n + 2, 5 * NG)
                    pool.tensor_tensor(pw[:, 1], rs[:, par], rs[:, par], ALU.mult).then_inc(p_c, 1)
                    wait(pool, p_c, n + 3, 5 * NG)
                    pool.tensor_tensor(pw[:, 2], pw[:, 1], mv[:, par, :, 1], ALU.mult).then_inc(p_c, 1)
                    wait(pool, p_c, n + 4, 5 * NG)
                    pool.tensor_tensor(pw[:, 3], pw[:, 2], eps[:], ALU.add).then_inc(p_c, 1)
                    wait(pool, p_c, n + 5, 5 * NG)
                    pool.tensor_tensor(r2[:, par], pw[:, 3], nhalf[:], ALU.pow).then_inc(p_r, 1)
                    wait(pool, d_x1, g + 3)
                    pool.tensor_tensor(x3[:, bass.ds((g + 2) * GT, GT), :], x1[:, par], cvec_bc,
                                       ALU.add).then_inc(p_x3, 1)
                if valid(g - 1):
                    wait(pool, d_xh2, g)
                    pool.tensor_copy(xh2[:, bass.ds((g - 1) * GT, GT), 0:D], xh2s[:, o]).then_inc(p_xh2, 1)
            groups(pool, step, FIRST, LAST, LO, HI)

        @block.scalar
        def _(act):
            act.wait_ge(d_c, 1)

            def xpose_max(T, t):
                if valid(T + 2, NT):
                    q = t % 2
                    wait(act, t_m, T + 3, NT)
                    wait(act, t_st, T + 1, NT)
                    nc.scalar.copy(mT[:, q], mps[0:32, :]).then_inc(e_mt, 1)

            def step(g, par):
                o = 1 - par
                for t in range(GT):
                    T = g * GT + t
                    if valid(T + 1, NT):
                        q = (t + 1) % 2
                        wait(act, t_st, T + 2, NT)
                        wait(act, t_pv, T, NT)
                        nc.scalar.activation(pt[:, q].rearrange("p r b c -> p (r b c)"),
                                             pair[:].rearrange("p r c -> p (r c)"), ACT.Exp).then_inc(e_exp, 1)
                    if t == 0 and valid(g + 2):
                        wait(act, t_a, g + 1)
                        nc.scalar.copy(
                            vtx[:, par].rearrange("p (t l r) -> p t l r", l=16, r=4),
                            vts[:, bass.ds((g + 2) * GT, GT)].rearrange("p t b r -> p (t b) r").unsqueeze(2)
                            .broadcast_to([P, GB, 16, 4])).then_inc(e_vtx, 1)
                    if t == 1 and valid(g + 1):
                        wait(act, t_k, g + 2)
                        wait(act, t_st, g * GT, NT)
                        wait(act, d_qb, g)
                        for h2 in range(2):
                            last = nc.scalar.activation(
                                km[:, o, :, h2], g1[:].rearrange("p (b k) -> p b k", b=GB), ACT.Identity,
                                bias=bqm[:, 4 + h2:5 + h2], scale=cols[:, C_MK + h2:C_MK + h2 + 1])
                        last.then_inc(e_km, 1)
                    if t == 3 and valid(g - 2):
                        wait(act, t_b2, g - 1)
                        wait(act, t_l, g - 3)
                        wait(act, s_xt[par], nth(g - 4, par), 16 * NG)
                        nc.scalar.activation(x2nT[:, par], g1[:], ACT.Identity,
                                             bias=cols[:, C_B2:C_B2 + 1],
                                             scale=cols[:, C_G2:C_G2 + 1]).then_inc(e_x2n, 1)
                    if valid(T, NT):
                        wait(act, t_pv, T + 1, NT)
                        wait(act, t_dn, T - 1, NT)
                        nc.scalar.copy(dn[:, t % 2], cd[L:VW, 0:2 * P]).then_inc(e_dn, 1)
                    xpose_max(T, t)
                    if t == 0 and valid(g + 1):
                        wait(act, t_q, g + 2)
                        wait(act, t_st, g * GT, NT)
                        wait(act, d_qb, g)
                        for hp in range(4):
                            last = nc.scalar.activation(
                                qm[:, o, :, hp], g0[:].rearrange("p (b q) -> p b q", b=GB), ACT.Identity,
                                bias=bqm[:, hp:hp + 1], scale=cols[:, C_MQ + hp:C_MQ + hp + 1])
                        last.then_inc(e_qm, 1)
                    if t == 3 and valid(g + 2):
                        wait(act, p_r, g + 3)
                        wait(act, d_x1, g + 3)
                        wait(act, t_b, g + 1)
                        for i in range(GT):
                            last = nc.scalar.activation(xh[:, par, i], x1[:, par, i], ACT.Copy,
                                                        scale=r2[:, par, i:i + 1])
                        last.then_inc(e_xh, 1)
            groups(act, step, FIRST, LAST, LO, HI)

        @block.vector
        def _(dve):
            nc.vector.memset(nhalf[:], -0.5)
            nc.vector.memset(eps[:], EPS)
            dve.wait_ge(s_c2, 16 * NC2)
            for i in range(2):
                nc.vector.tensor_copy(
                    vm[:, i, :, :, :, L:].rearrange("p b r h w -> p (b r) h w"),
                    dmask[:].unsqueeze(1).broadcast_to([P, 2 * GB, 4, H // 2]))
            for hp in range(4):
                nc.vector.tensor_tensor(bqm[:, hp:hp + 1], cols[:, C_BQ:C_BQ + 1],
                                        cols[:, C_MQ + hp:C_MQ + hp + 1], ALU.mult)
            for h2 in range(2):
                last = nc.vector.tensor_tensor(bqm[:, 4 + h2:5 + h2], cols[:, C_BK:C_BK + 1],
                                               cols[:, C_MK + h2:C_MK + h2 + 1], ALU.mult)
            last.then_inc(d_c, 1)
            dve.wait_ge(d_c, 1)

            def maxima(T, t):
                if valid(T + 2, NT):
                    q = t % 2
                    wait(dve, t_s, T + 3, NT)
                    for r in range(2):
                        last = nc.vector.tensor_reduce(mx[:, q, 8 * r:8 * r + 8],
                                                       sbank[r][:].rearrange("p (n k) -> p n k", k=L), AX.X, ALU.max)
                    last.then_inc(d_max, 1)
                    wait(dve, d_max, T + 3, NT)
                    wait(dve, t_m, T + 1, NT)
                    nc.vector.tensor_scalar(mhl[:, q, 0:16], mx[:, q], -1.0, None, ALU.mult).then_inc(d_mhi, 1)
                    wait(dve, d_mhi, T + 3, NT)
                    nc.vector.scalar_tensor_tensor(mhl[:, q, 16:32], mx[:, q], -1.0, mhl[:, q, 0:16],
                                                   ALU.mult, ALU.subtract).then_inc(d_mh, 1)

            def normalise(g, T, t, par):
                if valid(T, NT):
                    q = t % 2
                    wait(dve, t_dn, T + 1, NT)
                    nc.vector.reciprocal(rd[:, q], cd[:, 2 * P:3 * P]).then_inc(d_rd, 1)
                    wait(dve, d_rd, T + 1, NT)
                    if t == 0:
                        wait(dve, t_o, g - 1)
                    for r in range(2):
                        rows = slice(r * L, (r + 1) * L)
                        last = nc.vector.tensor_tensor(ctxT[rows, par, t * P:(t + 1) * P],
                                                       cd[0:L, r * P:(r + 1) * P], rd[rows, q], ALU.mult)
                    last.then_inc(d_ctx, 1)

            def step(g, par):
                o = 1 - par
                for t in range(GT):
                    T = g * GT + t
                    maxima(T, t)
                    if t == 0:
                        if valid(g + 1):
                            wait(dve, t_b, g + 2)
                            wait(dve, t_v, g)
                            nc.vector.tensor_scalar(xnT[:, o], g1[:], cols[:, C_G1:C_G1 + 1],
                                                    cols[:, C_B1:C_B1 + 1], ALU.mult, ALU.add).then_inc(d_xnT, 1)
                    if t == 1 and valid(g + 1):
                        wait(dve, e_qm, g + 2)
                        wait(dve, t_s, g * GT, NT)
                        nc.vector.tensor_copy(qmb[:, o].rearrange("p b h q -> p (b h q)"),
                                              qm[:, o].rearrange("p b h q -> p (b h q)"))
                        wait(dve, e_km, g + 2)
                        nc.vector.tensor_copy(kmb[:, o].rearrange("p b h k -> p (b h k)"),
                                              km[:, o].rearrange("p b h k -> p (b h k)")).then_inc(d_qb, 1)
                    if t == 2 and valid(g - 1):
                        wait(dve, t_o, g)
                        wait(dve, p_x3, g)
                        xg = x3[:, bass.ds((g - 1) * GT, GT), :]
                        nc.vector.tensor_tensor(xg, xg, g1[:].rearrange("p (t d) -> p t d", t=GT),
                                                ALU.add).then_inc(d_x3, 1)
                        wait(dve, d_x3, g)
                        settle(nc.vector, idle[:])
                        for i in range(GT):
                            last = nc.vector.bn_stats(st6b[:, i], x3[:, (g - 1) * GT + i, :])
                        last.then_inc(d_bsb, 1)
                        wait(dve, d_bsb, g)
                        settle(nc.vector, idle[:])
                        for i in range(GT):
                            last = nc.vector.bn_aggr(mvb[:, i], st6b[:, i])
                        last.then_inc(d_stb, 1)
                    if t == 3 and valid(g + 2):
                        wait(dve, p_c, (g + 2) * 5 + 2, 5 * NG)
                        wait(dve, e_xh, g + 1)
                        wait(dve, p_x3, g + 1)
                        for i in range(GT):
                            last = nc.vector.tensor_scalar(x1[:, par, i], x2[:, par, i], mv[:, par, i, 0:1],
                                                           rs[:, par, i:i + 1], ALU.subtract, ALU.mult)
                        last.then_inc(d_x1, 1)
                    normalise(g, T, t, par)
                    if t == 0 and valid(g - 3):
                        wait(dve, t_l, g - 2)
                        nc.vector.tensor_copy(logits[:, bass.ds((g - 3) * GT, GT), :],
                                              lps.rearrange("p (t e) -> p t e", t=GT)).then_inc(d_lg, 1)
                    if t == 1 and valid(g + 1):
                        wait(dve, t_v, g + 2)
                        wait(dve, t_pv, g * GT, NT)
                        for h2 in range(2):
                            rows = slice(h2 * L, (h2 + 1) * L)
                            dst = vm[rows, o].rearrange("p b r h w -> p (b r) (h w)").rearrange(
                                "p n (s d) -> p n s d", d=DH)
                            first, apart = h2, (VW + 2 * DH) // DH
                            last = nc.vector.tensor_copy(
                                dst[:, :, first:first + 3 * apart + 1:apart],
                                g0[rows].rearrange("p (n h d) -> p n h d", h=4, d=DH))
                        last.then_inc(d_vm, 1)
                    if t == 2 and valid(g + 2):
                        wait(dve, t_a, g + 3)
                        wait(dve, p_xb, g + 3)
                        wait(dve, d_x1, g + 1)
                        wait(dve, s_x2[par], nth(g, par), 16 * NG)
                        nc.vector.tensor_tensor(x2[:, par], g0[:].rearrange("p (t d) -> p t d", t=GT),
                                                xin[:, par], ALU.add).then_inc(d_x2, 1)
                        wait(dve, d_x2, g + 3)
                        for i in range(GT):
                            last = nc.vector.bn_stats(st6[:, i], x2[:, par, i])
                        last.then_inc(d_bs, 1)
                        wait(dve, d_bs, g + 3)
                        wait(dve, p_r, g + 1)
                        settle(nc.vector, idle[:])
                        for i in range(GT):
                            last = nc.vector.bn_aggr(mv[:, par, i], st6[:, i])
                        last.then_inc(d_st, 1)
                    if t == 3 and valid(g - 1):
                        wait(dve, p_rsb, g)
                        wait(dve, t_b2, g - 2)
                        wait(dve, p_xh2, g - 2)
                        for i in range(GT):
                            last = nc.vector.tensor_scalar(xh2s[:, o, i], x3[:, (g - 1) * GT + i, :],
                                                           mvb[:, i, 0:1], rsb[:, i:i + 1], ALU.subtract, ALU.mult)
                        last.then_inc(d_xh2, 1)
            groups(dve, step, FIRST, LAST, LO, HI)

        @block.tensor
        def _(pe):
            pe.wait_ge(s_c2, 16 * NC2)

            def scores_q(T, t, qpar):
                if valid(T + 2, NT):
                    wait(pe, d_max, T + 2, NT)
                    lb = (t + 2) % GT * 2
                    for b in range(2):
                        for hh in range(2):
                            for r in range(2):
                                rows = slice(r * L, (r + 1) * L)
                                c = (b * 2 + hh) * P
                                last = nc.tensor.matmul(
                                    sbank[r][:, c:c + P],
                                    qmb[rows, qpar, lb + b, 2 * hh:2 * hh + 2].rearrange("p h q -> p (h q)"),
                                    kmb[rows, qpar, lb + b].rearrange("p h k -> p (h k)"),
                                    start=True, stop=True)
                    last.then_inc(t_s, 1)

            def scores_k(T, t, kpar):
                if valid(T + 1, NT):
                    q = (t + 1) % 2
                    wait(pe, e_exp, T + 1, NT)
                    lb = (t + 1) % GT * 2
                    for b in range(2):
                        for r in range(2):
                            rows = slice(r * L, (r + 1) * L)
                            nc.tensor.matmul(
                                pair[:, r, b * 4 * L:(b + 1) * 4 * L],
                                km[rows, kpar, lb + b].rearrange("p h k -> p (h k)"),
                                qm[rows, kpar, lb + b].rearrange("p h q -> p (h q)"),
                                start=(b == 0), stop=False, skip_group_check=True)
                    wait(pe, e_mt, T + 2, NT)
                    for r in range(2):
                        for b in range(2):
                            for hh in range(2):
                                n = (r * 2 + b) * 2 + hh
                                c = (b * 2 + hh) * P
                                last = nc.tensor.matmul(pair[:, r, c:c + P], msel[:, n], mT[:, q],
                                                        start=False, stop=(b == 1 and hh == 1),
                                                        skip_group_check=True)
                    last.then_inc(t_st, 1)

            def weighted(g, T, t, par):
                if valid(T, NT):
                    q = t % 2
                    wait(pe, e_exp, T + 1, NT)
                    if t == 0:
                        wait(pe, d_vm, g + 1)
                    wait(pe, d_ctx, T, NT)
                    for r in range(2):
                        for b in range(2):
                            for hp in range(4):
                                last = nc.tensor.matmul(
                                    cd[0:VW, (r * 2 + b) * L:(r * 2 + b + 1) * L], vm[:, par, t * 2 + b, r, hp],
                                    pt[:, q, r, b, hp * L:(hp + 1) * L], start=(hp == 0), stop=(hp == 3))
                    last.then_inc(t_pv, 1)

            def spread_den(T, t):
                if valid(T, NT):
                    wait(pe, e_dn, T + 1, NT)
                    for r in range(2):
                        last = nc.tensor.matmul(cd[r * L:(r + 1) * L, 2 * P:3 * P], dspread[:],
                                                dn[:, t % 2, r * P:(r + 1) * P], start=True, stop=True)
                    last.then_inc(t_dn, 1)

            def xpose_max(T, t):
                if valid(T + 2, NT):
                    q = t % 2
                    wait(pe, d_mh, T + 3, NT)
                    wait(pe, e_mt, T + 2, NT)
                    nc.tensor.transpose(mps[0:32, :], mhl[:, q], identb[:]).then_inc(t_m, 1)

            def step(g, par):
                o = 1 - par
                for t in range(GT):
                    T = g * GT + t
                    scores_k(T, t, par if t < 3 else o)
                    if t == 2 and valid(g + 1):
                        wait(pe, d_qb, g + 2)
                    scores_q(T, t, par if t < 2 else o)
                    if t == 0 and valid(g + 1):
                        wait(pe, e_xh, g + 2)
                        wait(pe, e_x2n, g - 2)
                        for i in range(GT):
                            last = nc.tensor.transpose(g1[:, i * P:(i + 1) * P], xh[:, o, i], ident[:])
                        last.then_inc(t_b, 1)
                    if t == 1 and valid(g + 1):
                        wait(pe, d_lg, g - 2)
                        nc.tensor.matmul(g1[:], wqk[:, D:2 * D], xnT[:, o], start=True, stop=True).then_inc(t_k, 1)
                    if t == 2 and valid(g - 1):
                        wait(pe, d_ctx, g * GT, NT)
                        wait(pe, e_km, g + 2)
                        wait(pe, d_lg, g - 2)
                        for i in range(GT):
                            last = nc.tensor.matmul(g1[:, i * P:(i + 1) * P], ctxT[:, o, i * P:(i + 1) * P], wo[:],
                                                    start=True, stop=True)
                        last.then_inc(t_o, 1)
                    if t == 3 and valid(g - 2):
                        wait(pe, d_xh2, g - 1)
                        wait(pe, d_x3, g)
                        wait(pe, d_lg, g - 2)
                        for i in range(GT):
                            last = nc.tensor.transpose(g1[:, i * P:(i + 1) * P], xh2s[:, par, i], ident[:])
                        last.then_inc(t_b2, 1)
                    weighted(g, T, t, par)
                    xpose_max(T, t)
                    if t == 0 and valid(g + 1):
                        wait(pe, d_xnT, g + 2)
                        wait(pe, d_x2, g + 2)
                        nc.tensor.matmul(g0[:], wqk[:, 0:D], xnT[:, o], start=True, stop=True).then_inc(t_q, 1)
                    if t == 0 and valid(g - 3):
                        wait(pe, e_x2n, g - 2)
                        wait(pe, d_xnT, g + 2)
                        for i in range(GT):
                            last = nc.tensor.matmul(lps[:, i * (E + 2):(i + 1) * (E + 2)],
                                                    x2nT[:, o, i * P:(i + 1) * P], gc[:], start=True, stop=True)
                        last.then_inc(t_l, 1)
                    if t == 1 and valid(g + 1):
                        wait(pe, e_qm, g + 2)
                        for b in range(GB):
                            for h2 in range(2):
                                last = nc.tensor.matmul(g0[h2 * L:(h2 + 1) * L, b * L:(b + 1) * L],
                                                        xnT[:, o, b * L:(b + 1) * L], wv[:, h2],
                                                        start=True, stop=True)
                        last.then_inc(t_v, 1)
                    if t == 2 and valid(g + 2):
                        wait(pe, e_vtx, g + 3)
                        wait(pe, d_vm, g + 2)
                        for i in range(GT):
                            last = nc.tensor.matmul(g0[:, i * P:(i + 1) * P], vtx[:, par, i * P:(i + 1) * P], m2[:],
                                                    start=True, stop=True)
                        last.then_inc(t_a, 1)
                    spread_den(T, t)
            groups(pe, step, FIRST, LAST, LO, HI)


def experts(K, scope):
    nc, a, out, bank, pair, cols, ident = (K[n] for n in "nc a out bank pair cols ident".split())
    x3, xh2, xt_dram, logits, sem, xs_dram = K["x3"], K["xh2"], K["xt_dram"], K["logits"], K["sem"], K["xs_dram"]

    def sb(name, shape, dt=F32):
        return K["sb"](name, shape, dt, scope)

    w1 = sb("w1", [P, E, W1W])
    w2 = sb("w2", [P, E, FC * D])
    rw1 = sb("rw1", [P, FF])
    rw2 = sb("rw2", [P, FC, D])
    rb2 = sb("rb2", [P, D])
    c1 = sb("c1", [P, NT])
    c0g = sb("c0g", [P, NT])
    token = sb("token", [P, NT])
    slot = sb("slot", [P, NT], I32)
    eid = sb("eid", [1, SLOTS], I32)
    prio = sb("prio", [P, E])
    triu = sb("triu", [P, P], BF16)
    oneb = sb("oneb", [P, P], BF16)
    jrow = sb("jrow", [1, SLOTS])
    dif = sb("dif", [P, NT, E])
    ex = sb("ex", [P, NT, E])
    oh = sb("oh", [P, NT, E])
    ohb = sb("ohb", [P, NT, E], BF16)
    tmp = sb("tmp", [P, NT, E])
    cum = [sb(f"cum{i}", [P, NT + 1, E]) for i in range(2)]
    cumb = sb("cumb", [P, NT + 1, E], BF16)
    r1 = sb("r1", [P, NT])
    r2 = sb("r2r", [P, NT])
    gate = sb("gate", [P, NT])
    cl = sb("cl", [P, NT, 2])
    ec = sb("ec", [P, NT, 2])
    small = sb("small", [P, 8, E])
    smalli = sb("smalli", [P, 2, E], I32)
    cmp = sb("cmp", [1, SLOTS, E])
    er = sb("er", [1, SLOTS])
    hs = sb("hs", [P, 2, FC, GT * P])
    x2g = sb("x2g", [P, IB, GT, D])
    tmp2 = sb("tmp2", [P, GT, D])
    xg = sb("xg", [P, IB, GT * P])
    xsl = sb("xsl", [P, IB, 2, XW])
    xsT = sb("xsT", [P, 2, 2 * P])
    w1b = sb("w1b", [P, YB, W1W])
    hT = sb("hT", [P, 2, FC, P])
    weight = sb("weight", [P, YB])
    number = sb("number", [P, YB], I32)
    yb2 = sb("yb2", [P, 2, D])
    ysb = sb("ysb", [P, YB, D])

    rbank = [bank[2], bank[3]]
    rankb, totb = bank[4], bank[5]
    xbank = bank[3]
    s_r, s_w, s_sc, s_base = sem("s_r"), sem("s_w"), sem("s_sc"), sem("s_base")
    r_d, r_e, r_ec, r_oh, r_cum, r_rank, d_idx = (sem("r_" + n) for n in "d e ec oh cum rank idx".split())
    s_xr, s_xg, s_xs = ([sem(f"{n}{i}") for i in range(IB)] for n in "s_xr s_xg s_xs".split())
    s_acc = [sem(f"s_acc{i}") for i in range(YB)]
    f_l1, f_ge, f_l2, f_r, f_x3, f_a = (sem("f_" + n) for n in "l1 ge l2 r x3 a".split())
    x_tr, x_xt, x_meta, x_w1, x_l1, x_ge, x_l2, x_b2, x_y = (
        sem("x_" + n) for n in "tr xt meta w1 l1 ge l2 b2 y".split())
    NR, NSH, NW = 5, 3, 5
    s_sh = sem("s_sh")
    NU = SLOTS // 2
    out_v = out[0:B * L, :].rearrange("(t p) d -> p t d", p=P)
    x2_v = K["x2_dram"].rearrange("(t p) d -> p t d", p=P)
    xs_v = xs_dram.rearrange("(t p) d -> p t d", p=P)

    def per_tile(v):
        return v[:].unsqueeze(2).broadcast_to([P, NT, E])

    with nc.Block() as block:
        @block.sync
        def _(sp):
            def load(g, buf):
                wait(sp, f_l1, FC * (g - IB + 1), FC * NG)
                sp.dma_start(xg[:, buf], xt_dram[bass.ds(g, 1)].rearrange("g p c -> p (g c)")).then_inc(s_xg[buf], 16)
                wait(sp, f_a, g - IB + 1)
                sp.dma_start(x2g[:, buf], x2_v[:, bass.ds(g * GT, GT), :]).then_inc(s_xr[buf], 16)

            def base(g):
                wait(sp, f_x3, g + 1)
                sp.dma_start(out_v[:, bass.ds(g * GT, GT), :], x3[:, bass.ds(g * GT, GT), :]).then_inc(s_base, 16)

            sp.dma_start(rw1[:], a["rw1"]).then_inc(s_sh, 16)
            load(0, 0)
            sp.dma_start(rw2[:], a["rw2"]).then_inc(s_sh, 16)
            sp.dma_start(rb2[:], a["rb2"].partition_broadcast(P)).then_inc(s_sh, 16)
            for dst, src in ((prio[:], a["prio"].partition_broadcast(P)), (triu[:].bitcast(U16), a["triu"]),
                             (oneb[:].bitcast(U16), a["oneb"]), (jrow[:], a["jrow"]), (token[:], a["token"])):
                sp.dma_start(dst, src).then_inc(s_r, 16)
            for g in range(1, IB):
                load(g, g)
            sp.dma_start(w1[:, :, FF + FC:], bass.AP(a["b2"].tensor, 0, [[0, P], [D, E], [1, D]])).then_inc(s_w, 16)
            for h in range(2):
                half = slice(h * E // 2, (h + 1) * E // 2)
                sp.dma_start(w1[:, half, 0:FF + FC], a["w1"][:, half]).then_inc(s_w, 16)
                sp.dma_start(w2[:, half], a["w2"][:, half]).then_inc(s_w, 16)

            def ahead(g, buf):
                load(g, buf)
                base(g - IB)
            groups(sp, ahead, IB, NG - 1, IB, NG, IB)
            for g in range(NG - IB, NG):
                base(g)
            sp.wait_ge(s_sc, 16 * NT)

            def slots(u, buf):
                wait(sp, x_tr, u - IB + 1, NU)
                wait(sp, x_meta, u - IB + 1, NU)
                sp.dma_start(xsl[:, buf], xs_v[:, bass.ds(u * 2, 2), :]).then_inc(s_xs[buf], 16)
            groups(sp, slots, 0, NU - 1, IB, NU, IB)
            sp.wait_ge(s_base, 16 * NG)

        @block.gpsimd
        def _(pool):
            pool.wait_ge(d_idx, 1)
            for T in range(NT):
                pool.indirect_dma_start(xs_dram, bass.IndirectOffsetOnAxis(ap=slot[:, T:T + 1], axis=0),
                                        xh2[:, T], None).then_inc(s_sc, 16)
            pool.wait_ge(s_sc, 16 * NT)
            pool.wait_ge(s_base, 16 * NG)
            for v in range(SLOTS):
                pool.wait_ge(x_y, v + 1)
                pool.indirect_dma_start(out, bass.IndirectOffsetOnAxis(ap=number[:, v % YB:v % YB + 1], axis=0),
                                        ysb[:, v % YB], None, compute_op=ALU.add).then_inc(s_acc[v % YB], 16)
            for i in range(YB):
                pool.wait_ge(s_acc[i], 16 * (SLOTS // YB))

        @block.scalar
        def _(act):
            act.wait_ge(r_e, 1)
            nc.scalar.activation(ex[:].rearrange("p t e -> p (t e)"), dif[:].rearrange("p t e -> p (t e)"),
                                 ACT.Exp)
            nc.scalar.activation(ec[:].rearrange("p t e -> p (t e)"), cl[:].rearrange("p t e -> p (t e)"),
                                 ACT.Exp).then_inc(r_ec, 1)

            def shared(g, par):
                for j in range(FC):
                    wait(act, f_l2, g - 1)
                    wait(act, f_l1, FC * g + j + 1, FC * NG)
                    nc.scalar.activation(hs[:, par, j], bank[j % 2][:], ACT.Gelu,
                                         bias=cols[:, C_RB1 + j:C_RB1 + j + 1]).then_inc(f_ge, 1)
            groups(act, shared, 0, NG - 1, 2, NG)

            def step(u, par):
                for k in range(2):
                    v = u * 2 + k
                    wait(act, x_l1, v + 1, SLOTS)
                    wait(act, x_l2, v - 1, SLOTS)
                    for j in range(FC):
                        last = nc.scalar.activation(hT[:, k, j], pair[:, k, j * P:(j + 1) * P], ACT.Gelu,
                                                    bias=w1b[:, 2 * par + k, FF + j:FF + j + 1])
                    last.then_inc(x_ge, 1)
            groups(act, step, 0, NU - 1, 2, NU)

        @block.vector
        def _(dve):
            links = [0]

            def link(ins):
                links[0] += 1
                ins.then_inc(r_d, 1)
                dve.wait_ge(r_d, links[0])

            lg = logits[:, :, 0:E]
            nc.vector.tensor_reduce(r1[:], lg, AX.X, ALU.max)
            link(nc.vector.tensor_tensor(cl[:], logits[:, :, E:E + 2],
                                         K["coefb"][:].unsqueeze(1).broadcast_to([P, NT, 2]), ALU.add))
            nc.vector.tensor_tensor(dif[:], lg, per_tile(r1), ALU.subtract)
            link(nc.vector.tensor_reduce(r2[:], cl[:], AX.X, ALU.max))
            nc.vector.tensor_tensor(cl[:], cl[:], r2[:].unsqueeze(2).broadcast_to([P, NT, 2]),
                                    ALU.subtract).then_inc(r_e, 1)
            dve.wait_ge(s_r, 16 * NR)
            dve.wait_ge(r_e, 1)
            link(nc.vector.scalar_tensor_tensor(tmp[:], dif[:], 0.0,
                                                prio[:].unsqueeze(1).broadcast_to([P, NT, E]), ALU.is_ge, ALU.mult))
            link(nc.vector.tensor_reduce(r1[:], tmp[:], AX.X, ALU.max))
            link(nc.vector.tensor_tensor(oh[:], tmp[:], per_tile(r1), ALU.is_equal))
            nc.vector.tensor_copy(ohb[:], oh[:]).then_inc(r_oh, 1)
            nc.vector.memset(cum[0][:, 0], 0.0)
            nc.vector.memset(cum[1][:, 0], 0.0)
            link(nc.vector.tensor_copy(cum[0][:, 1:NT + 1], oh[:]))
            k, src, dst = 1, cum[0], cum[1]
            while k < NT:
                nc.vector.tensor_copy(dst[:, 1:k + 1], src[:, 1:k + 1])
                link(nc.vector.tensor_tensor(dst[:, k + 1:NT + 1], src[:, k + 1:NT + 1], src[:, 1:NT + 1 - k],
                                             ALU.add))
                k, src, dst = 2 * k, dst, src
            nc.vector.tensor_copy(cumb[:], src[:]).then_inc(r_cum, 1)
            dve.wait_ge(r_ec, 1)
            nc.vector.tensor_reduce(r1[:], ex[:], AX.X, ALU.add)
            link(nc.vector.tensor_reduce(r2[:], ec[:], AX.X, ALU.add))
            nc.vector.reciprocal(gate[:], r1[:])
            link(nc.vector.reciprocal(r2[:], r2[:]))
            nc.vector.tensor_tensor(c1[:], ec[:, :, 1], r2[:], ALU.mult)
            link(nc.vector.tensor_tensor(c0g[:], ec[:, :, 0], r2[:], ALU.mult))
            nc.vector.tensor_tensor(xh2[:, :, D], c0g[:], gate[:], ALU.mult)
            link(nc.vector.tensor_copy(xh2[:, :, D + 1], token[:]))

            rb2_bc = rb2[:].unsqueeze(1).broadcast_to([P, GT, D])

            def shared(g, buf):
                rows = x3[:, bass.ds(g * GT, GT), :]
                wait(dve, s_xr[buf], nth(g, buf, NG, IB), 16 * NG)
                nc.vector.tensor_tensor(rows, rows, x2g[:, buf], ALU.add).then_inc(f_a, 1)
                wait(dve, f_l2, g + 1)
                wait(dve, f_x3, g)
                nc.vector.tensor_tensor(tmp2[:], rbank[buf % 2][:].rearrange("p (t d) -> p t d", t=GT), rb2_bc,
                                        ALU.add).then_inc(f_r, 1)
                wait(dve, f_r, g + 1)
                wait(dve, f_a, g + 1)
                for i in range(GT):
                    T = g * GT + i
                    last = nc.vector.scalar_tensor_tensor(x3[:, T, :], tmp2[:, i], c1[:, bass.ds(T, 1)],
                                                          x3[:, T, :], ALU.mult, ALU.add)
                last.then_inc(f_x3, 1)
            dve.wait_ge(s_sh, 16 * NSH)
            shared(0, 0)
            shared(1, 1)

            dve.wait_ge(r_rank, 1)
            link(nc.vector.tensor_scalar(smalli[:, 0], totb[:, 0:E], float(P - 1), None, ALU.add))
            link(nc.vector.tensor_scalar(smalli[:, 1], smalli[:, 0], 7, None, ALU.logical_shift_right))
            link(nc.vector.tensor_copy(small[:, 0], smalli[:, 1]))
            k, i = 1, 0
            while k < E:
                nc.vector.tensor_copy(small[:, i + 1, 0:k], small[:, i, 0:k])
                link(nc.vector.tensor_tensor(small[:, i + 1, k:E], small[:, i, k:E], small[:, i, 0:E - k], ALU.add))
                k, i = 2 * k, i + 1
            end = small[:, i]
            link(nc.vector.tensor_tensor(small[:, i + 1], end, small[:, 0], ALU.subtract))
            link(nc.vector.tensor_scalar(small[:, i + 2], small[:, i + 1], float(P), None, ALU.mult))
            link(nc.vector.tensor_tensor(tmp[:], rankb[:].rearrange("p (t e) -> p t e", e=E),
                                         small[:, i + 2].unsqueeze(1).broadcast_to([P, NT, E]), ALU.add))
            link(nc.vector.tensor_tensor(tmp[:], tmp[:], oh[:], ALU.mult))
            link(nc.vector.tensor_reduce(r1[:], tmp[:], AX.X, ALU.add))
            nc.vector.tensor_copy(slot[:], r1[:]).then_inc(d_idx, 1)
            link(nc.vector.tensor_tensor(cmp[:], jrow[:].unsqueeze(2).broadcast_to([1, SLOTS, E]),
                                         end[0:1].unsqueeze(1).broadcast_to([1, SLOTS, E]), ALU.is_ge))
            link(nc.vector.tensor_reduce(er[:], cmp[:], AX.X, ALU.add))
            nc.vector.tensor_scalar(eid[:], er[:], float(E - 1), None, ALU.min).then_inc(d_idx, 1)
            groups(dve, shared, 2, NG - 1, IB, NG, IB)
            dve.wait_ge(s_w, 16 * NW)
            dve.wait_ge(d_idx, 2)

            def spread(u, par):
                wait(dve, x_tr, u + 1, NU)
                wait(dve, x_l1, 2 * (u - 1), SLOTS)
                nc.vector.tensor_scalar(xsT[:, par], xbank[:, 0:2 * P], cols[:, C_G2:C_G2 + 1],
                                        cols[:, C_B2:C_B2 + 1], ALU.mult, ALU.add).then_inc(x_xt, 1)

            def meta(u, buf, par):
                wait(dve, s_xs[buf], nth(u, buf, NU, IB), 16 * NU)
                wait(dve, x_y, 2 * (u - 1), SLOTS)
                nc.vector.tensor_copy(weight[:, 2 * par:2 * par + 2], xsl[:, buf, :, D])
                for k in range(2):
                    wait(dve, s_acc[2 * par + k], nth(u - 2, par, NU), 8 * NU)
                nc.vector.tensor_copy(number[:, 2 * par:2 * par + 2], xsl[:, buf, :, D + 1]).then_inc(x_meta, 1)

            def fetch(u, par, k):
                v = u * 2 + k
                e = dve.value_load(eid[0:1, bass.ds(v, 1)], min_val=0, max_val=E - 1)
                wait(dve, x_y, v - 3, SLOTS)
                wait(dve, x_ge, v - 3, SLOTS)
                nc.vector.tensor_copy(w1b[:, 2 * par + k], w1[:, e, :]).then_inc(x_w1, 1)

            def rows_out(v, par, k):
                i = 2 * par + k
                wait(dve, x_l2, v + 1, SLOTS)
                wait(dve, x_y, v - 1, SLOTS)
                nc.vector.tensor_tensor(yb2[:, k], bank[4 + k][:, 0:D], w1b[:, i, FF + FC:], ALU.add).then_inc(x_b2, 1)
                wait(dve, x_b2, v + 1, SLOTS)
                nc.vector.tensor_scalar(ysb[:, i], yb2[:, k], weight[:, i:i + 1], None, ALU.mult).then_inc(x_y, 1)

            def step(u, buf):
                par = buf % 2
                o = 1 - par
                if valid(u + 1, NU):
                    fetch(u + 1, o, 0)
                if valid(u, NU):
                    meta(u, buf, par)
                if valid(u - 1, NU):
                    rows_out(u * 2 - 1, o, 1)
                if valid(u + 1, NU):
                    spread(u + 1, o)
                if valid(u + 1, NU):
                    fetch(u + 1, o, 1)
                if valid(u, NU):
                    rows_out(u * 2, par, 0)
            groups(dve, step, -1, NU, IB, NU - IB, IB)

        @block.tensor
        def _(pe):
            pe.wait_ge(s_sh, 16 * NSH)

            def shared(g, buf):
                par = buf % 2
                if valid(g):
                    wait(pe, s_xg[buf], nth(g, buf, NG, IB), 16 * NG)
                    for j in range(FC):
                        wait(pe, f_ge, FC * g + j - 1, FC * NG)
                        nc.tensor.matmul(bank[j % 2][:], rw1[:, j * P:(j + 1) * P], xg[:, buf],
                                         start=True, stop=True).then_inc(f_l1, 1)
                if valid(g - 1):
                    wait(pe, f_ge, FC * g, FC * NG)
                    wait(pe, f_r, g - 2)
                    for i in range(GT):
                        for j in range(FC):
                            last = nc.tensor.matmul(rbank[1 - par][:, i * P:(i + 1) * P],
                                                    hs[:, 1 - par, j, i * P:(i + 1) * P], rw2[:, j],
                                                    start=(j == 0), stop=(j == FC - 1))
                    last.then_inc(f_l2, 1)

            def ranks():
                pe.wait_ge(s_r, 16 * NR)
                pe.wait_ge(r_oh, 1)
                pe.wait_ge(r_cum, 1)
                nc.tensor.matmul(rankb[:], triu[:], ohb[:].rearrange("p t e -> p (t e)"), start=True, stop=False)
                nc.tensor.matmul(rankb[:], oneb[:], cumb[:, 0:NT].rearrange("p t e -> p (t e)"),
                                 start=False, stop=True)
                nc.tensor.matmul(totb[:, 0:E], oneb[:], cumb[:, NT], start=True, stop=True).then_inc(r_rank, 1)

            for g in range(3):
                shared(g, g)
            ranks()
            shared(3, 3)
            groups(pe, shared, IB, NG, IB, NG, IB)
            pe.wait_ge(f_x3, NG)
            pe.wait_ge(s_w, 16 * NW)
            pe.wait_ge(d_idx, 2)

            def turn(u, buf):
                wait(pe, s_xs[buf], nth(u, buf, NU, IB), 16 * NU)
                wait(pe, x_xt, u, NU)
                for k in range(2):
                    last = nc.tensor.transpose(xbank[:, k * P:(k + 1) * P], xsl[:, buf, k, 0:D], ident[:])
                last.then_inc(x_tr, 1)

            def layer2(v, k):
                e = pe.value_load(eid[0:1, bass.ds(v, 1)], min_val=0, max_val=E - 1)
                wait(pe, x_ge, v + 1, SLOTS)
                wait(pe, x_b2, v - 1, SLOTS)
                for j in range(FC):
                    last = nc.tensor.matmul(bank[4 + k][:, 0:D], hT[:, k, j], w2[:, e, j * D:(j + 1) * D],
                                            start=(j == 0), stop=(j == FC - 1))
                last.then_inc(x_l2, 1)

            def step(u, buf):
                par = buf % 2
                if isinstance(u, int) and u == 0:
                    turn(u, buf)
                for k in range(2):
                    v = u * 2 + k
                    if valid(u, NU):
                        if k == 0:
                            wait(pe, x_xt, u + 1, NU)
                        wait(pe, x_w1, v + 1, SLOTS)
                        wait(pe, x_ge, v - 1, SLOTS)
                        for j in range(FC):
                            last = nc.tensor.matmul(pair[:, k, j * P:(j + 1) * P],
                                                    w1b[:, 2 * par + k, j * P:(j + 1) * P],
                                                    xsT[:, par, k * P:(k + 1) * P], start=True, stop=True)
                        last.then_inc(x_l1, 1)
                    if k == 0 and valid(u + 1, NU):
                        turn(u + 1, (buf + 1) % IB)
                    if valid(v - 1, SLOTS):
                        layer2(v - 1, 1 - k)
            groups(pe, step, 0, NU, IB, NU - IB, IB)


_OUT = ((B, L, D), "float32")


def layouts(i):
    import numpy as np
    f = np.float32
    heads = np.arange(P) // DH
    rev = (L - np.arange(L)) % L
    mq = np.stack([((heads % 8) // 2 == hp) / np.sqrt(DH) for hp in range(4)], 1).astype(f)
    mk = np.stack([heads % 2 == h2 for h2 in range(2)], 1).astype(f)
    wqkv, bqkv = i["L0_ffn_Wqkv"], i["L0_ffn_bqkv"]
    msel = np.zeros((32, 8, 2, L), np.uint16)
    for n in range(8):
        for h2 in range(2):
            msel[2 * n + h2, n, h2] = BF16_ONE
            msel[16 + 2 * n + h2, n, h2] = BF16_ONE
    sel = np.zeros((16, DQ, 2, 16, 4), f)
    for r in range(4):
        for p in range(2):
            sel[np.arange(16), 2 * r + p, p, np.arange(16), r] = 1
    dmask = np.zeros((2, L, 4, 4, 2), f)
    for hp in range(4):
        for h2 in range(2):
            dmask[h2, :, hp, hp, h2] = 1
    blank = np.zeros((P, GT, XW), f)
    blank[:, :, D + 1] = B * L + np.arange(YB)[None, :] * P + np.arange(P)[:, None]
    w1 = i["L0_ffn_W1"].transpose(1, 0, 2)
    b1 = i["L0_ffn_b1"].reshape(E, FC, P).transpose(2, 0, 1)
    return {
        "x": i["x"].reshape(B * L, D),
        "ctx": i["ctx_1024"].reshape(B * L, D),
        "wq8": i["L0_xattn_Wq"],
        "bq8": i["L0_xattn_bq"].reshape(1, DQ),
        "wout_rev": np.concatenate([i["L0_xattn_Wout"][rev], i["L0_xattn_Wout"][L + rev]], 0),
        "bout": i["L0_xattn_bout"].reshape(1, D),
        "cols": np.concatenate([np.stack([i["L0_ffn_ln1_g"], i["L0_ffn_ln1_b"], i["L0_ffn_ln2_g"],
                                          i["L0_ffn_ln2_b"], bqkv[0:D], bqkv[D:2 * D], bqkv[2 * D:]], 1),
                                i["L0_ffn_rb1"].reshape(FC, P).T, mq, mk], 1),
        "wqk": wqkv[:, 0:2 * D],
        "wv": wqkv[:, 2 * D:].reshape(D, 8, 2, DH).transpose(0, 2, 1, 3).reshape(D, 2, L),
        "wo": i["L0_ffn_Wo"],
        "bo": i["L0_ffn_bo"].reshape(1, D),
        "gc": np.concatenate([i["L0_ffn_gate_w"], i["L0_ffn_coef_w"]], 1),
        "coef_b": i["L0_ffn_coef_b"].reshape(1, 2),
        "w1": np.concatenate([w1, b1], 2),
        "w2": i["L0_ffn_W2"].reshape(E, FC, P, D).transpose(2, 0, 1, 3).reshape(P, E, FC * D),
        "b2": i["L0_ffn_b2"].reshape(E, D),
        "rw1": i["L0_ffn_rW1"],
        "rw2": i["L0_ffn_rW2"].reshape(FC, P, D).transpose(1, 0, 2),
        "rb2": i["L0_ffn_rb2"].reshape(1, D),
        "ident": np.eye(P, dtype=f),
        "identb": np.diag(np.full(P, BF16_ONE, np.uint16)),
        "oneb": np.full((P, P), BF16_ONE, np.uint16),
        "triu": np.triu(np.full((P, P), BF16_ONE, np.uint16), 1),
        "sel": sel.reshape(P, 2, L),
        "msel": msel.reshape(32, 8, P),
        "dmask": dmask.reshape(P, 4, H // 2),
        "dspread": np.repeat(np.eye(H // 2, dtype=f), DH, 1),
        "prio": np.arange(E, 0, -1, dtype=f).reshape(1, E),
        "blank": blank,
        "token": (np.arange(NT)[None, :] * P + np.arange(P)[:, None]).astype(f),
        "jrow": np.arange(SLOTS, dtype=f).reshape(1, SLOTS),
    }


def kernel(**inputs):
    import numpy as np
    import concourse.bacc as bacc
    from concourse.bass_utils import run_bass_kernel_spmd

    nc = bacc.Bacc("TRN2", target_bir_lowering=False, num_devices=1)
    arrays = {n: np.ascontiguousarray(v) for n, v in layouts({n: np.asarray(v) for n, v in inputs.items()}).items()}
    aps = {n: nc.dram_tensor(f"in_{n}", v.shape, mybir.dt.from_np(v.dtype), kind="ExternalInput").ap()
           for n, v in arrays.items()}
    out = nc.dram_tensor("out_0", (B * L + YB * P, D), F32, kind="ExternalOutput").ap()
    build(nc, aps, out)
    r = run_bass_kernel_spmd(nc, [{f"in_{n}": v for n, v in arrays.items()}], core_ids=[0])
    return r.results[0]["out_0"][:B * L].reshape(_OUT[0])
```

```python
from contextlib import ExitStack

import concourse.bass as bass
from concourse import mybir

F32 = mybir.dt.float32
F32R = mybir.dt.float32r
BF16 = mybir.dt.bfloat16
I32 = mybir.dt.int32
U16 = mybir.dt.uint16
ALU = mybir.AluOpType
ACT = mybir.ActivationFunctionType
AX = mybir.AxisListType

P = 128
B, L, D = 128, 64, 128
NT = B * L // P
GT = 4
NG = NT // GT
GB = GT * P // L
IB = 4
DQ = 8
H, DH = 16, 8
E = 8
FF = 512
FC = FF // P
SLOTS = NT + E
K_TOP = 11
EPS = 1e-5
NEG = -3.0e38
BF16_ONE = 0x3F80
W1W = FF + FC + D
XW = D + 2
VW = L + H // 2
NR = 8
NC2 = 9
YB = 4

C_G1, C_B1, C_G2, C_B2, C_BQ, C_BK, C_BV, C_RB1 = 0, 1, 2, 3, 4, 5, 6, 7
C_MQ = C_RB1 + FC
C_MK = C_MQ + 4
C_BA = C_MK + 2
NCOL = C_BA + 1


def groups(eng, step, first, last, lo, hi, n=2):
    assert lo % n == 0 and hi % n == 0
    for g in range(first, lo):
        step(g, g % n)
    with eng.Fori(0, (hi - lo) // n) as i:
        for k in range(n):
            step(i * n + (lo + k), k)
    for g in range(hi, last + 1):
        step(g, g % n)


def valid(g, n=NG):
    return not isinstance(g, int) or 0 <= g < n


def wait(eng, sem, count, most=NG):
    if isinstance(count, int):
        count = min(count, most)
        if count <= 0:
            return
    eng.wait_ge(sem, count)


def nth(g, par, most=NG, n=2):
    if isinstance(g, int):
        g = min(g, most - n + par)
    return 16 // n * (g - par + n)


def settle(eng, cell):
    eng.memset(cell, 0.0)


def build(nc, a, out):
    ctx = ExitStack()
    with ctx:
        def sb(name, shape, dt=F32, scope=ctx):
            return scope.enter_context(nc.sbuf_tensor(name, shape, dt))

        def sem(name):
            return ctx.enter_context(nc.semaphore(name))

        bank = [ctx.enter_context(nc.psum_tensor(f"bank{i}", [P, 512], F32)) for i in range(6)]
        pair = ctx.enter_context(nc.psum_tensor("pair", [P, 2, 512], F32))

        corr_dram = nc.dram_tensor("corr_dram", [L, 2 * L], F32, kind="Internal").ap()
        shift_dram = nc.dram_tensor("shift_dram", [1, 2 * L], F32, kind="Internal").ap()
        xs_dram = nc.dram_tensor("xs_dram", [SLOTS * P, XW], F32, kind="Internal").ap()
        xa_dram = nc.dram_tensor("xa_dram", [B * 4, D], F32, kind="Internal").ap()
        xt_dram = nc.dram_tensor("xt_dram", [NG, P, GT * P], F32, kind="Internal").ap()

        cols = sb("cols", [P, NCOL])
        ident = sb("ident", [P, P])
        ones = sb("ones", [P, P])
        x3 = sb("x3", [P, NT, D])
        xh2 = sb("xh2", [P, NT, XW])
        logits = sb("logits", [P, NT, E + 2])
        coefb = sb("coefb", [P, 2])
        s_const = sem("s_const")
        x2_dram = nc.dram_tensor("x2_dram", [B * L, D], F32, kind="Internal").ap()
        K = dict(x2_dram=x2_dram, xa_dram=xa_dram, nc=nc, a=a, out=out, sb=sb, sem=sem, bank=bank, pair=pair, cols=cols, ident=ident,
                 ones=ones, x3=x3, xh2=xh2, xt_dram=xt_dram, logits=logits, coefb=coefb, s_const=s_const,
                 corr_dram=corr_dram, shift_dram=shift_dram, xs_dram=xs_dram)
        K.update(rw1=sb("rw1", [P, FF]), rw2=sb("rw2", [P, FC, D]), rb2=sb("rb2", [P, D]), prio=sb("prio", [P, E]),
                 triu=sb("triu", [P, P], BF16), oneb=sb("oneb", [P, P], BF16), jrow=sb("jrow", [1, SLOTS]),
                 token=sb("token", [P, NT]), s_r=sem("s_r"))
        with ExitStack() as mid:
            cvec = sb("cvec", [P, D], scope=mid)
            wo = sb("wo", [P, D], scope=mid)
            vm = sb("vm", [P, 2, GB, 2, 4, VW], scope=mid)
            K.update(
                wqk=sb("wqk", [P, 2 * D], scope=mid),
                wv=sb("wv", [P, D], scope=mid),
                gc=sb("gc", [P, E + 2], scope=mid),
                bout=sb("bout", [P, D], scope=mid),
                identb=sb("identb", [P, P], BF16, scope=mid),
                msel=sb("msel", [32, 8, P], BF16, scope=mid),
                dmask=sb("dmask", [P, 4, H // 2], scope=mid),
                dspread=sb("dspread", [H // 2, L], scope=mid),
                blank=sb("blank", [P, GT, XW], scope=mid),
                bqm=sb("bqm", [P, 6], scope=mid),
                xin=sb("xin", [P, 2, GT, D], scope=mid),
                s_c2=sem("s_c2"), s_xi=[sem(f"s_xi{i}") for i in range(2)])
            with ExitStack() as scope:
                correlate(K, scope, cvec, wo, vm)
            with ExitStack() as scope:
                attention(K, scope, cvec, wo, vm)
        with ExitStack() as scope:
            experts(K, scope)


def correlate(K, scope, cvec, wo, vm):
    nc, a, bank, cols, ident, ones = K["nc"], K["a"], K["bank"], K["cols"], K["ident"], K["ones"]
    s_const, s_c2, sem = K["s_const"], K["s_c2"], K["sem"]
    corr_dram, shift_dram = K["corr_dram"], K["shift_dram"]

    def sb(name, shape, dt=F32):
        return K["sb"](name, shape, dt, scope)

    wq8 = sb("wq8", [P, DQ])
    wqp = sb("wqp", [P, 4, 4 * DQ])
    sel = sb("sel", [P, 2, L])
    wout = sb("wout", [P, D])
    bo_bc = sb("bo_bc", [P, D])
    xin = sb("xin1", [P, IB, GT, D])
    cin = sb("cin1", [P, IB, GT, D])
    xn = sb("xn1", [P, 2, GT, D])
    cT = sb("cT1", [P, 2, GT * P])
    xT = sb("xT1", [P, 2, GT * P])
    st6 = sb("st6", [P, 2, GT, 6])
    mv = sb("mv1", [P, 2, GT, 2])
    ve = sb("ve1", [P, 2, GT])
    rs = sb("rs1", [P, 2, GT])
    nhalf = sb("nhalf1", [P, GT])
    eps = sb("eps1", [P, GT])
    idle = sb("idle1", [P, 1])

    kqT = sb("kqT", [P, 2, 4 * P])

    s_x, s_c = ([sem(f"{n}{i}") for i in range(IB)] for n in ("c_x", "c_c"))
    d_nh, d_bs, d_st, d_norm, d_wq = (sem(n) for n in ("c_nh", "c_bs", "c_st", "c_norm", "c_wq"))
    p_ve, p_rs = sem("c_ve"), sem("c_rs")
    t_c, t_x, t_mm = sem("c_tc"), sem("c_tx"), sem("c_mm")
    e_c, e_x, e_kq = sem("c_ec"), sem("c_ex"), sem("c_ekq")
    NCONST = 6
    s_constp = sem("s_constp")
    x_src = a["x"].rearrange("(t p) d -> p t d", p=P)
    c_src = a["ctx"].rearrange("(t p) d -> p t d", p=P)

    with nc.Block() as block:
        @block.sync
        def _(sp):
            sp.dma_start(ident[:], a["ident"]).then_inc(s_const, 16)
            sp.dma_start(wq8[:], a["wq8"]).then_inc(s_const, 16)

            def load(g, buf):
                wait(sp, t_c, g - IB + 1)
                sp.dma_start(cin[:, buf], c_src[:, bass.ds(g * GT, GT), :]).then_inc(s_c[buf], 16)
                wait(sp, d_norm, g - IB + 1)
                sp.dma_start(xin[:, buf], x_src[:, bass.ds(g * GT, GT), :]).then_inc(s_x[buf], 16)
            groups(sp, load, 0, NG - 1, IB, NG, IB)
            for dst, name in ((K["wqk"][:], "wqk"), (K["wv"][:], "wv"), (K["gc"][:], "gc"),
                              (K["identb"][:].bitcast(U16), "identb"), (K["msel"][:].bitcast(U16), "msel"),
                              (K["dmask"][:], "dmask"), (K["dspread"][:], "dspread"), (K["blank"][:], "blank")):
                sp.dma_start(dst, a[name]).then_inc(K["s_c2"], 16)
            sp.dma_start(K["bout"][:], a["bout"].partition_broadcast(P)).then_inc(K["s_c2"], 16)
            for g in range(2):
                sp.dma_start(K["xin"][:, g], x_src[:, bass.ds(g * GT, GT), :]).then_inc(K["s_xi"][g], 16)

        @block.gpsimd
        def _(pool):
            pool.dma_start(cols[:], a["cols"]).then_inc(s_constp, 16)
            pool.dma_start(sel[:], a["sel"]).then_inc(s_constp, 16)
            pool.dma_start(wout[:], a["wout_rev"]).then_inc(s_constp, 16)
            pool.dma_start(bo_bc[:], a["bo"].partition_broadcast(P)).then_inc(s_constp, 16)
            pool.dma_start(wo[:], a["wo"]).then_inc(s_constp, 16)
            pool.dma_start(K["coefb"][:], a["coef_b"].partition_broadcast(P)).then_inc(s_constp, 16)
            pool.wait_ge(d_nh, 1)

            def rstd(g, buf):
                if valid(g + 1):
                    o = (buf + 1) % 2
                    wait(pool, d_st, g + 2)
                    wait(pool, d_norm, g)
                    pool.tensor_tensor(ve[:, o], mv[:, o, :, 1], eps[:], ALU.add).then_inc(p_ve, 1)
                    wait(pool, p_ve, g + 2)
                    pool.tensor_tensor(rs[:, o], ve[:, o], nhalf[:], ALU.pow).then_inc(p_rs, 1)
            groups(pool, rstd, -1, NG, IB, NG - IB, IB)

        @block.vector
        def _(dve):
            nc.vector.memset(eps[:], EPS)
            nc.vector.memset(nhalf[:], -0.5).then_inc(d_nh, 1)
            nc.vector.memset(ones[:], 1.0)
            nc.vector.memset(wqp[:], 0.0).then_inc(d_wq, 1)
            dve.wait_ge(s_const, 32)
            dve.wait_ge(d_wq, 1)
            for m in range(4):
                last = nc.vector.tensor_copy(wqp[:, m, m * DQ:(m + 1) * DQ], wq8[:])
            last.then_inc(d_wq, 1)

            def step(g, buf):
                par = buf % 2
                o = 1 - par
                nxt = (buf + 1) % IB
                if valid(g + 1):
                    wait(dve, s_x[nxt], nth(g + 1, nxt, NG, IB), 16 * NG)
                    wait(dve, d_st, g)
                    for t in range(GT):
                        last = nc.vector.bn_stats(st6[:, o, t], xin[:, nxt, t])
                    last.then_inc(d_bs, 1)
                    wait(dve, d_bs, g + 2)
                    wait(dve, d_norm, g)
                    settle(nc.vector, idle[:])
                    for t in range(GT):
                        last = nc.vector.bn_aggr(mv[:, o, t], st6[:, o, t])
                    last.then_inc(d_st, 1)
                if valid(g):
                    wait(dve, p_rs, g + 1)
                    wait(dve, t_x, g - 1)
                    for t in range(GT):
                        last = nc.vector.tensor_scalar(xn[:, par, t], xin[:, buf, t], mv[:, par, t, 0:1],
                                                       rs[:, par, t:t + 1], ALU.subtract, ALU.mult)
                    last.then_inc(d_norm, 1)
            groups(dve, step, -1, NG - 1, IB, NG - IB, IB)

        @block.scalar
        def _(act):
            act.wait_ge(s_constp, 16 * NCONST)

            def keep(blk4):
                for w in range(2):
                    last = nc.scalar.activation(kqT[:, w, bass.ds(blk4 * (P // 4), P)], bank[4 + w][:, 0:P],
                                                ACT.Identity, bias=cols[:, C_BA:C_BA + 1])
                last.then_inc(e_kq, 4)

            def step(g, buf):
                par = buf % 2
                wait(act, t_mm, g - 1)
                if buf == 1 and valid(g - 2):
                    keep(g - 5)
                wait(act, t_c, g + 1)
                nc.scalar.copy(cT[:, par], bank[par][:]).then_inc(e_c, 1)
                wait(act, t_x, g + 1)
                nc.scalar.copy(xT[:, par], bank[2 + par][:]).then_inc(e_x, 1)
            groups(act, step, 0, NG - 1, IB, NG, IB)
            act.wait_ge(t_mm, NG)
            keep(NG - 4)

        @block.tensor
        def _(pe):
            pe.wait_ge(s_const, 32)
            pe.wait_ge(d_wq, 2)

            def step(g, buf):
                par = buf % 2
                if valid(g):
                    wait(pe, s_c[buf], nth(g, buf, NG, IB), 16 * NG)
                    wait(pe, e_c, g - 1)
                    for t in range(GT):
                        last = nc.tensor.transpose(bank[par][:, t * P:(t + 1) * P], cin[:, buf, t], ident[:])
                    last.then_inc(t_c, 1)
                if valid(g - 1):
                    o = 1 - par
                    wait(pe, e_c, g)
                    wait(pe, e_x, g)
                    m = (buf + 3) % 4
                    if m == 0:
                        wait(pe, e_kq, g - 1)
                    for w, src in enumerate((cT, xT)):
                        for t in range(GT):
                            last = nc.tensor.matmul(
                                bank[4 + w][t * 4 * DQ:(t + 1) * 4 * DQ, 0:P],
                                wqp[:, m], src[:, o, t * P:(t + 1) * P], start=(m == 0), stop=(m == 3),
                                skip_group_check=True)
                    last.then_inc(t_mm, 1)
                if valid(g):
                    wait(pe, d_norm, g + 1)
                    wait(pe, e_x, g - 1)
                    for t in range(GT):
                        last = nc.tensor.transpose(bank[2 + par][:, t * P:(t + 1) * P], xn[:, par, t], ident[:])
                    last.then_inc(t_x, 1)
            groups(pe, step, 0, NG, IB, NG, IB)

    kT, qT = (kqT[:, w].rearrange("p (b l) -> p b l", l=P) for w in range(2))
    g2 = sb("g2", [L, 2, L])
    gs = sb("gs", [L, L])
    cor = sb("cor", [P, L])
    c2 = sb("c2", [P, L])
    c3 = sb("c3", [P, L])
    top = sb("top", [P, 16])
    nmax = sb("nmax", [P, 1])
    ew = sb("ew", [P, L])
    wsh = sb("wsh", [P, L])
    wsum = sb("wsum", [P, 2])
    wrow = sb("wrow", [P, 2, L])
    vts = sb("vts", [P, NG, 2, 4, GT])
    m2 = sb("m2", [P, D])
    xa = sb("xa", [P, 4, D])
    circ = sb("circ", [P, P])
    bvb = sb("bvb", [P, P])
    m_g, m_v, m_cor, m_m2, m_cv = (sem(n) for n in ("m_g", "m_v", "m_cor", "m_m2", "m_cv"))
    m_g2, m_bv, m_link, m_ex, m_w, m_z = (sem(n) for n in ("m_g2", "m_bv", "m_link", "m_ex", "m_w", "m_z"))
    m_gd, m_gl, m_wd, m_wl, m_vm = (sem(n) for n in ("m_gd", "m_gl", "m_wd", "m_wl", "m_vm"))
    m_vt, m_mm, m_ar, m_xa, m_xd = (sem(n) for n in ("m_vt", "m_mm", "m_ar", "m_xa", "m_xd"))

    with nc.Block() as block:
        @block.sync
        def _(sp):
            sp.wait_ge(m_g2, 1)
            sp.dma_start(corr_dram, g2[:].rearrange("t a s -> t (a s)")).then_inc(m_gd, 16)
            sp.wait_ge(m_gd, 16)
            sp.dma_start(gs[:], bass.AP(corr_dram.tensor, 0, [[2 * L + 1, L], [1, L]])).then_inc(m_gl, 16)
            sp.wait_ge(m_w, 1)
            sp.dma_start(shift_dram, wrow[0:1].rearrange("p a s -> p (a s)")).then_inc(m_wd, 16)
            sp.wait_ge(m_wd, 16)
            sp.wait_ge(m_z, 1)
            for i in range(2):
                sp.dma_start(circ[i * L:(i + 1) * L, i * L:(i + 1) * L],
                             bass.AP(shift_dram.tensor, 0, [[1, L], [1, L]])).then_inc(m_wl, 16)
            sp.wait_ge(m_wl, 32)
            sp.wait_ge(m_xa, 1)
            sp.dma_start(K["xa_dram"].rearrange("(k p) d -> p k d", p=P), xa[:]).then_inc(m_xd, 16)
            sp.wait_ge(m_xd, 16)

        @block.gpsimd
        def _(pool):
            pool.memset(vm[:], 0.0).then_inc(m_vm, 1)

        @block.tensor
        def _(pe):
            n = 0
            for blk in range(4):
                for b in range(2):
                    last = nc.tensor.matmul(bank[2][0:L, 0:L], kT[:, blk, b * L:(b + 1) * L],
                                            qT[:, blk, b * L:(b + 1) * L], start=(n == 0), stop=(n == 7))
                    n += 1
            last.then_inc(m_g, 1)
            for i in range(2):
                for blk in range(4):
                    for b in range(2):
                        c = (blk * 2 + b) * L
                        last = nc.tensor.matmul(bank[3][i * L:(i + 1) * L, c:c + L], kT[:, blk, b * L:(b + 1) * L],
                                                sel[:, i], start=True, stop=True)
            last.then_inc(m_v, 1)
            pe.wait_ge(m_bv, 1)
            nc.tensor.matmul(bank[1][:, 0:D], bvb[:], wo[:], start=True, stop=True).then_inc(m_cv, 1)
            pe.wait_ge(m_gl, 16)
            nc.tensor.matmul(bank[0][:, 0:L], ones[0:L, :], gs[:], start=True, stop=True).then_inc(m_cor, 1)
            pe.wait_ge(m_wl, 32)
            nc.tensor.matmul(bank[0][:, P:2 * P], circ[:], wout[:], start=True, stop=True).then_inc(m_m2, 1)
            pe.wait_ge(m_vt, 1)
            pe.wait_ge(m_mm, 1)
            for i in range(4):
                last = nc.tensor.matmul(bank[2][:, i * P:(i + 1) * P],
                                        vts[:, 4 * i:4 * i + 4].rearrange("p g b r t -> p (g b r t)"), m2[:],
                                        start=True, stop=True)
            last.then_inc(m_ar, 1)

        @block.scalar
        def _(act):
            act.wait_ge(m_link, 6)
            nc.scalar.activation(ew[:], cor[:], ACT.Exp, bias=nmax[:]).then_inc(m_ex, 1)

        @block.vector
        def _(dve):
            nc.vector.memset(circ[:], 0.0).then_inc(m_z, 1)
            nc.vector.tensor_scalar(bvb[:], ones[:], cols[:, C_BV:C_BV + 1], None, ALU.mult).then_inc(m_bv, 1)
            dve.wait_ge(m_g, 1)
            nc.vector.tensor_copy(g2[:], bank[2][0:L, 0:L].unsqueeze(1).broadcast_to([L, 2, L])).then_inc(m_g2, 1)
            dve.wait_ge(m_v, 1)
            for blk in range(4):
                last = nc.vector.tensor_copy(
                    vts[:, 4 * blk:4 * blk + 4].rearrange("p g b r t -> p b g t r"),
                    bank[3][:, blk * P:(blk + 1) * P].rearrange("p (b g t r) -> p b g t r", b=2, g=4, t=GT))
            last.then_inc(m_vt, 1)
            dve.wait_ge(m_cv, 1)
            nc.vector.tensor_tensor(cvec[:], bank[1][:, 0:D], bo_bc[:], ALU.add)

            dve.wait_ge(s_c2, 16 * NC2)
            dve.wait_ge(m_vm, 1)
            for i in range(2):
                nc.vector.tensor_copy(
                    vm[:, i, :, :, :, L:].rearrange("p b r h w -> p (b r) h w"),
                    K["dmask"][:].unsqueeze(1).broadcast_to([P, 2 * GB, 4, H // 2]))
            for hp in range(4):
                nc.vector.tensor_tensor(K["bqm"][:, hp:hp + 1], cols[:, C_BQ:C_BQ + 1],
                                        cols[:, C_MQ + hp:C_MQ + hp + 1], ALU.mult)
            for h2 in range(2):
                nc.vector.tensor_tensor(K["bqm"][:, 4 + h2:5 + h2], cols[:, C_BK:C_BK + 1],
                                        cols[:, C_MK + h2:C_MK + h2 + 1], ALU.mult)

            links = [0]

            def link(ins):
                links[0] += 1
                ins.then_inc(m_link, 1)
                dve.wait_ge(m_link, links[0])

            dve.wait_ge(m_cor, 1)
            link(nc.vector.tensor_scalar(cor[:], bank[0][:, 0:L], 1.0 / (B * DQ), None, ALU.mult))
            link(nc.vector.max(top[:, 0:8], cor[:]))
            link(nc.vector.match_replace(c2[:], top[:, 0:8], cor[:], NEG))
            link(nc.vector.max(top[:, 8:16], c2[:]))
            link(nc.vector.memset(top[:, K_TOP:16], NEG))
            link(nc.vector.tensor_scalar(nmax[:], top[:, 0:1], -1.0, None, ALU.mult))
            link(nc.vector.match_replace(c3[:], top[:, 8:16], c2[:], NEG))
            link(nc.vector.tensor_tensor(c2[:], c3[:], cor[:], ALU.is_lt))
            dve.wait_ge(m_ex, 1)
            link(nc.vector.tensor_tensor(wsh[:], ew[:], c2[:], ALU.mult))
            link(nc.vector.tensor_reduce(wsum[:, 0:1], wsh[:], AX.X, ALU.add))
            link(nc.vector.reciprocal(wsum[:, 1:2], wsum[:, 0:1]))
            nc.vector.tensor_scalar(wrow[:], wsh[:].unsqueeze(1).broadcast_to([P, 2, L]), wsum[:, 1:2], None,
                                    ALU.mult).then_inc(m_w, 1)
            dve.wait_ge(m_m2, 1)
            nc.vector.tensor_copy(m2[:], bank[0][:, P:2 * P]).then_inc(m_mm, 1)
            dve.wait_ge(m_ar, 1)
            nc.vector.tensor_tensor(xa[:], bank[2][:].rearrange("p (k d) -> p k d", k=4),
                                    K["bout"][:].unsqueeze(1).broadcast_to([P, 4, D]), ALU.add).then_inc(m_xa, 1)


def attention(K, scope, cvec, wo, vm):
    nc, a, bank, pair, cols, ident = K["nc"], K["a"], K["bank"], K["pair"], K["cols"], K["ident"]
    x3, xh2, xt_dram, logits, sem = K["x3"], K["xh2"], K["xt_dram"], K["logits"], K["sem"]

    def sb(name, shape, dt=F32):
        return K["sb"](name, shape, dt, scope)

    wqk, wv, gc, identb, msel, dspread, blank, bqm, xin = (
        K[n] for n in "wqk wv gc identb msel dspread blank bqm xin".split())
    x2 = sb("x2", [P, 2, GT, D])
    x1 = sb("x1", [P, 2, GT, D])
    xh = sb("xh", [P, 2, GT, D])
    xag = sb("xag", [P, 2, GT, D])
    xnT = sb("xnT", [P, 2, GT * P])
    qm = sb("qm", [P, 2, GB, 4, L])
    km = sb("km", [P, 2, GB, 2, L])
    qmb = sb("qmb", [P, 2, GB, 4, L], BF16)
    kmb = sb("kmb", [P, 2, GB, 2, L], BF16)
    pt = sb("pt", [P, 2, 2, 2, 4 * L])
    rd = sb("rd", [P, 2, P])
    ctxT = sb("ctxT", [P, 2, GT * P])
    mx = sb("mx", [P, 2, 16])
    mhl = sb("mhl", [P, 2, 32], BF16)
    mT = sb("mT", [32, 2, P], BF16)
    st6 = sb("st6a", [P, GT, 6])
    mv = sb("mva", [P, 2, GT, 2])
    st6b = sb("st6b", [P, GT, 6])
    mvb = sb("mvb", [P, GT, 2])
    rsb = sb("rsb", [P, GT])
    veb = sb("veb", [P, GT])
    pw = sb("pw", [P, 5, GT])
    rs = sb("rs", [P, 2, GT])
    r2 = sb("r2", [P, 2, GT])
    nhalf = sb("nhalf", [P, GT])
    eps = sb("eps", [P, GT])
    idle = sb("idle", [P, 2])
    x2nT = sb("x2nT", [P, 2, GT * P])
    xh2s = sb("xh2s", [P, 2, GT, D])
    dn = sb("dn", [H // 2, 2, 2 * P])

    g0, g1 = bank[0], bank[1]
    sbank = [bank[2], bank[3]]
    cd = bank[4]
    mps = bank[5][:, 0:P // 2].bitcast(BF16)
    lps = g0[:, 0:GT * (E + 2)]

    s_xi, s_z = K["s_xi"], sem("s_z")
    s_xt, s_x2, s_xa = ([sem(f"{n}{i}") for i in range(2)] for n in ("s_xt", "s_x2", "s_xa"))
    xa_src = K["xa_dram"].rearrange("(g b r t) d -> g b r (t d)", b=2, r=4, t=GT)
    x2_dst = K["x2_dram"].rearrange("(t p) d -> p t d", p=P)
    (t_b, t_q, t_k, t_v, t_o, t_b2, t_l) = (sem("t_" + n) for n in "b q k v o b2 l".split())
    t_s, t_m, t_st, t_pv, t_dn = (sem(n) for n in ("t_s", "t_m", "t_st", "t_pv", "t_dn"))
    e_qm, e_km, e_xh, e_x2n, e_dn, e_exp, e_mt = (
        sem("e_" + n) for n in "qm km xh x2n dn exp mt".split())
    (d_c, d_max, d_mhi, d_mh, d_rd, d_ctx, d_xnT, d_qb, d_vm, d_x3, d_bsb, d_stb, d_xh2, d_bs, d_st,
     d_x1, d_lg) = (sem("d_" + n) for n in
                    "c max mhi mh rd ctx xnT qb vm x3 bsb stb xh2 bs st x1 lg".split())
    p_x2, p_c, p_b, p_rsb, p_r, p_x3, p_xh2 = (sem("p_" + n) for n in "x2 c b rsb r x3 xh2".split())
    NZ = SLOTS // GT
    z_dst = K["xs_dram"].rearrange("(t p) d -> p t d", p=P)
    LO, HI = 4, NG - 2
    FIRST, LAST = -2, NG + 1
    x_src = a["x"].rearrange("(t p) d -> p t d", p=P)

    with nc.Block() as block:
        @block.sync
        def _(sp):
            def rows(g, buf):
                for b in range(2):
                    src = xa_src[bass.ds(g, 1), b].rearrange("o r c -> (o r) c")
                    sp.dma_start(xag[b * L:(b + 1) * L, buf].rearrange("p t d -> p (t d)"),
                                 src.unsqueeze(0).broadcast_to([L // 4, 4, GT * D])).then_inc(s_xa[buf], 16)
            rows(0, 0)
            rows(1, 1)

            def step(g, par):
                if valid(g + 3) and not (isinstance(g, int) and g < -1):
                    wait(sp, p_x2, g + 2)
                    sp.dma_start(xin[:, 1 - par], x_src[:, bass.ds((g + 3) * GT, GT), :]).then_inc(s_xi[1 - par], 16)
                    rows(g + 3, 1 - par)
                if valid(g + 2):
                    wait(sp, p_x2, g + 3)
                    sp.dma_start(x2_dst[:, bass.ds((g + 2) * GT, GT), :], x2[:, par]).then_inc(s_x2[par], 16)
                if valid(g - 2):
                    wait(sp, e_x2n, g - 1)
                    sp.dma_start(xt_dram[bass.ds(g - 2, 1)].rearrange("g p c -> p (g c)"),
                                 x2nT[:, par]).then_inc(s_xt[par], 16)
                if valid(g + 2, NZ):
                    sp.dma_start(z_dst[:, bass.ds((g + 2) * GT, GT), :], blank[:]).then_inc(s_z, 16)
            sp.dma_start(K["out"][B * L:, :].rearrange("(t p) d -> p t d", p=P), blank[:, :, 0:D]).then_inc(s_z, 16)
            for dst, src in ((K["rw1"][:], a["rw1"]), (K["rw2"][:], a["rw2"]),
                             (K["rb2"][:], a["rb2"].partition_broadcast(P)),
                             (K["prio"][:], a["prio"].partition_broadcast(P)), (K["triu"][:].bitcast(U16), a["triu"]),
                             (K["oneb"][:].bitcast(U16), a["oneb"]), (K["jrow"][:], a["jrow"]),
                             (K["token"][:], a["token"])):
                sp.dma_start(dst, src).then_inc(K["s_r"], 16)
            groups(sp, step, -3, LAST, LO, NG - 4)
            for i in range(2):
                sp.wait_ge(s_xt[i], 8 * NG)
                sp.wait_ge(s_x2[i], 8 * NG)
            sp.wait_ge(s_z, 16 * (NZ + 1))
            sp.wait_ge(K["s_r"], 16 * NR)

        @block.gpsimd
        def _(pool):
            pool.wait_ge(d_c, 1)
            cvec_bc = cvec[:].unsqueeze(1).broadcast_to([P, GT, D])

            def step(g, par):
                o = 1 - par
                if valid(g + 2):
                    wait(pool, s_xi[par], nth(g + 2, par), 16 * NG)
                    wait(pool, s_xa[par], 2 * nth(g + 2, par), 32 * NG)
                    wait(pool, d_x1, g + 1)
                    wait(pool, s_x2[par], nth(g, par), 16 * NG)
                    pool.tensor_tensor(x2[:, par], xin[:, par], xag[:, par], ALU.add).then_inc(p_x2, 1)
                if valid(g + 2):
                    wait(pool, d_st, g + 3)
                    wait(pool, d_x1, g + 1)
                    wait(pool, e_xh, g + 1)
                    n = (g + 2) * 5
                    pool.tensor_tensor(pw[:, 0], mv[:, par, :, 1], eps[:], ALU.add).then_inc(p_c, 1)
                    wait(pool, p_c, n + 1, 5 * NG)
                    pool.tensor_tensor(rs[:, par], pw[:, 0], nhalf[:], ALU.pow).then_inc(p_c, 1)
                    wait(pool, p_c, n + 2, 5 * NG)
                    pool.tensor_tensor(pw[:, 1], rs[:, par], rs[:, par], ALU.mult).then_inc(p_c, 1)
                    wait(pool, p_c, n + 3, 5 * NG)
                    pool.tensor_tensor(pw[:, 2], pw[:, 1], mv[:, par, :, 1], ALU.mult).then_inc(p_c, 1)
                    wait(pool, p_c, n + 4, 5 * NG)
                    pool.tensor_tensor(pw[:, 3], pw[:, 2], eps[:], ALU.add).then_inc(p_c, 1)
                    wait(pool, p_c, n + 5, 5 * NG)
                    pool.tensor_tensor(r2[:, par], pw[:, 3], nhalf[:], ALU.pow).then_inc(p_r, 1)
                if valid(g - 1):
                    wait(pool, d_stb, g)
                    wait(pool, d_xh2, g - 1)
                    pool.tensor_tensor(veb[:], mvb[:, :, 1], eps[:], ALU.add).then_inc(p_b, 1)
                    wait(pool, p_b, g)
                    pool.tensor_tensor(rsb[:], veb[:], nhalf[:], ALU.pow).then_inc(p_rsb, 1)
                if valid(g + 2):
                    wait(pool, d_x1, g + 3)
                    pool.tensor_tensor(x3[:, bass.ds((g + 2) * GT, GT), :], x1[:, par], cvec_bc,
                                       ALU.add).then_inc(p_x3, 1)
                if valid(g - 1):
                    wait(pool, d_xh2, g)
                    pool.tensor_copy(xh2[:, bass.ds((g - 1) * GT, GT), 0:D], xh2s[:, o]).then_inc(p_xh2, 1)
            groups(pool, step, FIRST, LAST, LO, HI)

        @block.scalar
        def _(act):
            def xpose_max(T, t):
                if valid(T + 2, NT):
                    q = t % 2
                    wait(act, t_m, T + 3, NT)
                    wait(act, t_st, T + 1, NT)
                    nc.scalar.copy(mT[:, q], mps[0:32, :]).then_inc(e_mt, 1)

            def step(g, par):
                o = 1 - par
                for t in range(GT):
                    T = g * GT + t
                    if valid(T + 1, NT):
                        q = (t + 1) % 2
                        wait(act, t_st, T + 2, NT)
                        wait(act, t_pv, T, NT)
                        nc.scalar.activation(pt[:, q].rearrange("p r b c -> p (r b c)"),
                                             pair[:].rearrange("p r c -> p (r c)"), ACT.Exp).then_inc(e_exp, 1)
                    if t == 1 and valid(g + 1):
                        wait(act, t_k, g + 2)
                        wait(act, t_st, g * GT, NT)
                        wait(act, d_qb, g)
                        for h2 in range(2):
                            last = nc.scalar.activation(
                                km[:, o, :, h2], g1[:].rearrange("p (b k) -> p b k", b=GB), ACT.Identity,
                                bias=bqm[:, 4 + h2:5 + h2], scale=cols[:, C_MK + h2:C_MK + h2 + 1])
                        last.then_inc(e_km, 1)
                    if t == 3 and valid(g - 2):
                        wait(act, t_b2, g - 1)
                        wait(act, t_l, g - 3)
                        wait(act, s_xt[par], nth(g - 4, par), 16 * NG)
                        nc.scalar.activation(x2nT[:, par], g1[:], ACT.Identity,
                                             bias=cols[:, C_B2:C_B2 + 1],
                                             scale=cols[:, C_G2:C_G2 + 1]).then_inc(e_x2n, 1)
                    if valid(T, NT):
                        wait(act, t_pv, T + 1, NT)
                        wait(act, t_dn, T - 1, NT)
                        nc.scalar.copy(dn[:, t % 2], cd[L:VW, 0:2 * P]).then_inc(e_dn, 1)
                    xpose_max(T, t)
                    if t == 0 and valid(g + 1):
                        wait(act, t_q, g + 2)
                        wait(act, t_st, g * GT, NT)
                        wait(act, d_qb, g)
                        for hp in range(4):
                            last = nc.scalar.activation(
                                qm[:, o, :, hp], g0[:].rearrange("p (b q) -> p b q", b=GB), ACT.Identity,
                                bias=bqm[:, hp:hp + 1], scale=cols[:, C_MQ + hp:C_MQ + hp + 1])
                        last.then_inc(e_qm, 1)
                    if t == 3 and valid(g + 2):
                        wait(act, p_r, g + 3)
                        wait(act, d_x1, g + 3)
                        wait(act, t_b, g + 1)
                        for i in range(GT):
                            last = nc.scalar.activation(xh[:, par, i], x1[:, par, i], ACT.Copy,
                                                        scale=r2[:, par, i:i + 1])
                        last.then_inc(e_xh, 1)
            groups(act, step, FIRST, LAST, LO, HI)

        @block.vector
        def _(dve):
            nc.vector.memset(nhalf[:], -0.5)
            nc.vector.memset(eps[:], EPS).then_inc(d_c, 1)
            dve.wait_ge(d_c, 1)

            def maxima(T, t):
                if valid(T + 2, NT):
                    q = t % 2
                    wait(dve, t_s, T + 3, NT)
                    for r in range(2):
                        last = nc.vector.tensor_reduce(mx[:, q, 8 * r:8 * r + 8],
                                                       sbank[r][:].rearrange("p (n k) -> p n k", k=L), AX.X, ALU.max)
                    last.then_inc(d_max, 1)
                    wait(dve, d_max, T + 3, NT)
                    wait(dve, t_m, T + 1, NT)
                    nc.vector.tensor_scalar(mhl[:, q, 0:16], mx[:, q], -1.0, None, ALU.mult).then_inc(d_mhi, 1)
                    wait(dve, d_mhi, T + 3, NT)
                    nc.vector.scalar_tensor_tensor(mhl[:, q, 16:32], mx[:, q], -1.0, mhl[:, q, 0:16],
                                                   ALU.mult, ALU.subtract).then_inc(d_mh, 1)

            def keep_logits(m):
                wait(dve, t_l, m + 1)
                nc.vector.tensor_copy(logits[:, bass.ds(m * GT, GT), :],
                                      lps.rearrange("p (t e) -> p t e", t=GT)).then_inc(d_lg, 1)

            def normalise(g, T, t, par):
                if valid(T, NT):
                    q = t % 2
                    wait(dve, t_dn, T + 1, NT)
                    nc.vector.reciprocal(rd[:, q], cd[:, 2 * P:3 * P]).then_inc(d_rd, 1)
                    wait(dve, d_rd, T + 1, NT)
                    if t == 0:
                        wait(dve, t_o, g - 1)
                    for r in range(2):
                        rows = slice(r * L, (r + 1) * L)
                        last = nc.vector.tensor_tensor(ctxT[rows, par, t * P:(t + 1) * P],
                                                       cd[0:L, r * P:(r + 1) * P], rd[rows, q], ALU.mult)
                    last.then_inc(d_ctx, 1)

            def step(g, par):
                o = 1 - par
                for t in range(GT):
                    T = g * GT + t
                    maxima(T, t)
                    if t == 0:
                        if valid(g + 1):
                            wait(dve, t_b, g + 2)
                            wait(dve, t_v, g)
                            nc.vector.tensor_scalar(xnT[:, o], g1[:], cols[:, C_G1:C_G1 + 1],
                                                    cols[:, C_B1:C_B1 + 1], ALU.mult, ALU.add).then_inc(d_xnT, 1)
                    if t == 1 and valid(g + 1):
                        wait(dve, e_qm, g + 2)
                        wait(dve, t_s, g * GT, NT)
                        nc.vector.tensor_copy(qmb[:, o].rearrange("p b h q -> p (b h q)"),
                                              qm[:, o].rearrange("p b h q -> p (b h q)"))
                        wait(dve, e_km, g + 2)
                        nc.vector.tensor_copy(kmb[:, o].rearrange("p b h k -> p (b h k)"),
                                              km[:, o].rearrange("p b h k -> p (b h k)")).then_inc(d_qb, 1)
                    if t == 3 and valid(g + 2):
                        wait(dve, p_c, (g + 2) * 5 + 2, 5 * NG)
                        wait(dve, e_xh, g + 1)
                        wait(dve, p_x3, g + 1)
                        for i in range(GT):
                            last = nc.vector.tensor_scalar(x1[:, par, i], x2[:, par, i], mv[:, par, i, 0:1],
                                                           rs[:, par, i:i + 1], ALU.subtract, ALU.mult)
                        last.then_inc(d_x1, 1)
                    normalise(g, T, t, par)
                    if t == 0 and valid(g + 2):
                        wait(dve, p_x2, g + 3)
                        settle(nc.vector, idle[:, 1:2])
                        for i in range(GT):
                            last = nc.vector.bn_stats(st6[:, i], x2[:, par, i])
                        last.then_inc(d_bs, 1)
                        wait(dve, d_bs, g + 3)
                        wait(dve, p_r, g + 1)
                        settle(nc.vector, idle[:, 1:2])
                        for i in range(GT):
                            last = nc.vector.bn_aggr(mv[:, par, i], st6[:, i])
                        last.then_inc(d_st, 1)
                    if t == 2 and valid(g - 1):
                        wait(dve, t_o, g)
                        wait(dve, p_x3, g)
                        xg = x3[:, bass.ds((g - 1) * GT, GT), :]
                        nc.vector.tensor_tensor(xg, xg, g1[:].rearrange("p (t d) -> p t d", t=GT),
                                                ALU.add).then_inc(d_x3, 1)
                        wait(dve, d_x3, g)
                        settle(nc.vector, idle[:, 0:1])
                        for i in range(GT):
                            last = nc.vector.bn_stats(st6b[:, i], x3[:, (g - 1) * GT + i, :])
                        last.then_inc(d_bsb, 1)
                        wait(dve, d_bsb, g)
                        settle(nc.vector, idle[:, 0:1])
                        for i in range(GT):
                            last = nc.vector.bn_aggr(mvb[:, i], st6b[:, i])
                        last.then_inc(d_stb, 1)
                    if t == 1 and valid(g + 1):
                        wait(dve, t_v, g + 2)
                        wait(dve, t_pv, g * GT, NT)
                        apart = (VW + 2 * DH) // DH
                        for h2 in range(2):
                            for b2 in range(2):
                                dst = vm[h2 * L:(h2 + 1) * L, o].rearrange(
                                    "p (t b) r h (s d) -> p b t r (h s) d", b=2, d=DH)[:, b2]
                                last = nc.vector.tensor_copy(
                                    dst[:, :, :, h2:h2 + 3 * apart + 1:apart],
                                    g0[b2 * L:(b2 + 1) * L].rearrange("p (t r h e d) -> p e t r h d", t=GT, r=2, e=2,
                                                                      d=DH)[:, h2])
                        last.then_inc(d_vm, 1)
                    if t == 3 and valid(g - 1):
                        wait(dve, p_rsb, g)
                        wait(dve, t_b2, g - 2)
                        wait(dve, p_xh2, g - 2)
                        for i in range(GT):
                            last = nc.vector.tensor_scalar(xh2s[:, o, i], x3[:, (g - 1) * GT + i, :],
                                                           mvb[:, i, 0:1], rsb[:, i:i + 1], ALU.subtract, ALU.mult)
                        last.then_inc(d_xh2, 1)
                    if t == 3 and valid(g - 3, NG - 2):
                        keep_logits(g - 3)
                    if t == 3 and isinstance(g, int) and g - 2 in (NG - 2, NG - 1):
                        keep_logits(g - 2)
            groups(dve, step, FIRST, LAST, LO, HI)

        @block.tensor
        def _(pe):
            def scores_q(T, t, qpar):
                if valid(T + 2, NT):
                    wait(pe, d_max, T + 2, NT)
                    lb = (t + 2) % GT * 2
                    for b in range(2):
                        for hh in range(2):
                            for r in range(2):
                                rows = slice(r * L, (r + 1) * L)
                                c = (b * 2 + hh) * P
                                last = nc.tensor.matmul(
                                    sbank[r][:, c:c + P],
                                    qmb[rows, qpar, lb + b, 2 * hh:2 * hh + 2].rearrange("p h q -> p (h q)"),
                                    kmb[rows, qpar, lb + b].rearrange("p h k -> p (h k)"),
                                    start=True, stop=True)
                    last.then_inc(t_s, 1)

            def scores_k(T, t, kpar):
                if valid(T + 1, NT):
                    q = (t + 1) % 2
                    wait(pe, e_exp, T + 1, NT)
                    lb = (t + 1) % GT * 2
                    for b in range(2):
                        for r in range(2):
                            rows = slice(r * L, (r + 1) * L)
                            nc.tensor.matmul(
                                pair[:, r, b * 4 * L:(b + 1) * 4 * L],
                                km[rows, kpar, lb + b].rearrange("p h k -> p (h k)"),
                                qm[rows, kpar, lb + b].rearrange("p h q -> p (h q)"),
                                start=(b == 0), stop=False, skip_group_check=True)
                    wait(pe, e_mt, T + 2, NT)
                    for r in range(2):
                        for b in range(2):
                            for hh in range(2):
                                n = (r * 2 + b) * 2 + hh
                                c = (b * 2 + hh) * P
                                last = nc.tensor.matmul(pair[:, r, c:c + P], msel[:, n], mT[:, q],
                                                        start=False, stop=(b == 1 and hh == 1),
                                                        skip_group_check=True)
                    last.then_inc(t_st, 1)

            def weighted(g, T, t, par):
                if valid(T, NT):
                    q = t % 2
                    wait(pe, e_exp, T + 1, NT)
                    if t == 0:
                        wait(pe, d_vm, g + 1)
                    wait(pe, d_ctx, T, NT)
                    for r in range(2):
                        for b in range(2):
                            for hp in range(4):
                                last = nc.tensor.matmul(
                                    cd[0:VW, (r * 2 + b) * L:(r * 2 + b + 1) * L], vm[:, par, t * 2 + b, r, hp],
                                    pt[:, q, r, b, hp * L:(hp + 1) * L], start=(hp == 0), stop=(hp == 3))
                    last.then_inc(t_pv, 1)

            def route(m, buf, g):
                wait(pe, e_x2n, m + 1)
                wait(pe, d_vm, g + 2)
                wait(pe, d_lg, m)
                for i in range(GT):
                    last = nc.tensor.matmul(lps[:, i * (E + 2):(i + 1) * (E + 2)],
                                            x2nT[:, buf, i * P:(i + 1) * P], gc[:], start=True, stop=True)
                last.then_inc(t_l, 1)

            def spread_den(T, t):
                if valid(T, NT):
                    wait(pe, e_dn, T + 1, NT)
                    for r in range(2):
                        last = nc.tensor.matmul(cd[r * L:(r + 1) * L, 2 * P:3 * P], dspread[:],
                                                dn[:, t % 2, r * P:(r + 1) * P], start=True, stop=True)
                    last.then_inc(t_dn, 1)

            def xpose_max(T, t):
                if valid(T + 2, NT):
                    q = t % 2
                    wait(pe, d_mh, T + 3, NT)
                    wait(pe, e_mt, T + 2, NT)
                    nc.tensor.transpose(mps[0:32, :], mhl[:, q], identb[:]).then_inc(t_m, 1)

            def step(g, par):
                o = 1 - par
                for t in range(GT):
                    T = g * GT + t
                    scores_k(T, t, par if t < 3 else o)
                    if t == 2 and valid(g + 1):
                        wait(pe, d_qb, g + 2)
                    scores_q(T, t, par if t < 2 else o)
                    if t == 0 and valid(g + 1):
                        wait(pe, e_xh, g + 2)
                        wait(pe, e_x2n, g - 2)
                        for i in range(GT):
                            last = nc.tensor.transpose(g1[:, i * P:(i + 1) * P], xh[:, o, i], ident[:])
                        last.then_inc(t_b, 1)
                    if t == 1 and valid(g + 1):
                        nc.tensor.matmul(g1[:], wqk[:, D:2 * D], xnT[:, o], start=True, stop=True).then_inc(t_k, 1)
                    if t == 3 and valid(g - 2):
                        wait(pe, d_xh2, g - 1)
                        wait(pe, d_x3, g)
                        for i in range(GT):
                            last = nc.tensor.transpose(g1[:, i * P:(i + 1) * P], xh2s[:, par, i], ident[:])
                        last.then_inc(t_b2, 1)
                    weighted(g, T, t, par)
                    xpose_max(T, t)
                    if t == 0 and valid(g + 1):
                        wait(pe, d_xnT, g + 2)
                        wait(pe, d_vm, g + 1)
                        wait(pe, d_lg, g - 3)
                        nc.tensor.matmul(g0[:], wqk[:, 0:D], xnT[:, o], start=True, stop=True).then_inc(t_q, 1)
                    if t == 1 and valid(g + 1):
                        wait(pe, e_qm, g + 2)
                        for i in range(GT):
                            last = nc.tensor.matmul(g0[:, i * P:(i + 1) * P], xnT[:, o, i * P:(i + 1) * P], wv[:],
                                                    start=True, stop=True)
                        last.then_inc(t_v, 1)
                    if t == 2 and valid(g - 1):
                        wait(pe, d_ctx, g * GT, NT)
                        wait(pe, e_km, g + 2)
                        for i in range(GT):
                            last = nc.tensor.matmul(g1[:, i * P:(i + 1) * P], ctxT[:, o, i * P:(i + 1) * P], wo[:],
                                                    start=True, stop=True)
                        last.then_inc(t_o, 1)
                    if t == 3 and valid(g - 3, NG - 2):
                        route(g - 3, o, g)
                    if t == 3 and isinstance(g, int) and g - 2 in (NG - 2, NG - 1):
                        route(g - 2, par, g)
                    spread_den(T, t)
            groups(pe, step, FIRST, LAST, LO, HI)


def experts(K, scope):
    nc, a, out, bank, pair, cols, ident = (K[n] for n in "nc a out bank pair cols ident".split())
    x3, xh2, xt_dram, logits, sem, xs_dram = K["x3"], K["xh2"], K["xt_dram"], K["logits"], K["sem"], K["xs_dram"]

    def sb(name, shape, dt=F32):
        return K["sb"](name, shape, dt, scope)

    rw1, rw2, rb2, prio, triu, oneb, jrow, token = (K[n] for n in "rw1 rw2 rb2 prio triu oneb jrow token".split())
    w1 = sb("w1", [P, E, W1W])
    w2 = sb("w2", [P, E, FC * D])
    c1 = sb("c1", [P, NT])
    c0g = sb("c0g", [P, NT])
    slot = sb("slot", [P, NT], I32)
    eid = sb("eid", [1, SLOTS], I32)
    dif = sb("dif", [P, NT, E])
    ex = sb("ex", [P, NT, E])
    oh = sb("oh", [P, NT, E])
    ohb = sb("ohb", [P, NT, E], BF16)
    tmp = sb("tmp", [P, NT, E])
    cum = [sb(f"cum{i}", [P, NT + 1, E]) for i in range(2)]
    cumb = sb("cumb", [P, NT + 1, E], BF16)
    r1 = sb("r1", [P, NT])
    r2 = sb("r2r", [P, NT])
    gate = sb("gate", [P, NT])
    cl = sb("cl", [P, NT, 2])
    ec = sb("ec", [P, NT, 2])
    small = sb("small", [P, 8, E])
    smalli = sb("smalli", [P, 2, E], I32)
    cmp = sb("cmp", [1, SLOTS, E])
    er = sb("er", [1, SLOTS])
    hs = sb("hs", [P, 2, FC, GT * P])
    x2g = sb("x2g", [P, IB, GT, D])
    tmp2 = sb("tmp2", [P, GT, D])
    xg = sb("xg", [P, IB, GT * P])
    rw1h, rw1l = sb("rw1h", [P, FF], F32R), sb("rw1l", [P, FF], F32R)
    xgh, xgl = sb("xgh", [P, 2, GT * P], F32R), sb("xgl", [P, 2, GT * P], F32R)
    xsl = sb("xsl", [P, IB, 2, XW])
    xsT = sb("xsT", [P, 2, 2 * P])
    w1b = sb("w1b", [P, YB, W1W])
    hT = sb("hT", [P, 2, FC, P])
    weight = sb("weight", [P, YB])
    number = sb("number", [P, YB], I32)
    yb2 = sb("yb2", [P, 2, D])
    ysb = sb("ysb", [P, YB, D])

    hbank = [bank[0][:], bank[1][:], pair[:, 0], pair[:, 1]]
    rbank = [bank[2], bank[3]]
    rankb, totb = bank[4], bank[5]
    xbank = bank[0]
    s_w, s_sc, s_base = sem("s_w"), sem("s_sc"), sem("s_base")
    r_d, r_e, r_ec, r_oh, r_cum, r_rank, d_idx = (sem("r_" + n) for n in "d e ec oh cum rank idx".split())
    s_xr, s_xg, s_xs = ([sem(f"{n}{i}") for i in range(IB)] for n in "s_xr s_xg s_xs".split())
    s_acc = [sem(f"s_acc{i}") for i in range(YB)]
    f_l1, f_ge, f_l2, f_r, f_x3, f_a, f_h, f_s = (sem("f_" + n) for n in "l1 ge l2 r x3 a h s".split())
    x_tr, x_xt, x_meta, x_w1, x_l1, x_ge, x_l2, x_b2, x_y = (
        sem("x_" + n) for n in "tr xt meta w1 l1 ge l2 b2 y".split())
    NW = 5
    NU = SLOTS // 2
    out_v = out[0:B * L, :].rearrange("(t p) d -> p t d", p=P)
    x2_v = K["x2_dram"].rearrange("(t p) d -> p t d", p=P)
    xs_v = xs_dram.rearrange("(t p) d -> p t d", p=P)

    def per_tile(v):
        return v[:].unsqueeze(2).broadcast_to([P, NT, E])

    with nc.Block() as block:
        @block.sync
        def _(sp):
            def load(g, buf):
                wait(sp, f_l1, FC * (g - IB + 1), FC * NG)
                sp.dma_start(xg[:, buf], xt_dram[bass.ds(g, 1)].rearrange("g p c -> p (g c)")).then_inc(s_xg[buf], 16)
                wait(sp, f_a, g - IB + 1)
                sp.dma_start(x2g[:, buf], x2_v[:, bass.ds(g * GT, GT), :]).then_inc(s_xr[buf], 16)

            def base(g):
                wait(sp, f_x3, g + 1)
                sp.dma_start(out_v[:, bass.ds(g * GT, GT), :], x3[:, bass.ds(g * GT, GT), :]).then_inc(s_base, 16)

            load(0, 0)
            for g in range(1, IB):
                load(g, g)
            sp.dma_start(w1[:, :, FF + FC:], bass.AP(a["b2"].tensor, 0, [[0, P], [D, E], [1, D]])).then_inc(s_w, 16)
            for h in range(2):
                half = slice(h * E // 2, (h + 1) * E // 2)
                sp.dma_start(w1[:, half, 0:FF + FC], a["w1"][:, half]).then_inc(s_w, 16)
                sp.dma_start(w2[:, half], a["w2"][:, half]).then_inc(s_w, 16)

            def ahead(g, buf):
                load(g, buf)
                base(g - IB)
            groups(sp, ahead, IB, NG - 1, IB, NG, IB)
            for g in range(NG - IB, NG - 2):
                base(g)
            sp.wait_ge(s_sc, 16 * NT)

            def slots(u, buf):
                wait(sp, x_tr, u - IB + 1, NU)
                wait(sp, x_meta, u - IB + 1, NU)
                sp.dma_start(xsl[:, buf], xs_v[:, bass.ds(u * 2, 2), :]).then_inc(s_xs[buf], 16)
            for u in range(IB):
                slots(u, u)
            for g in range(NG - 2, NG):
                base(g)
            groups(sp, slots, IB, NU - 1, IB, NU, IB)
            sp.wait_ge(s_base, 16 * NG)

        @block.gpsimd
        def _(pool):
            pool.wait_ge(d_idx, 1)
            for T in range(NT):
                pool.indirect_dma_start(xs_dram, bass.IndirectOffsetOnAxis(ap=slot[:, T:T + 1], axis=0),
                                        xh2[:, T], None).then_inc(s_sc, 16)
            pool.wait_ge(s_sc, 16 * NT)
            pool.wait_ge(s_base, 16 * NG)
            for v in range(SLOTS):
                pool.wait_ge(x_y, v + 1)
                pool.indirect_dma_start(out, bass.IndirectOffsetOnAxis(ap=number[:, v % YB:v % YB + 1], axis=0),
                                        ysb[:, v % YB], None, compute_op=ALU.add).then_inc(s_acc[v % YB], 16)
            for i in range(YB):
                pool.wait_ge(s_acc[i], 16 * (SLOTS // YB))

        @block.scalar
        def _(act):
            act.wait_ge(r_e, 1)
            nc.scalar.activation(ex[:].rearrange("p t e -> p (t e)"), dif[:].rearrange("p t e -> p (t e)"),
                                 ACT.Exp)
            nc.scalar.activation(ec[:].rearrange("p t e -> p (t e)"), cl[:].rearrange("p t e -> p (t e)"),
                                 ACT.Exp).then_inc(r_ec, 1)

            def shared(g, par):
                for j in range(FC):
                    wait(act, f_l2, g - 1)
                    wait(act, f_l1, FC * g + j + 1, FC * NG)
                    nc.scalar.activation(hs[:, par, j], hbank[j], ACT.Gelu,
                                         bias=cols[:, C_RB1 + j:C_RB1 + j + 1]).then_inc(f_ge, 1)
            groups(act, shared, 0, NG - 1, 2, NG)

            def step(u, par):
                for k in range(2):
                    v = u * 2 + k
                    wait(act, x_l1, v + 1, SLOTS)
                    wait(act, x_l2, v - 1, SLOTS)
                    for j in range(FC):
                        last = nc.scalar.activation(hT[:, k, j], pair[:, k, j * P:(j + 1) * P], ACT.Gelu,
                                                    bias=w1b[:, 2 * par + k, FF + j:FF + j + 1])
                    last.then_inc(x_ge, 1)
            groups(act, step, 0, NU - 1, 2, NU)

        @block.vector
        def _(dve):
            links = [0]

            def link(ins):
                links[0] += 1
                ins.then_inc(r_d, 1)
                dve.wait_ge(r_d, links[0])

            lg = logits[:, :, 0:E]
            nc.vector.tensor_reduce(r1[:], lg, AX.X, ALU.max)
            link(nc.vector.tensor_tensor(cl[:], logits[:, :, E:E + 2],
                                         K["coefb"][:].unsqueeze(1).broadcast_to([P, NT, 2]), ALU.add))
            nc.vector.tensor_tensor(dif[:], lg, per_tile(r1), ALU.subtract)
            link(nc.vector.tensor_reduce(r2[:], cl[:], AX.X, ALU.max))
            nc.vector.tensor_tensor(cl[:], cl[:], r2[:].unsqueeze(2).broadcast_to([P, NT, 2]),
                                    ALU.subtract).then_inc(r_e, 1)
            dve.wait_ge(r_e, 1)
            link(nc.vector.scalar_tensor_tensor(tmp[:], dif[:], 0.0,
                                                prio[:].unsqueeze(1).broadcast_to([P, NT, E]), ALU.is_ge, ALU.mult))
            link(nc.vector.tensor_reduce(r1[:], tmp[:], AX.X, ALU.max))
            link(nc.vector.tensor_tensor(oh[:], tmp[:], per_tile(r1), ALU.is_equal))
            nc.vector.tensor_copy(ohb[:], oh[:]).then_inc(r_oh, 1)
            nc.vector.memset(cum[0][:, 0], 0.0)
            nc.vector.memset(cum[1][:, 0], 0.0)
            link(nc.vector.tensor_copy(cum[0][:, 1:NT + 1], oh[:]))
            k, src, dst = 1, cum[0], cum[1]
            while k < NT:
                nc.vector.tensor_copy(dst[:, 1:k + 1], src[:, 1:k + 1])
                link(nc.vector.tensor_tensor(dst[:, k + 1:NT + 1], src[:, k + 1:NT + 1], src[:, 1:NT + 1 - k],
                                             ALU.add))
                k, src, dst = 2 * k, dst, src
            nc.vector.tensor_copy(cumb[:], src[:]).then_inc(r_cum, 1)
            dve.wait_ge(r_ec, 1)
            nc.vector.tensor_reduce(r1[:], ex[:], AX.X, ALU.add)
            link(nc.vector.tensor_reduce(r2[:], ec[:], AX.X, ALU.add))
            nc.vector.reciprocal(gate[:], r1[:])
            link(nc.vector.reciprocal(r2[:], r2[:]))
            nc.vector.tensor_tensor(c1[:], ec[:, :, 1], r2[:], ALU.mult)
            link(nc.vector.tensor_tensor(c0g[:], ec[:, :, 0], r2[:], ALU.mult))
            nc.vector.tensor_tensor(xh2[:, :, D], c0g[:], gate[:], ALU.mult)
            link(nc.vector.tensor_copy(xh2[:, :, D + 1], token[:]))

            rb2_bc = rb2[:].unsqueeze(1).broadcast_to([P, GT, D])

            def shared(g, buf):
                rows = x3[:, bass.ds(g * GT, GT), :]
                wait(dve, s_xr[buf], nth(g, buf, NG, IB), 16 * NG)
                nc.vector.tensor_tensor(rows, rows, x2g[:, buf], ALU.add).then_inc(f_a, 1)
                wait(dve, f_l2, g + 1)
                wait(dve, f_x3, g)
                nc.vector.tensor_tensor(tmp2[:], rbank[buf % 2][:].rearrange("p (t d) -> p t d", t=GT), rb2_bc,
                                        ALU.add).then_inc(f_r, 1)
                wait(dve, f_r, g + 1)
                wait(dve, f_a, g + 1)
                for i in range(GT):
                    T = g * GT + i
                    last = nc.vector.scalar_tensor_tensor(x3[:, T, :], tmp2[:, i], c1[:, bass.ds(T, 1)],
                                                          x3[:, T, :], ALU.mult, ALU.add)
                last.then_inc(f_x3, 1)

            def split(g, buf):
                par = buf % 2
                wait(dve, s_xg[buf], nth(g, buf, NG, IB), 16 * NG)
                wait(dve, f_l1, FC * (g - 1), FC * NG)
                nc.vector.tensor_copy(xgh[:, par], xg[:, buf]).then_inc(f_h, 1)
                wait(dve, f_h, g - 2, NG)
                nc.vector.tensor_tensor(xgl[:, par], xg[:, buf], xgh[:, par].bitcast(F32),
                                        ALU.subtract).then_inc(f_s, 1)
            shared(0, 0)
            nc.vector.tensor_copy(rw1h[:], rw1[:]).then_inc(f_h, 1)
            dve.wait_ge(f_h, 1)
            nc.vector.tensor_tensor(rw1l[:], rw1[:], rw1h[:].bitcast(F32), ALU.subtract).then_inc(f_s, 1)
            split(IB, 0)
            shared(1, 1)

            dve.wait_ge(r_rank, 1)
            link(nc.vector.tensor_scalar(smalli[:, 0], totb[:, 0:E], float(P - 1), None, ALU.add))
            link(nc.vector.tensor_scalar(smalli[:, 1], smalli[:, 0], 7, None, ALU.logical_shift_right))
            link(nc.vector.tensor_copy(small[:, 0], smalli[:, 1]))
            k, i = 1, 0
            while k < E:
                nc.vector.tensor_copy(small[:, i + 1, 0:k], small[:, i, 0:k])
                link(nc.vector.tensor_tensor(small[:, i + 1, k:E], small[:, i, k:E], small[:, i, 0:E - k], ALU.add))
                k, i = 2 * k, i + 1
            end = small[:, i]
            link(nc.vector.tensor_tensor(small[:, i + 1], end, small[:, 0], ALU.subtract))
            link(nc.vector.tensor_scalar(small[:, i + 2], small[:, i + 1], float(P), None, ALU.mult))
            link(nc.vector.tensor_tensor(tmp[:], rankb[:].rearrange("p (t e) -> p t e", e=E),
                                         small[:, i + 2].unsqueeze(1).broadcast_to([P, NT, E]), ALU.add))
            link(nc.vector.tensor_tensor(tmp[:], tmp[:], oh[:], ALU.mult))
            link(nc.vector.tensor_reduce(r1[:], tmp[:], AX.X, ALU.add))
            nc.vector.tensor_copy(slot[:], r1[:]).then_inc(d_idx, 1)
            link(nc.vector.tensor_tensor(cmp[:], jrow[:].unsqueeze(2).broadcast_to([1, SLOTS, E]),
                                         end[0:1].unsqueeze(1).broadcast_to([1, SLOTS, E]), ALU.is_ge))
            link(nc.vector.tensor_reduce(er[:], cmp[:], AX.X, ALU.add))
            nc.vector.tensor_scalar(eid[:], er[:], float(E - 1), None, ALU.min).then_inc(d_idx, 1)
            def ahead(g, buf):
                if not isinstance(g, int) or IB < g + 2 < NG:
                    split(g + 2, (buf + 2) % IB)
                shared(g, buf)
            groups(dve, ahead, 2, NG - 2, IB, NG - IB, IB)
            dve.wait_ge(s_w, 16 * NW)
            dve.wait_ge(d_idx, 2)

            def spread(u, par):
                wait(dve, x_tr, u + 1, NU)
                wait(dve, x_l1, 2 * (u - 1), SLOTS)
                nc.vector.tensor_scalar(xsT[:, par], xbank[:, 0:2 * P], cols[:, C_G2:C_G2 + 1],
                                        cols[:, C_B2:C_B2 + 1], ALU.mult, ALU.add).then_inc(x_xt, 1)

            def meta(u, buf, par):
                wait(dve, s_xs[buf], nth(u, buf, NU, IB), 16 * NU)
                wait(dve, x_y, 2 * (u - 1), SLOTS)
                nc.vector.tensor_copy(weight[:, 2 * par:2 * par + 2], xsl[:, buf, :, D])
                for k in range(2):
                    wait(dve, s_acc[2 * par + k], nth(u - 2, par, NU), 8 * NU)
                nc.vector.tensor_copy(number[:, 2 * par:2 * par + 2], xsl[:, buf, :, D + 1]).then_inc(x_meta, 1)

            def fetch(u, par, k):
                v = u * 2 + k
                e = dve.value_load(eid[0:1, bass.ds(v, 1)], min_val=0, max_val=E - 1)
                wait(dve, x_y, v - 3, SLOTS)
                wait(dve, x_ge, v - 3, SLOTS)
                nc.vector.tensor_copy(w1b[:, 2 * par + k], w1[:, e, :]).then_inc(x_w1, 1)

            def rows_out(v, par, k):
                i = 2 * par + k
                wait(dve, x_l2, v + 1, SLOTS)
                wait(dve, x_y, v - 1, SLOTS)
                nc.vector.tensor_tensor(yb2[:, k], bank[4 + k][:, 0:D], w1b[:, i, FF + FC:], ALU.add).then_inc(x_b2, 1)
                wait(dve, x_b2, v + 1, SLOTS)
                nc.vector.tensor_scalar(ysb[:, i], yb2[:, k], weight[:, i:i + 1], None, ALU.mult).then_inc(x_y, 1)

            def step(u, buf):
                par = buf % 2
                o = 1 - par
                if valid(u + 1, NU):
                    fetch(u + 1, o, 0)
                if valid(u, NU):
                    meta(u, buf, par)
                if valid(u - 1, NU):
                    rows_out(u * 2 - 1, o, 1)
                if valid(u + 1, NU):
                    spread(u + 1, o)
                if valid(u + 1, NU):
                    fetch(u + 1, o, 1)
                if valid(u, NU):
                    rows_out(u * 2, par, 0)
            step(-1, IB - 1)
            shared(NG - 1, IB - 1)
            groups(dve, step, 0, NU, IB, NU - IB, IB)

        @block.tensor
        def _(pe):
            def shared(g, buf):
                par = buf % 2
                if valid(g):
                    wait(pe, s_xg[buf], nth(g, buf, NG, IB), 16 * NG)
                    exact = isinstance(g, int) and g < IB
                    if not exact:
                        wait(pe, f_s, g - 2)
                    for j in range(FC):
                        wait(pe, f_ge, FC * (g - 1) + j + 1, FC * NG)
                        for n, (w, x) in enumerate(((rw1, xg[:, buf]),) if exact else
                                                   ((rw1h, xgh[:, par]), (rw1h, xgl[:, par]), (rw1l, xgh[:, par]))):
                            last = nc.tensor.matmul(hbank[j], w[:, j * P:(j + 1) * P], x,
                                                    start=(n == 0), stop=(exact or n == 2))
                        last.then_inc(f_l1, 1)
                if valid(g - 1):
                    wait(pe, f_ge, FC * g, FC * NG)
                    wait(pe, f_r, g - 2)
                    for i in range(GT):
                        for j in range(FC):
                            last = nc.tensor.matmul(rbank[1 - par][:, i * P:(i + 1) * P],
                                                    hs[:, 1 - par, j, i * P:(i + 1) * P], rw2[:, j],
                                                    start=(j == 0), stop=(j == FC - 1))
                    last.then_inc(f_l2, 1)

            def ranks():
                pe.wait_ge(r_oh, 1)
                pe.wait_ge(r_cum, 1)
                nc.tensor.matmul(rankb[:], triu[:], ohb[:].rearrange("p t e -> p (t e)"), start=True, stop=False)
                nc.tensor.matmul(rankb[:], oneb[:], cumb[:, 0:NT].rearrange("p t e -> p (t e)"),
                                 start=False, stop=True)
                nc.tensor.matmul(totb[:, 0:E], oneb[:], cumb[:, NT], start=True, stop=True).then_inc(r_rank, 1)

            def turn(u, buf):
                wait(pe, s_xs[buf], nth(u, buf, NU, IB), 16 * NU)
                wait(pe, x_xt, u, NU)
                for k in range(2):
                    last = nc.tensor.transpose(xbank[:, k * P:(k + 1) * P], xsl[:, buf, k, 0:D], ident[:])
                last.then_inc(x_tr, 1)

            for g in range(3):
                shared(g, g)
            ranks()
            shared(3, 3)
            groups(pe, shared, IB, NG - 1, IB, NG, IB)
            wait(pe, f_ge, FC * NG, FC * NG)
            turn(0, 0)
            shared(NG, 0)
            pe.wait_ge(s_w, 16 * NW)
            pe.wait_ge(d_idx, 2)

            def layer2(v, k):
                e = pe.value_load(eid[0:1, bass.ds(v, 1)], min_val=0, max_val=E - 1)
                wait(pe, x_ge, v + 1, SLOTS)
                wait(pe, x_b2, v - 1, SLOTS)
                for j in range(FC):
                    last = nc.tensor.matmul(bank[4 + k][:, 0:D], hT[:, k, j], w2[:, e, j * D:(j + 1) * D],
                                            start=(j == 0), stop=(j == FC - 1))
                last.then_inc(x_l2, 1)

            def step(u, buf):
                par = buf % 2
                for k in range(2):
                    v = u * 2 + k
                    if valid(u, NU):
                        if k == 0:
                            wait(pe, x_xt, u + 1, NU)
                        wait(pe, x_w1, v + 1, SLOTS)
                        wait(pe, x_ge, v - 1, SLOTS)
                        for j in range(FC):
                            last = nc.tensor.matmul(pair[:, k, j * P:(j + 1) * P],
                                                    w1b[:, 2 * par + k, j * P:(j + 1) * P],
                                                    xsT[:, par, k * P:(k + 1) * P], start=True, stop=True)
                        last.then_inc(x_l1, 1)
                    if k == 0 and valid(u + 1, NU):
                        turn(u + 1, (buf + 1) % IB)
                    if valid(v - 1, SLOTS):
                        layer2(v - 1, 1 - k)
            groups(pe, step, 0, NU, IB, NU - IB, IB)


_OUT = ((B, L, D), "float32")


def layouts(i):
    import numpy as np
    f = np.float32
    heads = np.arange(P) // DH
    rev = (L - np.arange(L)) % L
    mq = np.stack([((heads % 8) // 2 == hp) / np.sqrt(DH) for hp in range(4)], 1).astype(f)
    mk = np.stack([heads % 2 == h2 for h2 in range(2)], 1).astype(f)
    wqkv, bqkv = i["L0_ffn_Wqkv"], i["L0_ffn_bqkv"]
    msel = np.zeros((32, 8, 2, L), np.uint16)
    for n in range(8):
        for h2 in range(2):
            msel[2 * n + h2, n, h2] = BF16_ONE
            msel[16 + 2 * n + h2, n, h2] = BF16_ONE
    sel = np.zeros((16, DQ, 2, 16, 4), f)
    for r in range(4):
        for p in range(2):
            sel[np.arange(16), 2 * r + p, p, np.arange(16), r] = 1
    dmask = np.zeros((2, L, 4, 4, 2), f)
    for hp in range(4):
        for h2 in range(2):
            dmask[h2, :, hp, hp, h2] = 1
    blank = np.zeros((P, GT, XW), f)
    blank[:, :, D + 1] = B * L + np.arange(YB)[None, :] * P + np.arange(P)[:, None]
    w1 = i["L0_ffn_W1"].transpose(1, 0, 2)
    b1 = i["L0_ffn_b1"].reshape(E, FC, P).transpose(2, 0, 1)
    return {
        "x": i["x"].reshape(B * L, D),
        "ctx": i["ctx_1024"].reshape(B * L, D),
        "wq8": i["L0_xattn_Wq"],
        "wout_rev": np.concatenate([i["L0_xattn_Wout"][rev], i["L0_xattn_Wout"][L + rev]], 0),
        "bout": i["L0_xattn_bout"].reshape(1, D),
        "cols": np.concatenate([np.stack([i["L0_ffn_ln1_g"], i["L0_ffn_ln1_b"], i["L0_ffn_ln2_g"],
                                          i["L0_ffn_ln2_b"], bqkv[0:D], bqkv[D:2 * D], bqkv[2 * D:]], 1),
                                i["L0_ffn_rb1"].reshape(FC, P).T, mq, mk,
                                np.tile(i["L0_xattn_bq"], P // DQ)[:, None]], 1),
        "wqk": wqkv[:, 0:2 * D],
        "wv": wqkv[:, 2 * D:],
        "wo": i["L0_ffn_Wo"],
        "bo": i["L0_ffn_bo"].reshape(1, D),
        "gc": np.concatenate([i["L0_ffn_gate_w"], i["L0_ffn_coef_w"]], 1),
        "coef_b": i["L0_ffn_coef_b"].reshape(1, 2),
        "w1": np.concatenate([w1, b1], 2),
        "w2": i["L0_ffn_W2"].reshape(E, FC, P, D).transpose(2, 0, 1, 3).reshape(P, E, FC * D),
        "b2": i["L0_ffn_b2"].reshape(E, D),
        "rw1": i["L0_ffn_rW1"],
        "rw2": i["L0_ffn_rW2"].reshape(FC, P, D).transpose(1, 0, 2),
        "rb2": i["L0_ffn_rb2"].reshape(1, D),
        "ident": np.eye(P, dtype=f),
        "identb": np.diag(np.full(P, BF16_ONE, np.uint16)),
        "oneb": np.full((P, P), BF16_ONE, np.uint16),
        "triu": np.triu(np.full((P, P), BF16_ONE, np.uint16), 1),
        "sel": sel.reshape(4, 4, DQ, 2, L).transpose(1, 0, 2, 3, 4).reshape(P, 2, L),
        "msel": msel.reshape(32, 8, P),
        "dmask": dmask.reshape(P, 4, H // 2),
        "dspread": np.repeat(np.eye(H // 2, dtype=f), DH, 1),
        "prio": np.arange(E, 0, -1, dtype=f).reshape(1, E),
        "blank": blank,
        "token": (np.arange(NT)[None, :] * P + np.arange(P)[:, None]).astype(f),
        "jrow": np.arange(SLOTS, dtype=f).reshape(1, SLOTS),
    }


def kernel(**inputs):
    import numpy as np
    import concourse.bacc as bacc
    from concourse.bass_utils import run_bass_kernel_spmd

    nc = bacc.Bacc("TRN2", target_bir_lowering=False, num_devices=1)
    arrays = {n: np.ascontiguousarray(v) for n, v in layouts({n: np.asarray(v) for n, v in inputs.items()}).items()}
    aps = {n: nc.dram_tensor(f"in_{n}", v.shape, mybir.dt.from_np(v.dtype), kind="ExternalInput").ap()
           for n, v in arrays.items()}
    out = nc.dram_tensor("out_0", (B * L + YB * P, D), F32, kind="ExternalOutput").ap()
    build(nc, aps, out)
    r = run_bass_kernel_spmd(nc, [{f"in_{n}": v for n, v in arrays.items()}], core_ids=[0])
    return r.results[0]["out_0"][:B * L].reshape(_OUT[0])
```
